# Optimizing a Trainium2 kernel written in Bass

```python
import numpy as np
import jax
import jax.numpy as jnp

def _softmax(x, axis=-1):
    return jax.nn.softmax(x, axis=axis)

def _gelu(x):
    return jax.nn.gelu(x, approximate=True)

def _silu(x):
    return jax.nn.silu(x)

def _sigmoid(x):
    return jax.nn.sigmoid(x)

def _layernorm(x, axis=-1, eps=1e-05):
    m = jnp.mean(x, axis=axis, keepdims=True)
    v = jnp.var(x, axis=axis, keepdims=True)
    return (x - m) / jnp.sqrt(v + eps)

def _scatter_add(tgt, idx, src, axis=0):
    return tgt.at[idx].add(src)

def _segment_sum(src, seg, n):
    return jax.ops.segment_sum(src, seg, n)
kernel_name = 'mk_macaron_d1_jaxref_r8_510dfc'

def setup_inputs(seed: int=0):
    np.random.seed(seed)
    _w = jnp.asarray

    def _L0_attn_setup():
        import jax, jax.numpy as jnp
        import numpy as np
        D_MODEL = 256
        EXPAND = 2
        D_INNER = EXPAND * D_MODEL
        D_SSM = D_INNER
        D_STATE = 128
        NGROUPS = 1
        HEADDIM = 64
        NHEADS = D_SSM // HEADDIM
        D_CONV = 4
        CHUNK = 32
        CONV_DIM = D_SSM + 2 * NGROUPS * D_STATE
        D_IN_PROJ = 2 * D_INNER + 2 * NGROUPS * D_STATE + NHEADS
        EPS = 1e-05

        def silu(x):
            return x * jax.nn.sigmoid(x)

        def softplus(x):
            return jnp.log1p(jnp.exp(-jnp.abs(x))) + jnp.maximum(x, 0)

        def segsum(x):
            T = x.shape[-1]
            xe = jnp.broadcast_to(x[..., :, None], x.shape + (T,))
            mask_lo = jnp.tril(jnp.ones((T, T), dtype=bool), k=-1)
            xe = jnp.where(mask_lo, xe, 0.0)
            s = jnp.cumsum(xe, axis=-2)
            mask = jnp.tril(jnp.ones((T, T), dtype=bool), k=0)
            return jnp.where(mask, s, -jnp.inf)

        def ssd(x, A, B, C, chunk_size):
            b, s, h, p = x.shape
            c = s // chunk_size
            resh = lambda m: m.reshape((b, c, chunk_size) + m.shape[2:])
            x, A, B, C = (resh(x), resh(A), resh(B), resh(C))
            A = jnp.transpose(A, (0, 3, 1, 2))
            A_cumsum = jnp.cumsum(A, axis=-1)
            L = jnp.exp(segsum(A))
            Y_diag = jnp.einsum('bclhn,bcshn,bhcls,bcshp->bclhp', C, B, L, x)
            decay_states = jnp.exp(A_cumsum[..., -1:] - A_cumsum)
            states = jnp.einsum('bclhn,bhcl,bclhp->bchpn', B, decay_states, x)
            init = jnp.zeros_like(states[:, :1])
            states = jnp.concatenate([init, states], axis=1)
            A_last = jnp.pad(A_cumsum[:, :, :, -1], ((0, 0), (0, 0), (1, 0)))
            decay_chunk = jnp.exp(segsum(A_last))
            new_states = jnp.einsum('bhzc,bchpn->bzhpn', decay_chunk, states)
            states, final_state = (new_states[:, :-1], new_states[:, -1])
            state_decay_out = jnp.exp(A_cumsum)
            Y_off = jnp.einsum('bclhn,bchpn,bhcl->bclhp', C, states, state_decay_out)
            Y = (Y_diag + Y_off).reshape(b, s, h, p)
            return (Y, final_state)
        key = jax.random.key(seed)
        ks = jax.random.split(key, 8)
        u = jax.random.normal(ks[0], (2, 512, D_MODEL), dtype=jnp.float32)
        W_in = jax.random.normal(ks[1], (D_MODEL, D_IN_PROJ), dtype=jnp.float32) * D_MODEL ** (-0.5)
        conv_w = jax.random.uniform(ks[2], (D_CONV, CONV_DIM), dtype=jnp.float32, minval=-0.1, maxval=0.1)
        conv_b = jnp.zeros((CONV_DIM,), dtype=jnp.float32)
        dt = jnp.exp(jax.random.uniform(ks[3], (NHEADS,)) * (np.log(0.1) - np.log(0.001)) + np.log(0.001))
        dt = jnp.clip(dt, 0.0001)
        dt_bias = dt + jnp.log(jnp.expm1(dt))
        A_log = jnp.log(jax.random.uniform(ks[4], (NHEADS,), minval=1.0, maxval=16.0))
        D = jnp.ones((NHEADS,), dtype=jnp.float32)
        norm_scale = jnp.ones((D_SSM,), dtype=jnp.float32)
        W_out = jax.random.normal(ks[5], (D_INNER, D_MODEL), dtype=jnp.float32) * D_INNER ** (-0.5)
        return {'u': u, 'W_in': W_in, 'conv_w': conv_w, 'conv_b': conv_b, 'dt_bias': dt_bias, 'A_log': A_log, 'D': D, 'norm_scale': norm_scale, 'W_out': W_out}
    _L0_attn_in = _L0_attn_setup()

    def _L0_ffn_setup():
        import jax, jax.numpy as jnp
        import numpy as np
        from functools import partial
        SEQ, BATCH, HIDDEN = (256, 4, 256)
        FFN = 176
        N_EXPERTS = 8
        TOP_K = 2
        EPS = 1e-20
        key = jax.random.key(seed)
        k0, k1, k2, k3 = jax.random.split(key, 4)
        x = jax.random.normal(k0, (SEQ, BATCH, HIDDEN), dtype=jnp.float32)
        wg = jax.random.normal(k1, (N_EXPERTS, HIDDEN), dtype=jnp.float32) * 0.02
        w1 = jax.random.normal(k2, (N_EXPERTS, HIDDEN, 2 * FFN), dtype=jnp.float32) * 0.02
        w2 = jax.random.normal(k3, (N_EXPERTS, FFN, HIDDEN), dtype=jnp.float32) * 0.02
        return {'x': x, 'wg': wg, 'w1': w1, 'w2': w2}
    _L0_ffn_in = _L0_ffn_setup()
    _d = {'L0_attn_u': _L0_attn_in['u'], 'L0_attn_W_in': _L0_attn_in['W_in'], 'L0_attn_conv_w': _L0_attn_in['conv_w'], 'L0_attn_conv_b': _L0_attn_in['conv_b'], 'L0_attn_dt_bias': _L0_attn_in['dt_bias'], 'L0_attn_A_log': _L0_attn_in['A_log'], 'L0_attn_D': _L0_attn_in['D'], 'L0_attn_norm_scale': _L0_attn_in['norm_scale'], 'L0_attn_W_out': _L0_attn_in['W_out'], 'L0_ffn_wg': _L0_ffn_in['wg'], 'L0_ffn_w1': _L0_ffn_in['w1'], 'L0_ffn_w2': _L0_ffn_in['w2']}
    _x0 = _d['L0_attn_u']
    _d['L0_attn_u'] = jax.random.normal(jax.random.fold_in(jax.random.key(seed), 1), (4, 256, 256), dtype=_x0.dtype)
    del _x0
    return _d

def reference(L0_attn_u, L0_attn_W_in, L0_attn_conv_w, L0_attn_conv_b, L0_attn_dt_bias, L0_attn_A_log, L0_attn_D, L0_attn_norm_scale, L0_attn_W_out, L0_ffn_wg, L0_ffn_w1, L0_ffn_w2):

    def _L0_attn_ref(u, W_in, conv_w, conv_b, dt_bias, A_log, D, norm_scale, W_out):
        import jax, jax.numpy as jnp
        import numpy as np
        D_MODEL = 256
        EXPAND = 2
        D_INNER = EXPAND * D_MODEL
        D_SSM = D_INNER
        D_STATE = 128
        NGROUPS = 1
        HEADDIM = 64
        NHEADS = D_SSM // HEADDIM
        D_CONV = 4
        CHUNK = 32
        CONV_DIM = D_SSM + 2 * NGROUPS * D_STATE
        D_IN_PROJ = 2 * D_INNER + 2 * NGROUPS * D_STATE + NHEADS
        EPS = 1e-05

        def silu(x):
            return x * jax.nn.sigmoid(x)

        def softplus(x):
            return jnp.log1p(jnp.exp(-jnp.abs(x))) + jnp.maximum(x, 0)

        def segsum(x):
            T = x.shape[-1]
            xe = jnp.broadcast_to(x[..., :, None], x.shape + (T,))
            mask_lo = jnp.tril(jnp.ones((T, T), dtype=bool), k=-1)
            xe = jnp.where(mask_lo, xe, 0.0)
            s = jnp.cumsum(xe, axis=-2)
            mask = jnp.tril(jnp.ones((T, T), dtype=bool), k=0)
            return jnp.where(mask, s, -jnp.inf)

        def ssd(x, A, B, C, chunk_size):
            b, s, h, p = x.shape
            c = s // chunk_size
            resh = lambda m: m.reshape((b, c, chunk_size) + m.shape[2:])
            x, A, B, C = (resh(x), resh(A), resh(B), resh(C))
            A = jnp.transpose(A, (0, 3, 1, 2))
            A_cumsum = jnp.cumsum(A, axis=-1)
            L = jnp.exp(segsum(A))
            Y_diag = jnp.einsum('bclhn,bcshn,bhcls,bcshp->bclhp', C, B, L, x)
            decay_states = jnp.exp(A_cumsum[..., -1:] - A_cumsum)
            states = jnp.einsum('bclhn,bhcl,bclhp->bchpn', B, decay_states, x)
            init = jnp.zeros_like(states[:, :1])
            states = jnp.concatenate([init, states], axis=1)
            A_last = jnp.pad(A_cumsum[:, :, :, -1], ((0, 0), (0, 0), (1, 0)))
            decay_chunk = jnp.exp(segsum(A_last))
            new_states = jnp.einsum('bhzc,bchpn->bzhpn', decay_chunk, states)
            states, final_state = (new_states[:, :-1], new_states[:, -1])
            state_decay_out = jnp.exp(A_cumsum)
            Y_off = jnp.einsum('bclhn,bchpn,bhcl->bclhp', C, states, state_decay_out)
            Y = (Y_diag + Y_off).reshape(b, s, h, p)
            return (Y, final_state)
        b, s, _ = u.shape
        zxbcdt = u @ W_in
        z, xBC, dt = jnp.split(zxbcdt, [D_INNER, D_INNER + D_SSM + 2 * NGROUPS * D_STATE], axis=-1)
        xp = jnp.pad(xBC, ((0, 0), (D_CONV - 1, 0), (0, 0)))
        conv = conv_b
        for i in range(D_CONV):
            conv = conv + xp[:, i:i + s, :] * conv_w[i]
        xBC = silu(conv)
        x, B, C = jnp.split(xBC, [D_SSM, D_SSM + NGROUPS * D_STATE], axis=-1)
        x = x.reshape(b, s, NHEADS, HEADDIM)
        dt = softplus(dt + dt_bias)
        A = -jnp.exp(A_log)
        Bh = jnp.broadcast_to(B[:, :, None, :], (b, s, NHEADS, D_STATE))
        Ch = jnp.broadcast_to(C[:, :, None, :], (b, s, NHEADS, D_STATE))
        y, _final = ssd(x * dt[..., None], A * dt, Bh, Ch, CHUNK)
        y = y + x * D[None, None, :, None]
        y = y.reshape(b, s, D_SSM)
        y = y * silu(z)
        var = jnp.mean(jnp.square(y), axis=-1, keepdims=True)
        y = y * jax.lax.rsqrt(var + EPS) * norm_scale
        return y @ W_out

    def _L0_ffn_ref(x, wg, w1, w2):
        import jax, jax.numpy as jnp
        import numpy as np
        from functools import partial
        SEQ, BATCH, HIDDEN = (256, 4, 256)
        FFN = 176
        N_EXPERTS = 8
        TOP_K = 2
        EPS = 1e-20
        S, B, H = x.shape
        T = B * S
        xt = jnp.transpose(x, (1, 0, 2)).reshape(T, H)
        logits = xt @ wg.T
        scores = jax.nn.softmax(logits, axis=-1)
        topk_w, topk_i = jax.lax.top_k(scores, TOP_K)
        topk_w = topk_w / (jnp.sum(topk_w, axis=-1, keepdims=True) + EPS)
        C = jnp.zeros((T, N_EXPERTS), dtype=xt.dtype)
        C = C.at[jnp.arange(T)[:, None], topk_i].add(topk_w)

        def step(acc, inputs):
            w1e, w2e, ce = inputs
            h = xt @ w1e
            a, b = jnp.split(h, 2, axis=-1)
            y = jax.nn.silu(a) * b @ w2e
            return (acc + ce[:, None] * y, None)
        out0 = jnp.zeros((T, H), dtype=xt.dtype)
        out, _ = jax.lax.scan(step, out0, (w1, w2, C.T))
        return jnp.transpose(out.reshape(B, S, H), (1, 0, 2))
    x = L0_attn_u
    x = x + 0.5 * _L0_ffn_ref(_layernorm(x, axis=-1), L0_ffn_wg, L0_ffn_w1, L0_ffn_w2)
    x = x + _L0_attn_ref(_layernorm(x, axis=-1), L0_attn_W_in, L0_attn_conv_w, L0_attn_conv_b, L0_attn_dt_bias, L0_attn_A_log, L0_attn_D, L0_attn_norm_scale, L0_attn_W_out)
    x = x + 0.5 * _L0_ffn_ref(_layernorm(x, axis=-1), L0_ffn_wg, L0_ffn_w1, L0_ffn_w2)
    return x

_drawn_inputs = setup_inputs


def setup_inputs(seed=0):
    import zlib

    import numpy as np

    out = dict(_drawn_inputs(seed))
    spreads = {'L0_attn_conv_b': (0.0, 0.1), 'L0_attn_D': (1.0, 0.2), 'L0_attn_norm_scale': (1.0, 0.2)}
    factors = {'L0_attn_dt_bias': 8.0,
     'L0_attn_A_log': 8.0,
     'L0_ffn_wg': 8.0,
     'L0_ffn_w1': 7.758,
     'L0_ffn_w2': 7.747}
    for name, (base, spread) in spreads.items():
        noise = np.random.default_rng([zlib.crc32(name.encode()), seed]).standard_normal(out[name].shape)
        drawn = base * np.exp(spread * noise) if base else spread * noise
        out[name] = jnp.asarray(drawn.astype(out[name].dtype))
    for name, factor in factors.items():
        out[name] = (out[name] * factor).astype(out[name].dtype)
    return out
```

```python
from contextlib import ExitStack

import numpy as np
import concourse.bass as bass
from concourse import mybir

F32 = mybir.dt.float32
F32R = mybir.dt.float32r
BF16 = mybir.dt.bfloat16
I32 = mybir.dt.int32
U32 = mybir.dt.uint32
ALU = mybir.AluOpType
ACT = mybir.ActivationFunctionType
AX = mybir.AxisListType

P = 128
XG = 6
YB = 3
BIG = 4096.0
ROUND = 12582912.0
EPS = 1e-5
TOPK_EPS = 1e-20
ATANH = [1.0 / (2 * i + 1) for i in range(8)]


class Chain:

    def __init__(self, sem):
        self.sem, self.n = sem, 0

    def add(self, ins):
        ins.then_inc(self.sem, 1)
        self.n += 1


def build(nc, u_in, w_in, conv_w, conv_b, dt_bias, a_log, d_skip, norm_scale, w_out, wg_t, w1, w2, out):
    T, D = u_in.shape
    NT = T // P
    KD = D // P
    E, _, FF = w1.shape
    F = FF // 2
    FH = F // 2
    DI = w_out.shape[0]
    KI = DI // P
    NHEADS = a_log.shape[1]
    HD = DI // NHEADS
    CONVD = conv_w.shape[1]
    NC = CONVD // P
    TAPS = conv_w.shape[2]
    NPROJ = w_in.shape[1]
    SEQ = 2 * P
    NH = T // 512
    UNITS = 2 * NT + E - 1
    TK = 2 * NT
    EG = 2
    NWG = E // EG
    NW2 = 2

    xn_dram = nc.dram_tensor("xn_rows", (T, D), F32, kind="Internal").ap()
    y_dram = nc.dram_tensor("y_rows", (2 * T, D), F32, kind="Internal").ap()

    ctx = ExitStack()
    with ctx:
        def sb(name, shape, dt=F32):
            return ctx.enter_context(nc.sbuf_tensor(name, shape, dt))

        def sem(name):
            return ctx.enter_context(nc.semaphore(name))

        W1F, W2F = E * KD * FF, E * 2 * D
        x_sb = sb("x_sb", [P, NT, D])
        w1h = sb("w1h", [P, W1F], F32R)
        w2h = sb("w2h", [FH, W2F], F32R)
        winh = sb("winh", [P, KD, NPROJ], F32R)
        wouth = sb("wouth", [P, KI, D], F32R)

        def landing(name, shape):
            with nc.sbuf_tensor(name + "s", shape, F32) as raw:
                pass
            return raw, sb(name + "l", shape, F32R)

        w1s, w1l = landing("w1", [P, W1F])
        w2s, w2l = landing("w2", [FH, W2F])
        wins, winl = landing("win", [P, KD, NPROJ])
        wouts, woutl = landing("wout", [P, KI, D])

        ident = sb("ident", [P, P])
        tri = sb("tri", [P, P])
        after = sb("after", [P, P])
        before16 = sb("before16", [P, P], BF16)
        ones16 = sb("ones16", [P, P], BF16)
        lanes = sb("lanes", [P, P])
        tokid = sb("tokid", [P, TK])
        rowid = sb("rowid", [P, TK])
        mhalf = sb("mhalf", [P, NT])

        st = sb("st", [P, NT, 6])
        mv = sb("mv", [P, NT, 2])
        vare = sb("vare", [P, NT])
        rstd = sb("rstd", [P, NT])
        wgt = sb("wgt", [P, KD, E])
        idxf = sb("idxf", [P, 2, NT])
        wsum = sb("wsum", [P, NT])
        wrec = sb("wrec", [P, NT])
        cw = sb("cw", [P, 2, NT])
        tl = sb("tl", [P, E])
        tr = sb("tr", [P, E])
        incl = sb("incl", [P, E])
        base = sb("base", [P, E])
        zer = sb("zer", [P, E])
        slk = sb("slk", [P, TK])
        hif = sb("hif", [P, TK])
        hi = sb("hi", [P, TK])
        lo = sb("lo", [P, TK])
        gidx = sb("gidx", [P, UNITS], I32)
        sidx = sb("sidx", [P, UNITS], I32)
        uef = sb("uef", [P, UNITS])
        uem = sb("uem", [P, UNITS])
        ue = sb("ue", [P, UNITS], I32)
        cwt = sb("cwt", [P, NC, TAPS])
        cbt = sb("cbt", [P, NC])
        dtb = sb("dtb", [P, NHEADS])
        alog = sb("alog", [P, NHEADS])
        dsk = sb("dsk", [P, NHEADS])
        nsc = sb("nsc", [P, KI])
        ssq = sb("ssq", [P, NT])
        vy = sb("vy", [P, NT])
        ry = sb("ry", [P, NT])

        with nc.sbuf_tensor("xn", [P, NT, D], F32) as xn:
            pass
        xdt = sb("xdt", [P, 2, DI])
        yg = sb("yg", [P, 2, DI])

        with ExitStack() as ffn:
            def fb(name, shape, dt=F32):
                return ffn.enter_context(nc.sbuf_tensor(name, shape, dt))

            xT = fb("xT", [P, NT, KD, P])
            lane_oh = fb("lane_oh", [P, TK, P])
            yin = fb("yin", [P, 2, NT, D])
            unit_oh = fb("unit_oh", [P, TK, UNITS])
            tab = fb("tab", [P, TK, 2, UNITS])
            lmax = fb("lmax", [P, NT])
            gl = fb("gl", [P, NT, E])
            ge = fb("ge", [P, NT, E])
            gsum = fb("gsum", [P, NT])
            grec = fb("grec", [P, NT])
            sc = fb("sc", [P, NT, E])
            top = fb("top", [P, NT, 8])
            topi = fb("topi", [P, NT, 8], U32)
            oh = fb("oh", [P, TK, E])
            m16 = fb("m16", [P, 2 * NT - 1, E], BF16)
            slot = fb("slot", [P, NT, E])
            osl = fb("osl", [P, TK, E])
            ule = fb("ule", [P, UNITS, E])
            xg = fb("xg", [P, XG, D])
            uxh = fb("uxh", [P, 2, KD, P], F32R)
            uxl = fb("uxl", [P, 2, KD, P], F32R)
            sl = fb("sl", [P, 2, F])
            g = fb("g", [P, 2, F])
            gth = fb("gth", [FH, 2, 2, P], F32R)
            gtl = fb("gtl", [FH, 2, 2, P], F32R)
            yo = fb("yo", [P, YB, D])

        conv = sb("conv", [P, NC, T])
        sz = sb("sz", [P, NT, DI])
        with nc.sbuf_tensor("xTh", [P, NT, KD, P], F32R) as xTh, nc.sbuf_tensor("xTl", [P, NT, KD, P], F32R) as xTl:
            pass
        segm = sb("segm", [P, 2, NHEADS, P])
        mm = sb("mm", [P, 2, NHEADS, P])
        aexp = sb("aexp", [P, NHEADS])
        dtx = sb("dtx", [P, NT, NHEADS])
        dta = sb("dta", [P, NT, NHEADS])
        dtu = sb("dtu", [P, NT, NHEADS])
        dtr = sb("dtr", [P, NT, NHEADS])
        dts = sb("dts", [P, NT, NHEADS])
        dtq = sb("dtq", [P, NT, NHEADS])
        dtp = sb("dtp", [P, NT, NHEADS])
        dtv = sb("dtv", [P, NT, NHEADS])
        da = sb("da", [P, NT, NHEADS])
        ecum = sb("ecum", [P, NT, NHEADS])
        eend = sb("eend", [P, NT, NHEADS])
        dec = sb("dec", [P, NHEADS, P])
        cbm = sb("cbm", [P, 2, P])
        xs = sb("xs", [P, DI])
        xd = sb("xd", [P, DI])
        xde = sb("xde", [P, DI])
        btok = sb("btok", [P, P])
        state = sb("state", [P, DI])
        y1 = sb("y1", [P, DI])
        yf = sb("yf", [P, DI])
        ysq = sb("ysq", [P, DI])
        yth = sb("yth", [P, KI, P], F32R)
        ytl = sb("ytl", [P, KI, P], F32R)

        bank = [ctx.enter_context(nc.psum_tensor(f"bank{i}", [P, 512], F32)) for i in range(8)]
        tp = [bank[0], bank[1]]
        ps_xt = [bank[0][:, 0:D], bank[1][:, 0:D]]
        ps_gt = [bank[6][0:FH, 0:2 * P], bank[7][0:FH, 0:2 * P]]
        ps_h = [bank[2][:, 0:FF], bank[3][:, 0:FF]]
        ps_y = [bank[4][:, 0:D], bank[5][:, 0:D]]
        ps_log = bank[5][:, 0:NT * E].rearrange("p (t e) -> p t e", t=NT)
        ps_rank = bank[6][:, 0:NT * E].rearrange("p (t e) -> p t e", t=NT)
        ps_cnt = bank[7][:, 0:E]
        ps_tab = bank[5][:, 128:128 + 2 * UNITS]

        ld_x = [sem(f"ld_x{i}") for i in range(2)]
        ld_wg = sem("ld_wg")
        ld_small = sem("ld_small")
        ld_w1 = [sem(f"ld_w1_{i}") for i in range(NWG)]
        ld_w2 = [sem(f"ld_w2_{i}") for i in range(NW2)]
        ld_win = sem("ld_win")
        ld_wout = sem("ld_wout")
        consts = sem("consts")
        w_hi = sem("w_hi")
        w_lo = sem("w_lo")
        wout_scaled = sem("wout_scaled")
        dve_own = sem("dve_own")
        act_own = sem("act_own")
        pool_own = sem("pool_own")
        var_ready = sem("var_ready")
        rstd_ready = sem("rstd_ready")
        xn_ready = sem("xn_ready")
        xn_stored = sem("xn_stored")
        xt_psum = sem("xt_psum")
        xt_ready = sem("xt_ready")
        xtl_ready = sem("xtl_ready")
        logits_ready = sem("logits_ready")
        gate_in = sem("gate_in")
        gate_exp = sem("gate_exp")
        mask_ready = sem("mask_ready")
        rank_ready = sem("rank_ready")
        tab_in = sem("tab_in")
        tab_ready = sem("tab_ready")
        idx_ready = sem("idx_ready")
        expert_ready = sem("expert_ready")
        xg_landed = [sem(f"xg_landed{i}") for i in range(XG)]
        uxt_psum = sem("uxt_psum")
        uxh_ready = sem("uxh_ready")
        uxl_ready = sem("uxl_ready")
        h_ready = sem("h_ready")
        sl_ready = sem("sl_ready")
        g_ready = sem("g_ready")
        gt_psum = sem("gt_psum")
        gth_ready = sem("gth_ready")
        gtl_ready = sem("gtl_ready")
        y_psum = sem("y_psum")
        y_ready = sem("y_ready")
        y_stored = [sem(f"y_stored{i}") for i in range(YB)]
        y_back = [sem(f"y_back{i}") for i in range(4)]
        x_done = sem("x_done")
        out_stored = sem("out_stored")
        proj_psum = sem("proj_psum")
        tap_ready = sem("tap_ready")
        conv_sum = sem("conv_sum")
        conv_ready = sem("conv_ready")
        z_psum = sem("z_psum")
        z_ready = sem("z_ready")
        dt_psum = sem("dt_psum")
        dt_in = sem("dt_in")
        dt_exp = sem("dt_exp")
        a_exp = sem("a_exp")
        da_ready = sem("da_ready")
        cum_psum = sem("cum_psum")
        cum_exp = sem("cum_exp")
        xtok_psum = sem("xtok_psum")
        cb_psum = sem("cb_psum")
        seg_in = sem("seg_in")
        seg_psum = sem("seg_psum")
        xs_ready = sem("xs_ready")
        btok_ready = sem("btok_ready")
        dec_ready = sem("dec_ready")
        cbm_ready = sem("cbm_ready")
        mm_ready = sem("mm_ready")
        xdt_ready = sem("xdt_ready")
        xd_ready = sem("xd_ready")
        xde_ready = sem("xde_ready")
        ydiag_psum = sem("ydiag_psum")
        state_psum = sem("state_psum")
        state_ready = sem("state_ready")
        yoff_psum = sem("yoff_psum")
        yd_used = sem("yd_used")
        yf_ready = sem("yf_ready")
        yg_ready = sem("yg_ready")
        ssq_ready = sem("ssq_ready")
        vy_ready = sem("vy_ready")
        ry_ready = sem("ry_ready")
        yt_psum = sem("yt_psum")
        yth_ready = sem("yth_ready")
        ytl_ready = sem("ytl_ready")
        o_psum = sem("o_psum")
        o_used = sem("o_used")

        N_CONST = 10
        N_SMALL = 6

        block = ctx.enter_context(nc.Block())

        @block.sync
        def _(sp):
            xv = u_in.rearrange("(t p) d -> p t d", p=P)
            half = NT // 2
            for i in range(2):
                sp.dma_start(x_sb[:, i * half:(i + 1) * half, :], xv[:, i * half:(i + 1) * half, :])\
                  .then_inc(ld_x[i], 16)
            sp.dma_start(wgt[:, :, :], wg_t.rearrange("(k p) e -> p k e", p=P)).then_inc(ld_wg, 16)
            w1v = w1.rearrange("e (k p) f -> p e k f", p=P)
            w1sv = w1s[:, :].rearrange("p (e k f) -> p e k f", e=E, k=KD)
            for i in range(NWG):
                for e in range(i * EG, (i + 1) * EG):
                    sp.dma_start(w1sv[:, e, :, :], w1v[:, e, :, :]).then_inc(ld_w1[i], 16)
            w2v = w2.rearrange("e (j p) d -> p e j d", p=FH)
            w2sv = w2s[:, :].rearrange("p (e j d) -> p e j d", e=E, j=2)
            for e in range(E):
                sp.dma_start(w2sv[:, e, :, :], w2v[:, e, :, :]).then_inc(ld_w2[e // (E // NW2)], 16)

            def store_rows(q, f):
                for t in range(NT):
                    sp.wait_ge(xn_ready, NT * q + t + 1)
                    sp.dma_start(xn_dram[t * P:(t + 1) * P, :], xn[:, t, :]).then_inc(xn_stored, 16)

            def fetch_rows(f):
                for i in range(YB):
                    uses = len([u for u in range(UNITS * (f + 1)) if u % YB == i])
                    sp.wait_ge(y_stored[i], 16 * uses)
                yv = y_dram.rearrange("(c t p) d -> p c t d", c=2, p=P)
                step = NT // 4
                for i in range(4):
                    for c in range(2):
                        sp.dma_start(yin[:, c, i * step:(i + 1) * step, :], yv[:, c, i * step:(i + 1) * step, :])\
                          .then_inc(y_back[i], 16)

            store_rows(0, 0)
            sp.dma_start(wins[:, :, :], w_in.rearrange("(k p) n -> p k n", p=P)).then_inc(ld_win, 16)
            sp.dma_start(wouts[:, :, :], w_out.rearrange("(k p) n -> p k n", p=P)).then_inc(ld_wout, 16)
            sp.dma_start(cwt[:, :, :], conv_w.rearrange("a n k -> (a n) k").rearrange("(c p) k -> p c k", p=P))\
              .then_inc(ld_small, 16)
            sp.dma_start(cbt[:, :], conv_b).then_inc(ld_small, 16)
            sp.dma_start(nsc[:, :], norm_scale).then_inc(ld_small, 16)
            for dst, src in ((dtb, dt_bias), (alog, a_log), (dsk, d_skip)):
                sp.dma_start(dst[:, :], src.broadcast_to([P, NHEADS])).then_inc(ld_small, 16)
            fetch_rows(0)
            store_rows(2, 1)
            fetch_rows(1)
            for t in range(NT):
                sp.wait_ge(x_done, NT + t + 1)
                sp.dma_start(out[t * P:(t + 1) * P, :], x_sb[:, t, :]).then_inc(out_stored, 16)
            sp.wait_ge(out_stored, 16 * NT)

        @block.gpsimd
        def _(pool):
            own = Chain(pool_own)

            def select(dst, fill, compare, pattern, base, mult):
                pool.affine_select(out=dst, in_=dst, compare_op=compare, fill=fill, base=base,
                                   pattern=pattern, channel_multiplier=mult).then_inc(consts, 1)

            own.add(pool.memset(ident[:, :], 0.0))
            own.add(pool.memset(tri[:, :], 1.0))
            own.add(pool.memset(after[:, :], 1.0))
            own.add(pool.memset(before16[:, :], 1.0))
            pool.memset(ones16[:, :], 1.0).then_inc(consts, 1)
            pool.memset(mhalf[:, :], -0.5).then_inc(consts, 1)
            pool.memset(zer[:, :], 0.0).then_inc(consts, 1)
            pool.wait_ge(pool_own, own.n)
            select(ident[:, :], 1.0, ALU.not_equal, [[-1, P]], 0, 1)
            select(tri[:, :], 0.0, ALU.is_ge, [[1, P]], 0, -1)
            select(after[:, :], 0.0, ALU.is_gt, [[-1, P]], 0, 1)
            select(before16[:, :], 0.0, ALU.is_gt, [[1, P]], 0, -1)
            iota = dict(allow_small_or_imprecise_dtypes=True)
            pool.iota(lanes[:, :], pattern=[[1, P]], base=0, channel_multiplier=0, **iota).then_inc(consts, 1)
            tkv = tokid[:, :].rearrange("p (c t) -> p c t", c=2)
            pool.iota(tkv, pattern=[[0, 2], [P, NT]], base=0, channel_multiplier=1, **iota).then_inc(consts, 1)
            rkv = rowid[:, :].rearrange("p (c t) -> p c t", c=2)
            pool.iota(rkv, pattern=[[T, 2], [P, NT]], base=-int(BIG), channel_multiplier=1, **iota)\
                .then_inc(consts, 1)

            def deviations(q):
                pool.wait_ge(consts, N_CONST)
                pool.wait_ge(var_ready, q + 1)
                pool.tensor_tensor(rstd[:, :], vare[:, :], mhalf[:, :], ALU.pow).then_inc(rstd_ready, 1)

            def gather(f, s):
                u = f * UNITS + s
                if s == 0:
                    pool.wait_ge(idx_ready, f + 1)
                    pool.wait_ge(xn_stored, 16 * NT * (f + 1))
                if u >= XG:
                    pool.wait_ge(uxt_psum, u - XG + 1)
                pool.indirect_dma_start(xg[:, u % XG, :], None, xn_dram,
                                        bass.IndirectOffsetOnAxis(ap=gidx[:, s:s + 1], axis=0))\
                    .then_inc(xg_landed[u % XG], 16)

            def scatter(f, s):
                u = f * UNITS + s
                pool.wait_ge(y_ready, u + 1)
                pool.indirect_dma_start(y_dram, bass.IndirectOffsetOnAxis(ap=sidx[:, s:s + 1], axis=0),
                                        yo[:, u % YB, :], None, bounds_check=2 * T - 1, oob_is_err=False)\
                    .then_inc(y_stored[u % YB], 16)

            def moe(f):
                for s in range(XG):
                    gather(f, s)
                for s in range(UNITS):
                    scatter(f, s)
                    if s + XG < UNITS:
                        gather(f, s + XG)

            def seg_input(t):
                if t == 0:
                    pool.wait_ge(da_ready, 1)
                if t >= 2:
                    pool.wait_ge(seg_psum, 2 * (t - 1))
                pool.tensor_tensor(segm[:, t % 2, :, :], tri[:, :].unsqueeze(1).broadcast_to([P, NHEADS, P]),
                                   da[:, t, :].unsqueeze(2).broadcast_to([P, NHEADS, P]), ALU.mult)\
                    .then_inc(seg_in, 1)

            def skip_input(t):
                pool.wait_ge(xs_ready, t + 1)
                if t >= 1:
                    pool.wait_ge(yd_used, t)
                pool.tensor_tensor(xd[:, :].rearrange("p (h d) -> p h d", h=NHEADS),
                                   xs[:, :].rearrange("p (h d) -> p h d", h=NHEADS),
                                   dsk[:, :].unsqueeze(2).broadcast_to([P, NHEADS, HD]), ALU.mult)\
                    .then_inc(xd_ready, 1)
                if t % 2 == 0:
                    pool.wait_ge(xdt_ready, t + 1)
                    if t >= 2:
                        pool.wait_ge(state_psum, t // 2)
                    pool.tensor_tensor(xde[:, :].rearrange("p (h d) -> p h d", h=NHEADS),
                                       xdt[:, t % 2, :].rearrange("p (h d) -> p h d", h=NHEADS),
                                       eend[:, t, :].unsqueeze(2).broadcast_to([P, NHEADS, HD]), ALU.mult)\
                        .then_inc(xde_ready, 1)

            def y_deviation(t):
                pool.wait_ge(vy_ready, t + 1)
                pool.tensor_tensor(ry[:, t:t + 1], vy[:, t:t + 1], mhalf[:, 0:1], ALU.pow)\
                    .then_inc(ry_ready, 1)

            deviations(0)
            moe(0)
            deviations(1)
            pool.wait_ge(cum_exp, 2)
            seg_input(0)
            seg_input(1)
            skip_input(0)
            for t in range(NT):
                if t + 1 < NT:
                    skip_input(t + 1)
                if t + 2 < NT:
                    seg_input(t + 2)
                y_deviation(t)
            deviations(2)
            moe(1)

        @block.scalar
        def _(act):
            def turned(q, i):
                act.wait_ge(xt_psum, 4 * q + i + 1)
                dst = (xTh if q == 1 else xT)[:, 2 * i:2 * i + 2, :, :].rearrange("p t k n -> p (t k n)")
                act.activation(dst, tp[i % 2][:, :], ACT.Copy).then_inc(xt_ready, 1)

            def gate(f):
                act.wait_ge(gate_in, f + 1)
                act.activation(ge[:, :, :], gl[:, :, :], ACT.Exp).then_inc(gate_exp, 1)

            def unit_x(f, s):
                u = f * UNITS + s
                act.wait_ge(uxt_psum, u + 1)
                if u >= 2:
                    act.wait_ge(h_ready, u - 1)
                act.activation(uxh[:, u % 2, :, :].rearrange("p k n -> p (k n)"), ps_xt[u % 2], ACT.Copy)\
                    .then_inc(uxh_ready, 1)

            def unit_silu(f, s):
                u = f * UNITS + s
                act.wait_ge(h_ready, u + 1)
                if u >= 2:
                    act.wait_ge(g_ready, u - 1)
                act.activation(sl[:, u % 2, :], ps_h[u % 2][:, 0:F], ACT.Silu).then_inc(sl_ready, 1)

            def unit_g(f, s):
                u = f * UNITS + s
                act.wait_ge(gt_psum, u + 1)
                if u >= 2:
                    act.wait_ge(y_psum, u - 1)
                act.activation(gth[:, u % 2, :, :].rearrange("p k n -> p (k n)"), ps_gt[u % 2], ACT.Copy)\
                    .then_inc(gth_ready, 1)

            def moe(f):
                unit_x(f, 0)
                for s in range(UNITS + 1):
                    if s < UNITS:
                        unit_silu(f, s)
                    if s >= 1:
                        unit_g(f, s - 1)
                    if s + 1 < UNITS:
                        unit_x(f, s + 1)

            act.wait_ge(consts, N_CONST)
            for i in range(4):
                turned(0, i)
            gate(0)
            seg = EG * KD * FF
            for i in range(NWG):
                act.wait_ge(ld_w1[i], 16 * EG)
                act.activation(w1h[:, i * seg:(i + 1) * seg], w1s[:, i * seg:(i + 1) * seg], ACT.Copy)\
                    .then_inc(w_hi, 1)
            seg = E // NW2 * 2 * D
            for i in range(NW2):
                act.wait_ge(ld_w2[i], 16 * (E // NW2))
                act.activation(w2h[:, i * seg:(i + 1) * seg], w2s[:, i * seg:(i + 1) * seg], ACT.Copy)\
                    .then_inc(w_hi, 1)
            act.wait_ge(ld_win, 16)
            act.activation(winh[:, :, :], wins[:, :, :], ACT.Copy).then_inc(w_hi, 1)
            act.wait_ge(wout_scaled, KI)
            act.activation(wouth[:, :, :], wouts[:, :, :], ACT.Copy).then_inc(w_hi, 1)
            moe(0)

            for i in range(4):
                turned(1, i)
            for c in range(NC):
                for h in range(NH):
                    n = NH * c + h
                    act.wait_ge(proj_psum, n + 1)
                    act.activation(conv[:, c, 512 * h:512 * (h + 1)], bank[2 + n % 2][:, :], ACT.Copy,
                                   scale=cwt[:, c, TAPS - 1:TAPS]).then_inc(tap_ready, 1)
                for h in range(NH):
                    n = NH * c + h
                    act.wait_ge(conv_sum, n + 1)
                    part = conv[:, c, 512 * h:512 * (h + 1)]
                    act.activation(part, part, ACT.Silu, bias=cbt[:, c:c + 1]).then_inc(conv_ready, 1)
            for t in range(NT):
                act.wait_ge(z_psum, t + 1)
                act.activation(sz[:, t, :], bank[2 + t % 2][:, :], ACT.Silu).then_inc(z_ready, 1)
            act.wait_ge(dt_in, 1)
            act.activation(dtu[:, :, :], dta[:, :, :], ACT.Exp).then_inc(dt_exp, 1)
            act.activation(aexp[:, :], alog[:, :], ACT.Exp).then_inc(a_exp, 1)
            act.wait_ge(cum_psum, 2)
            act.activation(ecum[:, :, :].rearrange("p t h -> p (t h)"), bank[5][:, 64:128], ACT.Exp)\
                .then_inc(cum_exp, 1)
            act.activation(eend[:, :, :].rearrange("p t h -> p (t h)"), bank[5][:, 128:192], ACT.Exp)\
                .then_inc(cum_exp, 1)

            def front(t):
                act.wait_ge(xtok_psum, t + 1)
                if t >= 1:
                    act.wait_ge(xd_ready, t)
                act.activation(xs[:, :], bank[0][:, :], ACT.Copy).then_inc(xs_ready, 1)
                if t % 2 == 0:
                    act.wait_ge(cb_psum, t + 1)
                    if t >= 2:
                        act.wait_ge(state_psum, t // 2)
                    act.activation(btok[:, :], bank[1][:, 0:P], ACT.Copy).then_inc(btok_ready, 1)
                for i in range(2):
                    act.wait_ge(seg_psum, 2 * t + i + 1)
                    if t >= 1:
                        act.wait_ge(mm_ready, t)
                    hh = NHEADS // 2
                    act.activation(dec[:, i * hh:(i + 1) * hh, :].rearrange("p h l -> p (h l)"),
                                   bank[2 + i][:, :], ACT.Exp).then_inc(dec_ready, 1)

            def mid(t):
                if t % 2 == 0:
                    act.wait_ge(state_psum, t // 2 + 1)
                    if t >= 2:
                        act.wait_ge(yoff_psum, t // 2)
                    act.activation(state[:, :], bank[6][:, :], ACT.Copy).then_inc(state_ready, 1)
                act.wait_ge(yg_ready, t + 1)
                if t >= 1:
                    act.wait_ge(ssq_ready, t)
                act.activation(ysq[:, :], yg[:, t % 2, :], ACT.Square, accum_out=ssq[:, t:t + 1])\
                    .then_inc(ssq_ready, 1)

            def back(t):
                act.wait_ge(yt_psum, t + 1)
                if t >= 1:
                    act.wait_ge(o_psum, t)
                act.activation(yth[:, :, :].rearrange("p k n -> p (k n)"), bank[5][:, :], ACT.Copy)\
                    .then_inc(yth_ready, 1)

            front(0)
            for t in range(NT + 1):
                if t + 1 < NT:
                    front(t + 1)
                if t < NT:
                    mid(t)
                if t >= 1:
                    back(t - 1)

            for i in range(4):
                turned(2, i)
            gate(1)
            moe(1)

        @block.tensor
        def _(pe):
            def turn(q, i):
                pe.wait_ge(xn_ready, NT * q + 2 * i + 2)
                if i >= 2:
                    pe.wait_ge(xt_ready, 4 * q + i - 1)
                    if q == 1:
                        pe.wait_ge(xtl_ready, i - 1)
                for j in range(2):
                    for k in range(KD):
                        last = pe.transpose(tp[i % 2][:, (j * KD + k) * P:(j * KD + k + 1) * P],
                                            xn[:, 2 * i + j, k * P:(k + 1) * P], ident[:, :])
                last.then_inc(xt_psum, 1)

            def split3(out_ap, pairs, **kw):
                last = None
                n = len(pairs)
                for a in range(3):
                    for i, (lh, ll, rh, rl) in enumerate(pairs):
                        l, r = ((lh, rh), (lh, rl), (ll, rh))[a]
                        last = pe.matmul(out_ap, l, r, start=(a == 0 and i == 0), stop=(a == 2 and i == n - 1))
                return last

            def route(f):
                q = 2 * f
                pe.wait_ge(ld_wg, 16)
                for t in range(NT):
                    if t % 2 == 0:
                        pe.wait_ge(xt_ready, 4 * q + t // 2 + 1)
                    for k in range(KD):
                        last = pe.matmul(ps_log[:, t, :], xT[:, t, k, :], wgt[:, k, :],
                                         start=(k == 0), stop=(k == KD - 1))
                last.then_inc(logits_ready, 1)
                pe.wait_ge(mask_ready, f + 1)
                pe.matmul(ps_rank, before16[:, :], m16[:, NT - 1:2 * NT - 1, :], start=True, stop=False)
                for d in range(1, NT):
                    last = pe.matmul(ps_rank, ones16[:, :], m16[:, NT - 1 - d:2 * NT - 1 - d, :],
                                     start=False, stop=(d == NT - 1))
                last.then_inc(rank_ready, 1)
                for t in range(NT):
                    last = pe.matmul(ps_cnt, ones16[:, :], m16[:, NT - 1 + t, :], start=(t == 0), stop=(t == NT - 1))
                last.then_inc(rank_ready, 1)
                pe.wait_ge(tab_in, f + 1)
                for i in range(TK):
                    last = pe.matmul(ps_tab, lane_oh[:, i, :], tab[:, i, :, :].rearrange("p a u -> p (a u)"),
                                     start=(i == 0), stop=(i == TK - 1))
                last.then_inc(tab_ready, 1)

            def unit_turn_x(f, s):
                u = f * UNITS + s
                pe.wait_ge(xg_landed[u % XG], 16 * (u // XG + 1))
                if u >= 2:
                    pe.wait_ge(uxh_ready, u - 1)
                    pe.wait_ge(uxl_ready, u - 1)
                for k in range(KD):
                    last = pe.transpose(ps_xt[u % 2][:, k * P:(k + 1) * P], xg[:, u % XG, k * P:(k + 1) * P],
                                        ident[:, :])
                last.then_inc(uxt_psum, 1)

            def unit_up(f, s, e):
                u = f * UNITS + s
                pe.wait_ge(uxh_ready, u + 1)
                pe.wait_ge(uxl_ready, u + 1)
                if u >= 2:
                    pe.wait_ge(g_ready, u - 1)
                b = u % 2
                pairs = []
                for k in range(KD):
                    at = e * (KD * FF) + k * FF
                    pairs.append((uxh[:, b, k, :], uxl[:, b, k, :],
                                  w1h[:, bass.ds(at, FF)], w1l[:, bass.ds(at, FF)]))
                split3(ps_h[b], pairs).then_inc(h_ready, 1)

            def unit_turn_g(f, s):
                u = f * UNITS + s
                pe.wait_ge(g_ready, u + 1)
                if u >= 2:
                    pe.wait_ge(gth_ready, u - 1)
                    pe.wait_ge(gtl_ready, u - 1)
                for j in range(2):
                    last = pe.transpose(ps_gt[u % 2][:, j * P:(j + 1) * P], g[:, u % 2, j * FH:(j + 1) * FH],
                                        ident[:, :])
                last.then_inc(gt_psum, 1)

            def unit_down(f, s, e):
                u = f * UNITS + s
                pe.wait_ge(gth_ready, u + 1)
                pe.wait_ge(gtl_ready, u + 1)
                if u >= 2:
                    pe.wait_ge(y_ready, u - 1)
                b = u % 2
                pairs = []
                for j in range(2):
                    at = e * (2 * D) + j * D
                    pairs.append((gth[:, b, j, :], gtl[:, b, j, :],
                                  w2h[:, bass.ds(at, D)], w2l[:, bass.ds(at, D)]))
                split3(ps_y[b], pairs).then_inc(y_psum, 1)

            def moe(f):
                unit_turn_x(f, 0)
                pe.wait_ge(expert_ready, f + 1)
                if f == 0:
                    pe.wait_ge(w_hi, NWG + NW2)
                    pe.wait_ge(w_lo, NWG + NW2)
                expert = {}
                for s in range(UNITS + 2):
                    if s < UNITS:
                        expert[s] = pe.value_load(ue[0:1, s:s + 1], min_val=0, max_val=E - 1)
                        unit_up(f, s, expert[s])
                    if 1 <= s <= UNITS:
                        unit_turn_g(f, s - 1)
                    if s + 1 < UNITS:
                        unit_turn_x(f, s + 1)
                    if s >= 2:
                        unit_down(f, s - 2, expert.pop(s - 2))

            pe.wait_ge(consts, N_CONST)
            for i in range(4):
                turn(0, i)
            route(0)
            moe(0)

            for i in range(4):
                turn(1, i)
            pe.wait_ge(w_hi, NWG + NW2 + 2)
            pe.wait_ge(w_lo, NWG + NW2 + 2)
            for c in range(NC):
                for h in range(NH):
                    n = NH * c + h
                    pe.wait_ge(xt_ready, 4 + 2 * h + 2)
                    pe.wait_ge(xtl_ready, 2 * h + 2)
                    if n >= 2:
                        pe.wait_ge(conv_sum, n - 1)
                    col = DI + c * P
                    pairs = [(winh[:, k, col:col + P], winl[:, k, col:col + P],
                              xTh[:, 4 * h:4 * h + 4, k, :], xTl[:, 4 * h:4 * h + 4, k, :]) for k in range(KD)]
                    split3(bank[2 + n % 2][:, :].rearrange("p (t n) -> p t n", t=4), pairs).then_inc(proj_psum, 1)
            for t in range(NT):
                pairs = [(xTh[:, t, k, :], xTl[:, t, k, :], winh[:, k, DI + CONVD:NPROJ],
                          winl[:, k, DI + CONVD:NPROJ]) for k in range(KD)]
                last = split3(bank[5][:, t * NHEADS:(t + 1) * NHEADS], pairs)
            last.then_inc(dt_psum, 1)
            for t in range(NT):
                if t < 2:
                    pe.wait_ge(conv_sum, NC * NH - 1 + t)
                else:
                    pe.wait_ge(z_ready, t - 1)
                pairs = [(xTh[:, t, k, :], xTl[:, t, k, :], winh[:, k, 0:DI], winl[:, k, 0:DI])
                         for k in range(KD)]
                split3(bank[2 + t % 2][:, :], pairs).then_inc(z_psum, 1)
            pe.wait_ge(da_ready, 1)
            daf = da[:, :, :].rearrange("p t h -> p (t h)")
            pe.matmul(bank[5][:, 64:128], tri[:, :], daf, start=True, stop=True).then_inc(cum_psum, 1)
            pe.matmul(bank[5][:, 128:192], after[:, :], daf, start=True, stop=True).then_inc(cum_psum, 1)

            def front(t):
                if t == 0:
                    pe.wait_ge(conv_ready, NC * NH)
                if t >= 1:
                    pe.wait_ge(xs_ready, t)
                    pe.wait_ge(xdt_ready, t)
                tok = slice(t * P, (t + 1) * P)
                for c in range(KI):
                    last = pe.transpose(bank[0][:, c * P:(c + 1) * P], conv[:, c, tok], ident[:, :])
                last.then_inc(xtok_psum, 1)
                if t >= 1:
                    pe.wait_ge(cbm_ready, t)
                if t % 2 == 0:
                    pe.transpose(bank[1][:, 0:P], conv[:, KI, tok], ident[:, :])
                pe.matmul(bank[1][:, P:2 * P], conv[:, KI, tok], conv[:, KI + 1, tok], start=True, stop=True)\
                    .then_inc(cb_psum, 1)
                pe.wait_ge(seg_in, t + 1)
                hh = NHEADS // 2
                for i in range(2):
                    if t >= 1:
                        pe.wait_ge(dec_ready, 2 * t - 1 + i)
                    else:
                        pe.wait_ge(z_ready, NT - 1 + i)
                    pe.matmul(bank[2 + i][:, :], after[:, :],
                              segm[:, t % 2, i * hh:(i + 1) * hh, :].rearrange("p h l -> p (h l)"),
                              start=True, stop=True).then_inc(seg_psum, 1)

            def mid(t):
                tok = slice(t * P, (t + 1) * P)
                if t % 2 == 0:
                    pe.wait_ge(xde_ready, t // 2 + 1)
                    pe.wait_ge(btok_ready, t // 2 + 1)
                    if t >= 2:
                        pe.wait_ge(yf_ready, t // 2)
                    pe.matmul(bank[6][:, :], btok[:, :], xde[:, :], start=True, stop=True)\
                        .then_inc(state_psum, 1)
                else:
                    pe.wait_ge(state_ready, t // 2 + 1)
                    pe.matmul(bank[6][:, :], conv[:, KI + 1, tok], state[:, :], start=True, stop=True)\
                        .then_inc(yoff_psum, 1)
                pe.wait_ge(mm_ready, t + 1)
                pe.wait_ge(xdt_ready, t + 1)
                if t >= 1:
                    pe.wait_ge(yd_used, t)
                for h in range(NHEADS):
                    last = pe.matmul(bank[4][:, h * HD:(h + 1) * HD], mm[:, t % 2, h, :],
                                     xdt[:, t % 2, h * HD:(h + 1) * HD], start=True, stop=True)
                last.then_inc(ydiag_psum, 1)

            def back(t):
                pe.wait_ge(yg_ready, t + 1)
                if t >= 1:
                    pe.wait_ge(yth_ready, t)
                    pe.wait_ge(ytl_ready, t)
                else:
                    pe.wait_ge(cum_exp, 2)
                for k in range(KI):
                    last = pe.transpose(bank[5][:, k * P:(k + 1) * P], yg[:, t % 2, k * P:(k + 1) * P],
                                        ident[:, :])
                last.then_inc(yt_psum, 1)
                pe.wait_ge(yth_ready, t + 1)
                pe.wait_ge(ytl_ready, t + 1)
                if t >= 1:
                    pe.wait_ge(o_used, t)
                pairs = [(yth[:, k, :], ytl[:, k, :], wouth[:, k, :], woutl[:, k, :]) for k in range(KI)]
                split3(bank[7][:, 0:D], pairs).then_inc(o_psum, 1)

            front(0)
            for t in range(NT + 1):
                if t + 1 < NT:
                    front(t + 1)
                if t < NT:
                    mid(t)
                if t >= 1:
                    back(t - 1)

            for i in range(4):
                turn(2, i)
            route(1)
            moe(1)

        @block.vector
        def _(dve):
            own = Chain(dve_own)

            def settle():
                dve.wait_ge(dve_own, own.n)

            def normalise(q):
                for t in range(NT):
                    if q == 0 and t % (NT // 2) == 0:
                        dve.wait_ge(ld_x[t // (NT // 2)], 16)
                    own.add(dve.bn_stats(st[:, t, :], x_sb[:, t, :]))
                settle()
                for t in range(NT):
                    own.add(dve.bn_aggr(mv[:, t, :], st[:, t, :]))
                settle()
                dve.tensor_scalar(vare[:, :], mv[:, :, 1], EPS, None, ALU.add).then_inc(var_ready, 1)
                dve.wait_ge(rstd_ready, q + 1)
                for t in range(NT):
                    dve.tensor_scalar(xn[:, t, :], x_sb[:, t, :], mv[:, t, 0:1], rstd[:, t:t + 1],
                                      ALU.subtract, ALU.mult).then_inc(xn_ready, 1)

            def route(f):
                def over_e(a):
                    return a.unsqueeze(2).broadcast_to([P, NT, E])

                dve.wait_ge(logits_ready, f + 1)
                own.add(dve.tensor_reduce(lmax[:, :], ps_log, AX.X, ALU.max))
                settle()
                dve.tensor_tensor(gl[:, :, :], ps_log, over_e(lmax[:, :]), ALU.subtract).then_inc(gate_in, 1)
                dve.wait_ge(gate_exp, f + 1)
                own.add(dve.tensor_reduce(gsum[:, :], ge[:, :, :], AX.X, ALU.add))
                settle()
                own.add(dve.reciprocal(grec[:, :], gsum[:, :]))
                settle()
                own.add(dve.tensor_tensor(sc[:, :, :], ge[:, :, :], over_e(grec[:, :]), ALU.mult))
                settle()
                for t in range(NT):
                    own.add(dve.max(top[:, t, :], sc[:, t, :]))
                settle()
                for t in range(NT):
                    own.add(dve.max_index(topi[:, t, :], top[:, t, :], sc[:, t, :]))
                settle()
                for c in range(2):
                    own.add(dve.tensor_copy(idxf[:, c, :], topi[:, :, c]))
                settle()
                own.add(dve.tensor_tensor(
                    oh[:, :, :], idxf[:, :, :].rearrange("p c t -> p (c t)").unsqueeze(2).broadcast_to([P, TK, E]),
                    lanes[:, 0:E].unsqueeze(1).broadcast_to([P, TK, E]), ALU.is_equal))
                settle()
                own.add(dve.memset(m16[:, 0:NT - 1, :], 0.0))
                settle()
                dve.tensor_tensor(m16[:, NT - 1:2 * NT - 1, :], oh[:, 0:NT, :], oh[:, NT:TK, :], ALU.add).then_inc(mask_ready, 1)
                own.add(dve.tensor_tensor(wsum[:, :], top[:, :, 0], top[:, :, 1], ALU.add))
                settle()
                own.add(dve.tensor_scalar(wsum[:, :], wsum[:, :], TOPK_EPS, None, ALU.add))
                settle()
                own.add(dve.reciprocal(wrec[:, :], wsum[:, :]))
                settle()
                for c in range(2):
                    own.add(dve.scalar_tensor_tensor(out=cw[:, c, :], in0=top[:, :, c], scalar=0.5, in1=wrec[:, :],
                                                     op0=ALU.mult, op1=ALU.mult))
                dve.wait_ge(rank_ready, 2 * f + 2)
                own.add(dve.tensor_scalar(tr[:, :], ps_cnt, (P - 1) / 2.0, 1.0 / P, ALU.add, ALU.mult))
                settle()
                own.add(dve.tensor_scalar(tl[:, :], tr[:, :], ROUND, -ROUND, ALU.add, ALU.add))
                settle()
                own.add(dve.tensor_tensor_scan(incl[:, :], tl[:, :], zer[:, :], 0.0, ALU.add, ALU.add))
                settle()
                own.add(dve.tensor_tensor(base[:, :], incl[:, :], tl[:, :], ALU.subtract))
                settle()
                own.add(dve.scalar_tensor_tensor(out=slot[:, :, :],
                                                 in0=base[:, :].unsqueeze(1).broadcast_to([P, NT, E]),
                                                 scalar=float(P), in1=ps_rank, op0=ALU.mult, op1=ALU.add))
                settle()
                own.add(dve.tensor_tensor(osl[:, :, :].rearrange("p (c t) e -> p c (t e)", c=2),
                                          oh[:, :, :].rearrange("p (c t) e -> p c (t e)", c=2),
                                          slot[:, :, :].rearrange("p t e -> p (t e)").unsqueeze(1)
                                          .broadcast_to([P, 2, NT * E]), ALU.mult))
                settle()
                own.add(dve.tensor_reduce(slk[:, :], osl[:, :, :], AX.X, ALU.add))
                settle()
                own.add(dve.tensor_scalar(hif[:, :], slk[:, :], -(P - 1) / 2.0, 1.0 / P, ALU.add, ALU.mult))
                settle()
                own.add(dve.tensor_scalar(hi[:, :], hif[:, :], ROUND, -ROUND, ALU.add, ALU.add))
                settle()
                own.add(dve.scalar_tensor_tensor(out=lo[:, :], in0=hi[:, :], scalar=-float(P), in1=slk[:, :],
                                                 op0=ALU.mult, op1=ALU.add))
                own.add(dve.tensor_tensor(unit_oh[:, :, :], hi[:, :].unsqueeze(2).broadcast_to([P, TK, UNITS]),
                                          lanes[:, 0:UNITS].unsqueeze(1).broadcast_to([P, TK, UNITS]),
                                          ALU.is_equal))
                settle()
                own.add(dve.tensor_tensor(lane_oh[:, :, :], lo[:, :].unsqueeze(2).broadcast_to([P, TK, P]),
                                          lanes[:, :].unsqueeze(1).broadcast_to([P, TK, P]), ALU.is_equal))
                for a, ids in ((0, tokid), (1, rowid)):
                    own.add(dve.tensor_tensor(tab[:, :, a, :], unit_oh[:, :, :],
                                              ids[:, :].unsqueeze(2).broadcast_to([P, TK, UNITS]), ALU.mult))
                settle()
                dve.tensor_tensor(ule[:, :, :], incl[:, :].unsqueeze(1).broadcast_to([P, UNITS, E]),
                                  lanes[:, 0:UNITS].unsqueeze(2).broadcast_to([P, UNITS, E]), ALU.is_le)\
                   .then_inc(tab_in, 1)
                dve.wait_ge(tab_in, f + 1)
                own.add(dve.tensor_reduce(uef[:, :], ule[:, :, :], AX.X, ALU.add))
                settle()
                dve.tensor_scalar(ue[:, :], uef[:, :], float(E - 1), None, ALU.min).then_inc(expert_ready, 1)
                dve.wait_ge(tab_ready, f + 1)
                own.add(dve.tensor_copy(gidx[:, :], ps_tab[:, 0:UNITS]))
                dve.tensor_scalar(sidx[:, :], ps_tab[:, UNITS:2 * UNITS], BIG, None, ALU.add)\
                   .then_inc(dve_own, 1)
                own.n += 1
                settle()
                dve.tensor_copy(uem[:, :], uef[:, :]).then_inc(idx_ready, 1)

            def unit_x(f, s):
                u = f * UNITS + s
                dve.wait_ge(uxh_ready, u + 1)
                if u >= 2:
                    dve.wait_ge(h_ready, u - 1)
                dve.tensor_tensor(uxl[:, u % 2, :, :].rearrange("p k n -> p (k n)"), ps_xt[u % 2],
                                  uxh[:, u % 2, :, :].rearrange("p k n -> p (k n)").bitcast(F32),
                                  ALU.subtract).then_inc(uxl_ready, 1)

            def unit_gate(f, s):
                u = f * UNITS + s
                dve.wait_ge(sl_ready, u + 1)
                if u >= 2:
                    dve.wait_ge(gt_psum, u - 1)
                dve.tensor_tensor(g[:, u % 2, :], ps_h[u % 2][:, F:FF], sl[:, u % 2, :], ALU.mult)\
                   .then_inc(g_ready, 1)

            def unit_g(f, s):
                u = f * UNITS + s
                dve.wait_ge(gth_ready, u + 1)
                if u >= 2:
                    dve.wait_ge(y_psum, u - 1)
                dve.tensor_tensor(gtl[:, u % 2, :, :].rearrange("p k n -> p (k n)"), ps_gt[u % 2],
                                  gth[:, u % 2, :, :].rearrange("p k n -> p (k n)").bitcast(F32),
                                  ALU.subtract).then_inc(gtl_ready, 1)

            def unit_y(f, s):
                u = f * UNITS + s
                dve.wait_ge(y_psum, u + 1)
                if u >= YB:
                    dve.wait_ge(y_stored[u % YB], 16 * (u // YB))
                dve.tensor_copy(yo[:, u % YB, :], ps_y[u % 2]).then_inc(y_ready, 1)

            def moe(f):
                unit_x(f, 0)
                for s in range(UNITS + 2):
                    if s < UNITS:
                        unit_gate(f, s)
                    if 1 <= s <= UNITS:
                        unit_g(f, s - 1)
                    if s + 1 < UNITS:
                        unit_x(f, s + 1)
                    if s >= 2:
                        unit_y(f, s - 2)
                for c in range(2):
                    if c == 1:
                        settle()
                    for t in range(NT):
                        dve.wait_ge(y_back[t // (NT // 4)], 32 * (f + 1))
                        ins = dve.scalar_tensor_tensor(out=x_sb[:, t, :], in0=yin[:, c, t, :],
                                                       scalar=cw[:, c, t:t + 1], in1=x_sb[:, t, :],
                                                       op0=ALU.mult, op1=ALU.add)
                        if c == 0:
                            own.add(ins)
                        else:
                            ins.then_inc(x_done, 1)
                dve.wait_ge(x_done, NT * (f + 1))

            dve.wait_ge(consts, N_CONST)
            normalise(0)
            route(0)
            seg = EG * KD * FF
            for i in range(NWG):
                dve.wait_ge(w_hi, i + 1)
                at = slice(i * seg, (i + 1) * seg)
                dve.tensor_tensor(w1l[:, at], w1s[:, at], w1h[:, at].bitcast(F32), ALU.subtract).then_inc(w_lo, 1)
            seg = E // NW2 * 2 * D
            for i in range(NW2):
                dve.wait_ge(w_hi, NWG + i + 1)
                at = slice(i * seg, (i + 1) * seg)
                dve.tensor_tensor(w2l[:, at], w2s[:, at], w2h[:, at].bitcast(F32), ALU.subtract).then_inc(w_lo, 1)
            dve.wait_ge(ld_wout, 16)
            dve.wait_ge(ld_small, 16 * N_SMALL)
            for k in range(KI):
                dve.tensor_scalar(wouts[:, k, :], wouts[:, k, :], nsc[:, k:k + 1], None, ALU.mult)\
                   .then_inc(wout_scaled, 1)
            dve.wait_ge(w_hi, NWG + NW2 + 1)
            dve.tensor_tensor(winl[:, :, :], wins[:, :, :], winh[:, :, :].bitcast(F32), ALU.subtract).then_inc(w_lo, 1)
            dve.wait_ge(w_hi, NWG + NW2 + 2)
            dve.tensor_tensor(woutl[:, :, :], wouts[:, :, :], wouth[:, :, :].bitcast(F32), ALU.subtract).then_inc(w_lo, 1)
            moe(0)

            normalise(1)
            for i in range(4):
                dve.wait_ge(xt_ready, 4 + i + 1)
                dve.tensor_tensor(xTl[:, 2 * i:2 * i + 2, :, :].rearrange("p t k n -> p (t k n)"), tp[i % 2][:, :],
                                  xTh[:, 2 * i:2 * i + 2, :, :].rearrange("p t k n -> p (t k n)").bitcast(F32),
                                  ALU.subtract).then_inc(xtl_ready, 1)
            spans = 512 // SEQ
            for c in range(NC):
                for h in range(NH):
                    n = NH * c + h
                    dve.wait_ge(tap_ready, n + 1)
                    src = bank[2 + n % 2][:, :].rearrange("p (b s) -> p b s", b=spans)
                    dst = conv[:, c, 512 * h:512 * (h + 1)].rearrange("p (b s) -> p b s", b=spans)
                    for back in range(1, TAPS):
                        ins = dve.scalar_tensor_tensor(out=dst[:, :, back:SEQ], in0=src[:, :, 0:SEQ - back],
                                                       scalar=cwt[:, c, TAPS - 1 - back:TAPS - back],
                                                       in1=dst[:, :, back:SEQ], op0=ALU.mult, op1=ALU.add)
                        if back < TAPS - 1:
                            own.add(ins)
                            settle()
                        else:
                            ins.then_inc(conv_sum, 1)
            dve.wait_ge(dt_psum, 1)
            v = [P, NT, NHEADS]
            own.add(dve.tensor_tensor(dtx[:, :, :], bank[5][:, 0:NT * NHEADS].rearrange("p (t h) -> p t h", t=NT),
                                      dtb[:, :].unsqueeze(1).broadcast_to(v), ALU.add))
            settle()
            dve.scalar_tensor_tensor(out=dta[:, :, :], in0=dtx[:, :, :], scalar=-1.0, in1=dtx[:, :, :],
                                     op0=ALU.mult, op1=ALU.min).then_inc(dt_in, 1)
            dve.wait_ge(dt_exp, 1)
            own.add(dve.tensor_scalar(dtr[:, :, :], dtu[:, :, :], 2.0, None, ALU.add))
            settle()
            own.add(dve.reciprocal(dtp[:, :, :], dtr[:, :, :]))
            settle()
            own.add(dve.tensor_tensor(dts[:, :, :], dtu[:, :, :], dtp[:, :, :], ALU.mult))
            settle()
            own.add(dve.tensor_tensor(dtq[:, :, :], dts[:, :, :], dts[:, :, :], ALU.mult))
            settle()
            own.add(dve.tensor_scalar(dtp[:, :, :], dtq[:, :, :], ATANH[-1], None, ALU.mult))
            settle()
            for coef in ATANH[-2:0:-1]:
                own.add(dve.scalar_tensor_tensor(out=dtp[:, :, :], in0=dtp[:, :, :], scalar=coef,
                                                 in1=dtq[:, :, :], op0=ALU.add, op1=ALU.mult))
                settle()
            own.add(dve.scalar_tensor_tensor(out=dtr[:, :, :], in0=dtp[:, :, :], scalar=1.0, in1=dts[:, :, :],
                                             op0=ALU.add, op1=ALU.mult))
            own.add(dve.tensor_scalar(dta[:, :, :], dtx[:, :, :], 0.0, None, ALU.max))
            settle()
            own.add(dve.scalar_tensor_tensor(out=dtv[:, :, :], in0=dtr[:, :, :], scalar=2.0, in1=dta[:, :, :],
                                             op0=ALU.mult, op1=ALU.add))
            settle()
            dve.wait_ge(a_exp, 1)
            dve.scalar_tensor_tensor(out=da[:, :, :], in0=dtv[:, :, :], scalar=-1.0,
                                     in1=aexp[:, :].unsqueeze(1).broadcast_to(v), op0=ALU.mult, op1=ALU.mult)\
               .then_inc(da_ready, 1)

            def heads(a):
                return a.rearrange("p (h d) -> p h d", h=NHEADS)

            def front(t):
                dve.wait_ge(xs_ready, t + 1)
                if t >= 2:
                    dve.wait_ge(ydiag_psum, t - 1)
                    if t % 2 == 0:
                        dve.wait_ge(xde_ready, t // 2)
                dve.tensor_tensor(heads(xdt[:, t % 2, :]), heads(bank[0][:, :]),
                                  dtv[:, t, :].unsqueeze(2).broadcast_to([P, NHEADS, HD]), ALU.mult)\
                   .then_inc(xdt_ready, 1)
                dve.wait_ge(cb_psum, t + 1)
                dve.wait_ge(btok_ready, t // 2 + 1)
                if t >= 2:
                    dve.wait_ge(mm_ready, t - 1)
                dve.tensor_tensor(cbm[:, t % 2, :], bank[1][:, P:2 * P], tri[:, :], ALU.mult)\
                   .then_inc(cbm_ready, 1)
                dve.wait_ge(cbm_ready, t + 1)
                dve.wait_ge(dec_ready, 2 * t + 2)
                dve.tensor_tensor(mm[:, t % 2, :, :], dec[:, :, :],
                                  cbm[:, t % 2, :].unsqueeze(1).broadcast_to([P, NHEADS, P]), ALU.mult)\
                   .then_inc(mm_ready, 1)

            def mid(t):
                dve.wait_ge(ydiag_psum, t + 1)
                dve.wait_ge(xd_ready, t + 1)
                if t >= 1:
                    dve.wait_ge(yg_ready, t)
                dve.tensor_tensor(y1[:, :], bank[4][:, :], xd[:, :], ALU.add).then_inc(yd_used, 1)
                if t % 2 == 1:
                    dve.wait_ge(yoff_psum, t // 2 + 1)
                    dve.tensor_tensor(heads(yf[:, :]), heads(bank[6][:, :]),
                                      ecum[:, t, :].unsqueeze(2).broadcast_to([P, NHEADS, HD]), ALU.mult)\
                       .then_inc(yf_ready, 1)
                    dve.wait_ge(yf_ready, t // 2 + 1)
                    dve.wait_ge(yd_used, t + 1)
                    own.add(dve.tensor_tensor(y1[:, :], y1[:, :], yf[:, :], ALU.add))
                    settle()
                else:
                    dve.wait_ge(yd_used, t + 1)
                if t >= 2:
                    dve.wait_ge(yt_psum, t - 1)
                    dve.wait_ge(ssq_ready, t - 1)
                dve.tensor_tensor(yg[:, t % 2, :], y1[:, :], sz[:, t, :], ALU.mult).then_inc(yg_ready, 1)

            def back(t):
                dve.wait_ge(ssq_ready, t + 1)
                dve.tensor_scalar(vy[:, t:t + 1], ssq[:, t:t + 1], 1.0 / DI, EPS, ALU.mult, ALU.add)\
                   .then_inc(vy_ready, 1)
                dve.wait_ge(yth_ready, t + 1)
                if t >= 1:
                    dve.wait_ge(o_psum, t)
                dve.tensor_tensor(ytl[:, :, :].rearrange("p k n -> p (k n)"), bank[5][:, :],
                                  yth[:, :, :].rearrange("p k n -> p (k n)").bitcast(F32), ALU.subtract)\
                   .then_inc(ytl_ready, 1)
                dve.wait_ge(o_psum, t + 1)
                dve.wait_ge(ry_ready, t + 1)
                dve.scalar_tensor_tensor(out=x_sb[:, t, :], in0=bank[7][:, 0:D], scalar=ry[:, t:t + 1],
                                         in1=x_sb[:, t, :], op0=ALU.mult, op1=ALU.add).then_inc(o_used, 1)

            front(0)
            for t in range(NT + 1):
                if t + 1 < NT:
                    front(t + 1)
                if t < NT:
                    mid(t)
                if t >= 1:
                    back(t - 1)
            dve.wait_ge(o_used, NT)

            normalise(2)
            route(1)
            moe(1)


_PRE = "L0_attn_"


def kernel(**inputs):
    import concourse.bacc as bacc
    from concourse.bass_utils import run_bass_kernel_spmd

    get = {k: np.asarray(v) for k, v in inputs.items()}
    u = get["L0_attn_u"]
    conv_w = get["L0_attn_conv_w"]
    row = lambda a: np.ascontiguousarray(a.reshape(1, -1))
    cols = lambda a: np.ascontiguousarray(a.reshape(-1, P).T)
    arrays = {
        "u": np.ascontiguousarray(u.reshape(-1, u.shape[-1])),
        "w_in": np.ascontiguousarray(get["L0_attn_W_in"]),
        "conv_w": np.ascontiguousarray(conv_w.T[None]),
        "conv_b": cols(get["L0_attn_conv_b"]),
        "dt_bias": row(get["L0_attn_dt_bias"]),
        "a_log": row(get["L0_attn_A_log"]),
        "d_skip": row(get["L0_attn_D"]),
        "norm_scale": cols(get["L0_attn_norm_scale"]),
        "w_out": np.ascontiguousarray(get["L0_attn_W_out"]),
        "wg_t": np.ascontiguousarray(get["L0_ffn_wg"].T),
        "w1": np.ascontiguousarray(get["L0_ffn_w1"]),
        "w2": np.ascontiguousarray(get["L0_ffn_w2"]),
    }
    nc = bacc.Bacc("TRN2", target_bir_lowering=False, num_devices=1)
    args = [nc.dram_tensor(n, a.shape, mybir.dt.from_np(a.dtype), kind="ExternalInput").ap()
            for n, a in arrays.items()]
    out = nc.dram_tensor("out", arrays["u"].shape, F32, kind="ExternalOutput").ap()
    build(nc, *args, out)
    r = run_bass_kernel_spmd(nc, [arrays], core_ids=[0])
    return r.results[0]["out"].reshape(u.shape)
```

```python
from contextlib import ExitStack

import numpy as np
import concourse.bass as bass
from concourse import mybir

F32 = mybir.dt.float32
F32R = mybir.dt.float32r
BF16 = mybir.dt.bfloat16
I32 = mybir.dt.int32
U32 = mybir.dt.uint32
ALU = mybir.AluOpType
ACT = mybir.ActivationFunctionType
AX = mybir.AxisListType

P = 128
XG = 6
LEAD = 3
YB = 3
BIG = 4096.0
ROUND = 12582912.0
EPS = 1e-5
TOPK_EPS = 1e-20
ATANH = [1.0 / (2 * i + 1) for i in range(8)]


class Chain:

    def __init__(self, sem):
        self.sem, self.n = sem, 0

    def add(self, ins):
        ins.then_inc(self.sem, 1)
        self.n += 1


def build(nc, u_in, w_in, conv_w, conv_b, dt_bias, a_log, d_skip, norm_scale, w_out, wg_t, w1, w2, out):
    T, D = u_in.shape
    NT = T // P
    KD = D // P
    E, _, FF = w1.shape
    F = FF // 2
    FH = F // 2
    DI = w_out.shape[0]
    KI = DI // P
    NHEADS = a_log.shape[1]
    HD = DI // NHEADS
    CONVD = conv_w.shape[1]
    NC = CONVD // P
    TAPS = conv_w.shape[2]
    NPROJ = w_in.shape[1]
    SEQ = 2 * P
    NH = T // 512
    UNITS = 2 * NT + E - 1
    TK = 2 * NT
    EG = 2
    NWG = E // EG
    NW2 = 2
    NWP = 2
    SEG1, SEG2 = EG * KD * FF, E // NW2 * 2 * D
    ORDER = [KI, KI + 1] + list(range(KI))
    DT_AT = 5

    xn_dram = nc.dram_tensor("xn_rows", (T, D), F32, kind="Internal").ap()
    y_dram = nc.dram_tensor("y_rows", (2 * T, D), F32, kind="Internal").ap()

    ctx = ExitStack()
    with ctx:
        def sb(name, shape, dt=F32):
            return ctx.enter_context(nc.sbuf_tensor(name, shape, dt))

        def sem(name):
            return ctx.enter_context(nc.semaphore(name))

        W1F, W2F = E * KD * FF, E * 2 * D
        x_sb = sb("x_sb", [P, NT, D])
        w1h = sb("w1h", [P, W1F], F32R)
        w2h = sb("w2h", [FH, W2F], F32R)
        winh = sb("winh", [P, KD, NPROJ], F32R)
        wouth = sb("wouth", [P, KI, D], F32R)

        def landing(name, shape):
            with nc.sbuf_tensor(name + "s", shape, F32) as raw:
                pass
            return raw, sb(name + "l", shape, F32R)

        w1s, w1l = landing("w1", [P, W1F])
        w2s, w2l = landing("w2", [FH, W2F])
        with nc.sbuf_tensor("xn_late", [P, NT, D], F32) as xn_late:
            pass
        wins, winl = landing("win", [P, KD, NPROJ])
        wouts, woutl = landing("wout", [P, KI, D])

        ident = sb("ident", [P, P])
        tri = sb("tri", [P, P])
        after = sb("after", [P, P])
        before16 = sb("before16", [P, P], BF16)
        ones16 = sb("ones16", [P, P], BF16)
        lanes = sb("lanes", [P, UNITS])
        lanes16 = sb("lanes16", [P, P], BF16)
        prow = sb("prow", [P, 1])
        blk_id = sb("blk_id", [P, TK])
        mhalf = sb("mhalf", [P, NT])

        st = sb("st", [P, NT, 6])
        mv = sb("mv", [P, NT, 2])
        vare = sb("vare", [P, NT])
        rstd = sb("rstd", [P, NT])
        wgt = sb("wgt", [P, KD, E])
        idxf = sb("idxf", [P, 2, NT])
        wsum = sb("wsum", [P, NT])
        wrec = sb("wrec", [P, NT])
        cw = sb("cw", [P, 2, NT])
        tl = sb("tl", [P, E])
        tr = sb("tr", [P, E])
        incl = sb("incl", [P, E])
        base = sb("base", [P, E])
        zer = sb("zer", [P, E])
        slk = sb("slk", [P, TK])
        hif = sb("hif", [P, TK])
        hi = sb("hi", [P, TK])
        lo = sb("lo", [P, TK])
        urow = sb("urow", [P, UNITS])
        srow = sb("srow", [P, UNITS])
        cofs = sb("cofs", [P, UNITS])
        gidx = sb("gidx", [P, UNITS], I32)
        sidx = sb("sidx", [P, UNITS], I32)
        uef = sb("uef", [P, UNITS])
        ue = sb("ue", [P, UNITS], I32)
        cwt = sb("cwt", [P, NC, TAPS])
        cbt = sb("cbt", [P, NC])
        dtb = sb("dtb", [P, NHEADS])
        alog = sb("alog", [P, NHEADS])
        dsk = sb("dsk", [P, NHEADS])
        nsc = sb("nsc", [P, KI])
        ssq = sb("ssq", [P, NT])
        vy = sb("vy", [P, NT])
        ry = sb("ry", [P, NT])

        with nc.sbuf_tensor("xn", [P, NT, D], F32) as xn:
            pass
        xdt = sb("xdt", [P, 2, DI])
        yg = sb("yg", [P, 2, DI])

        with ExitStack() as ffn:
            def fb(name, shape, dt=F32):
                return ffn.enter_context(nc.sbuf_tensor(name, shape, dt))

            xT = fb("xT", [P, NT, KD, P])
            lane_oh = fb("lane_oh", [P, TK, P], BF16)
            yin = fb("yin", [P, 2, NT, D])
            unit_oh = fb("unit_oh", [P, TK, UNITS])
            tab = fb("tab", [P, 2, TK, UNITS], BF16)
            lmax = fb("lmax", [P, NT])
            gl = fb("gl", [P, NT, E])
            ge = fb("ge", [P, NT, E])
            gsum = fb("gsum", [P, NT])
            grec = fb("grec", [P, NT])
            sc = fb("sc", [P, NT, E])
            top = fb("top", [P, NT, 8])
            topi = fb("topi", [P, NT, 8], U32)
            oh = fb("oh", [P, TK, E])
            m16 = fb("m16", [P, 2 * NT - 1, E], BF16)
            slot = fb("slot", [P, NT, E])
            osl = fb("osl", [P, TK, E])
            ule = fb("ule", [P, UNITS, E])
            xg = fb("xg", [P, XG, D])
            uxh = fb("uxh", [P, 2, KD, P], F32R)
            uxl = fb("uxl", [P, 2, KD, P], F32R)
            sl = fb("sl", [P, 2, F])
            g = fb("g", [P, 2, F])
            gth = fb("gth", [FH, 2, 2, P], F32R)
            gtl = fb("gtl", [FH, 2, 2, P], F32R)
            yo = fb("yo", [P, YB, D])

        conv = sb("conv", [P, NC, T])
        sz = sb("sz", [P, NT, DI])
        with nc.sbuf_tensor("xTh", [P, NT, KD, P], F32R) as xTh, nc.sbuf_tensor("xTl", [P, NT, KD, P], F32R) as xTl:
            pass
        segm = sb("segm", [P, 2, NHEADS, P])
        mm = sb("mm", [P, 2, NHEADS, P])
        aexp = sb("aexp", [P, NHEADS])
        dtx = sb("dtx", [P, NT, NHEADS])
        dta = sb("dta", [P, NT, NHEADS])
        dtu = sb("dtu", [P, NT, NHEADS])
        dtr = sb("dtr", [P, NT, NHEADS])
        dts = sb("dts", [P, NT, NHEADS])
        dtq = sb("dtq", [P, NT, NHEADS])
        dtp = sb("dtp", [P, NT, NHEADS])
        dtv = sb("dtv", [P, NT, NHEADS])
        da = sb("da", [P, NT, NHEADS])
        ecum = sb("ecum", [P, NT, NHEADS])
        eend = sb("eend", [P, NT, NHEADS])
        dec = sb("dec", [P, NHEADS, P])
        cbm = sb("cbm", [P, 2, P])
        xs = sb("xs", [P, DI])
        xd = sb("xd", [P, DI])
        xde = sb("xde", [P, DI])
        btok = sb("btok", [P, P])
        state = sb("state", [P, DI])
        y1 = sb("y1", [P, DI])
        yf = sb("yf", [P, DI])
        ysq = sb("ysq", [P, DI])
        yth = sb("yth", [P, KI, P], F32R)
        ytl = sb("ytl", [P, KI, P], F32R)

        bank = [ctx.enter_context(nc.psum_tensor(f"bank{i}", [P, 512], F32)) for i in range(8)]
        ps_turn = [bank[0], bank[1], bank[2]]
        GT = NT // 2
        ps_log = [bank[3 + i][:, 0:GT * E].rearrange("p (t e) -> p t e", t=GT) for i in range(2)]
        ps_rank = bank[6][:, 0:NT * E].rearrange("p (t e) -> p t e", t=NT)
        ps_cnt = bank[7][:, 0:E]
        ps_tab = bank[5][:, 0:2 * UNITS]
        ps_xt = [bank[0][:, 0:D], bank[1][:, 0:D]]
        ps_h = [bank[2][:, 0:FF], bank[3][:, 0:FF]]
        ps_y = [bank[4][:, 0:D], bank[5][:, 0:D]]
        ps_gt = [bank[6][0:FH, 0:2 * P], bank[7][0:FH, 0:2 * P]]
        ps_proj = [bank[3], bank[4]]
        ps_z = [bank[5], bank[6]]
        TH = NT * NHEADS
        ps_dt, ps_cum, ps_end = (bank[7][:, i * TH:(i + 1) * TH] for i in range(3))
        ps_xtok = bank[0]
        ps_btok, ps_cb = bank[1][:, 0:P], bank[1][:, P:2 * P]
        ps_seg = [bank[2], bank[3]]
        ps_ydiag = bank[4]
        ps_yt = bank[5]
        ps_state = ps_yoff = bank[6]
        ps_o = bank[7][:, 0:D]

        ld_x = [sem(f"ld_x{i}") for i in range(2)]
        ld_wg = sem("ld_wg")
        ld_small = sem("ld_small")
        ld_w1 = [sem(f"ld_w1_{i}") for i in range(NWG)]
        ld_w2 = [sem(f"ld_w2_{i}") for i in range(NW2)]
        ld_win = sem("ld_win")
        ld_wout = sem("ld_wout")
        consts = sem("consts")
        w_hi = sem("w_hi")
        w_lo = sem("w_lo")
        w_lo_pool = sem("w_lo_pool")
        wout_scaled = sem("wout_scaled")
        dve_own = sem("dve_own")
        act_own = sem("act_own")
        pool_own = sem("pool_own")
        var_ready = sem("var_ready")
        rstd_ready = sem("rstd_ready")
        xn_ready = sem("xn_ready")
        xn_stored = sem("xn_stored")
        xt_psum = sem("xt_psum")
        xt_ready = sem("xt_ready")
        xtl_ready = sem("xtl_ready")
        logits_ready = sem("logits_ready")
        gate_in = sem("gate_in")
        gate_exp = sem("gate_exp")
        mask_ready = sem("mask_ready")
        rank_ready = sem("rank_ready")
        tab_in = sem("tab_in")
        tab_ready = sem("tab_ready")
        idx_ready = sem("idx_ready")
        expert_ready = sem("expert_ready")
        xg_landed = [sem(f"xg_landed{i}") for i in range(XG)]
        uxt_psum = sem("uxt_psum")
        uxh_ready = sem("uxh_ready")
        uxl_ready = sem("uxl_ready")
        h_ready = sem("h_ready")
        sl_ready = sem("sl_ready")
        g_ready = sem("g_ready")
        gt_psum = sem("gt_psum")
        gth_ready = sem("gth_ready")
        gtl_ready = sem("gtl_ready")
        y_psum = sem("y_psum")
        y_ready = sem("y_ready")
        y_stored = [sem(f"y_stored{i}") for i in range(YB)]
        y_back = [sem(f"y_back{i}") for i in range(4)]
        x_done = sem("x_done")
        out_stored = sem("out_stored")
        proj_psum = sem("proj_psum")
        tap_ready = sem("tap_ready")
        conv_sum = sem("conv_sum")
        conv_ready = sem("conv_ready")
        z_psum = sem("z_psum")
        z_ready = sem("z_ready")
        dt_psum = sem("dt_psum")
        dt_in = sem("dt_in")
        dt_exp = sem("dt_exp")
        a_exp = sem("a_exp")
        da_ready = sem("da_ready")
        cum_psum = sem("cum_psum")
        cum_exp = sem("cum_exp")
        xtok_psum = sem("xtok_psum")
        cb_psum = sem("cb_psum")
        seg_in = sem("seg_in")
        seg_psum = sem("seg_psum")
        xs_ready = sem("xs_ready")
        btok_ready = sem("btok_ready")
        dec_ready = sem("dec_ready")
        cbm_ready = sem("cbm_ready")
        mm_ready = sem("mm_ready")
        xdt_ready = sem("xdt_ready")
        xd_ready = sem("xd_ready")
        xde_ready = sem("xde_ready")
        ydiag_psum = sem("ydiag_psum")
        state_psum = sem("state_psum")
        state_ready = sem("state_ready")
        yoff_psum = sem("yoff_psum")
        yd_used = sem("yd_used")
        yf_ready = sem("yf_ready")
        yg_ready = sem("yg_ready")
        ssq_ready = sem("ssq_ready")
        vy_ready = sem("vy_ready")
        ry_ready = sem("ry_ready")
        yt_psum = sem("yt_psum")
        yth_ready = sem("yth_ready")
        ytl_ready = sem("ytl_ready")
        o_psum = sem("o_psum")
        o_used = sem("o_used")

        N_CONST = 11
        N_SMALL = 6

        block = ctx.enter_context(nc.Block())

        @block.sync
        def _(sp):
            xv = u_in.rearrange("(t p) d -> p t d", p=P)
            half = NT // 2
            for i in range(2):
                sp.dma_start(x_sb[:, i * half:(i + 1) * half, :], xv[:, i * half:(i + 1) * half, :])\
                  .then_inc(ld_x[i], 16)
            sp.dma_start(wgt[:, :, :], wg_t.rearrange("(k p) e -> p k e", p=P)).then_inc(ld_wg, 16)
            w1v = w1.rearrange("e (k p) f -> p e k f", p=P)
            w1sv = w1s[:, :].rearrange("p (e k f) -> p e k f", e=E, k=KD)
            for e in range(E):
                sp.dma_start(w1sv[:, e, :, :], w1v[:, e, :, :]).then_inc(ld_w1[e // EG], 16)
            w2v = w2.rearrange("e (j p) d -> p e j d", p=FH)
            w2sv = w2s[:, :].rearrange("p (e j d) -> p e j d", e=E, j=2)
            for e in range(E):
                sp.dma_start(w2sv[:, e, :, :], w2v[:, e, :, :]).then_inc(ld_w2[e // (E // NW2)], 16)

            def store_rows(q, src):
                for i in range(NT // 2):
                    sp.wait_ge(xn_ready, NT * q + 2 * i + 2)
                    dst = xn_dram[2 * i * P:2 * (i + 1) * P, :].rearrange("(t p) d -> p t d", p=P)
                    sp.dma_start(dst, src[:, 2 * i:2 * i + 2, :]).then_inc(xn_stored, 16)

            def fetch_rows(f):
                for i in range(YB):
                    uses = len([u for u in range(UNITS * (f + 1)) if u % YB == i])
                    sp.wait_ge(y_stored[i], 16 * uses)
                yv = y_dram.rearrange("(c t p) d -> p c t d", c=2, p=P)
                for i in range(NT // 2):
                    for c in range(2):
                        sp.dma_start(yin[:, c, 2 * i:2 * i + 2, :], yv[:, c, 2 * i:2 * i + 2, :])\
                          .then_inc(y_back[i], 16)

            store_rows(0, xn)
            sp.dma_start(cwt[:, :, :], conv_w.rearrange("a n k -> (a n) k").rearrange("(c p) k -> p c k", p=P))\
              .then_inc(ld_small, 16)
            sp.dma_start(cbt[:, :], conv_b).then_inc(ld_small, 16)
            sp.dma_start(nsc[:, :], norm_scale).then_inc(ld_small, 16)
            for dst, src in ((dtb, dt_bias), (alog, a_log), (dsk, d_skip)):
                sp.dma_start(dst[:, :], src.broadcast_to([P, NHEADS])).then_inc(ld_small, 16)
            sp.dma_start(wins[:, :, :], w_in.rearrange("(k p) n -> p k n", p=P)).then_inc(ld_win, 16)
            sp.dma_start(wouts[:, :, :], w_out.rearrange("(k p) n -> p k n", p=P)).then_inc(ld_wout, 16)
            fetch_rows(0)
            store_rows(2, xn_late)
            fetch_rows(1)
            for t in range(NT):
                sp.wait_ge(x_done, NT + t + 1)
                sp.dma_start(out[t * P:(t + 1) * P, :], x_sb[:, t, :]).then_inc(out_stored, 16)
            sp.wait_ge(out_stored, 16 * NT)

        @block.gpsimd
        def _(pool):
            own = Chain(pool_own)

            def select(dst, fill, compare, pattern, base, mult):
                pool.affine_select(out=dst, in_=dst, compare_op=compare, fill=fill, base=base,
                                   pattern=pattern, channel_multiplier=mult).then_inc(consts, 1)

            pool.memset(mhalf[:, :], -0.5).then_inc(consts, 1)
            own.add(pool.memset(ident[:, :], 0.0))
            own.add(pool.memset(tri[:, :], 1.0))
            own.add(pool.memset(after[:, :], 1.0))
            own.add(pool.memset(before16[:, :], 1.0))
            pool.memset(ones16[:, :], 1.0).then_inc(consts, 1)
            pool.memset(zer[:, :], 0.0).then_inc(consts, 1)
            pool.wait_ge(pool_own, own.n)
            select(ident[:, :], 1.0, ALU.not_equal, [[-1, P]], 0, 1)
            select(tri[:, :], 0.0, ALU.is_ge, [[1, P]], 0, -1)
            select(after[:, :], 0.0, ALU.is_gt, [[-1, P]], 0, 1)
            select(before16[:, :], 0.0, ALU.is_gt, [[1, P]], 0, -1)
            iota = dict(allow_small_or_imprecise_dtypes=True)
            pool.iota(lanes[:, :], pattern=[[1, UNITS]], base=0, channel_multiplier=0, **iota).then_inc(consts, 1)
            pool.iota(lanes16[:, :], pattern=[[1, P]], base=0, channel_multiplier=0, **iota).then_inc(consts, 1)
            pool.iota(prow[:, :], pattern=[[0, 1]], base=0, channel_multiplier=1, **iota).then_inc(consts, 1)
            pool.iota(blk_id[:, :], pattern=[[1, TK]], base=-int(BIG) // P, channel_multiplier=0, **iota)\
                .then_inc(consts, 1)

            def deviation(q, i):
                n = NT // 2 * q + i
                pool.wait_ge(var_ready, n + 1)
                pool.tensor_tensor(rstd[:, 2 * i:2 * i + 2], vare[:, 2 * i:2 * i + 2], mhalf[:, 0:2], ALU.pow)\
                    .then_inc(rstd_ready, 1)

            def gather(f, s):
                u = f * UNITS + s
                if s == 0:
                    pool.wait_ge(idx_ready, f + 1)
                    pool.wait_ge(xn_stored, 16 * (NT // 2) * (f + 1))
                if u >= XG:
                    pool.wait_ge(uxt_psum, u - XG + 1)
                pool.indirect_dma_start(xg[:, u % XG, :], None, xn_dram,
                                        bass.IndirectOffsetOnAxis(ap=gidx[:, s:s + 1], axis=0))\
                    .then_inc(xg_landed[u % XG], 16)

            def scatter(f, s):
                u = f * UNITS + s
                pool.wait_ge(y_ready, u + 1)
                pool.indirect_dma_start(y_dram, bass.IndirectOffsetOnAxis(ap=sidx[:, s:s + 1], axis=0),
                                        yo[:, u % YB, :], None, bounds_check=2 * T - 1, oob_is_err=False)\
                    .then_inc(y_stored[u % YB], 16)

            def moe(f):
                for s in range(XG + LEAD):
                    gather(f, s)
                for s in range(UNITS):
                    scatter(f, s)
                    if s + XG + LEAD < UNITS:
                        gather(f, s + XG + LEAD)

            def low_part(l, s_, h, at, n):
                pool.wait_ge(w_hi, n)
                pool.tensor_tensor(l[:, at], s_[:, at], h[:, at].bitcast(F32), ALU.subtract)\
                    .then_inc(w_lo_pool, 1)

            def seg_input(t):
                if t == 0:
                    pool.wait_ge(da_ready, 1)
                    pool.wait_ge(z_psum, NT)
                    pool.wait_ge(proj_psum, NC * NH)
                if t >= 2:
                    pool.wait_ge(seg_psum, 2 * (t - 1))
                pool.tensor_tensor(segm[:, t % 2, :, :], tri[:, :].unsqueeze(1).broadcast_to([P, NHEADS, P]),
                                   da[:, t, :].unsqueeze(2).broadcast_to([P, NHEADS, P]), ALU.mult)\
                    .then_inc(seg_in, 1)

            def skip_input(t):
                pool.wait_ge(xs_ready, t + 1)
                if t >= 1:
                    pool.wait_ge(yd_used, t)
                pool.tensor_tensor(xd[:, :].rearrange("p (h d) -> p h d", h=NHEADS),
                                   xs[:, :].rearrange("p (h d) -> p h d", h=NHEADS),
                                   dsk[:, :].unsqueeze(2).broadcast_to([P, NHEADS, HD]), ALU.mult)\
                    .then_inc(xd_ready, 1)

            def state_input(t):
                pool.wait_ge(xdt_ready, t + 1)
                if t == 0:
                    pool.wait_ge(cum_exp, 2)
                if t >= 2:
                    pool.wait_ge(state_psum, t // 2)
                pool.tensor_tensor(xde[:, :].rearrange("p (h d) -> p h d", h=NHEADS),
                                   xdt[:, t % 2, :].rearrange("p (h d) -> p h d", h=NHEADS),
                                   eend[:, t, :].unsqueeze(2).broadcast_to([P, NHEADS, HD]), ALU.mult)\
                    .then_inc(xde_ready, 1)

            def y_deviation(t):
                pool.wait_ge(vy_ready, t + 1)
                pool.tensor_tensor(ry[:, t:t + 1], vy[:, t:t + 1], mhalf[:, 0:1], ALU.pow)\
                    .then_inc(ry_ready, 1)

            pool.wait_ge(consts, N_CONST)
            for i in range(NT // 2):
                deviation(0, i)
            for i in range(NWG - NWP, NWG):
                low_part(w1l, w1s, w1h, slice(i * SEG1, (i + 1) * SEG1), i + 1)
            for i in range(NW2):
                low_part(w2l, w2s, w2h, slice(i * SEG2, (i + 1) * SEG2), NWG + i + 1)
            moe(0)
            for i in range(NT // 2):
                deviation(1, i)
            seg_input(0)
            seg_input(1)
            for i in range(NT + 3):
                if i < NT:
                    if i % 2 == 0:
                        state_input(i)
                    if i + 2 < NT:
                        seg_input(i + 2)
                if 2 <= i < NT + 2:
                    y_deviation(i - 2)
                if i < NT:
                    skip_input(i)
                if i >= 4 and i % 2 == 0:
                    deviation(2, i // 2 - 2)
            moe(1)

        @block.scalar
        def _(act):
            def turned(q, i):
                act.wait_ge(xt_psum, NT // 2 * q + i + 1)
                dst = (xTh if q == 1 else xT)[:, 2 * i:2 * i + 2, :, :].rearrange("p t k n -> p (t k n)")
                act.activation(dst, ps_turn[i % 3][:, :], ACT.Copy).then_inc(xt_ready, 1)

            def gate(f, i):
                act.wait_ge(gate_in, 2 * f + i + 1)
                at = slice(i * GT, (i + 1) * GT)
                act.activation(ge[:, at, :], gl[:, at, :], ACT.Exp).then_inc(gate_exp, 1)

            def high_part(dst, src, ready=None, count=16):
                if ready is not None:
                    act.wait_ge(ready, count)
                act.activation(dst, src, ACT.Copy).then_inc(w_hi, 1)

            def unit_x(f, s):
                u = f * UNITS + s
                act.wait_ge(uxt_psum, u + 1)
                if u >= 2:
                    act.wait_ge(h_ready, u - 1)
                act.activation(uxh[:, u % 2, :, :].rearrange("p k n -> p (k n)"), ps_xt[u % 2], ACT.Copy)\
                    .then_inc(uxh_ready, 1)

            def unit_silu(f, s):
                u = f * UNITS + s
                act.wait_ge(h_ready, u + 1)
                if u >= 2:
                    act.wait_ge(g_ready, u - 1)
                act.activation(sl[:, u % 2, :], ps_h[u % 2][:, 0:F], ACT.Silu).then_inc(sl_ready, 1)

            def unit_g(f, s):
                u = f * UNITS + s
                act.wait_ge(gt_psum, u + 1)
                if u >= 2:
                    act.wait_ge(y_psum, u - 1)
                act.activation(gth[:, u % 2, :, :].rearrange("p k n -> p (k n)"), ps_gt[u % 2], ACT.Copy)\
                    .then_inc(gth_ready, 1)

            def moe(f):
                unit_x(f, 0)
                unit_x(f, 1)
                for s in range(UNITS + 1):
                    if s < UNITS:
                        unit_silu(f, s)
                    if s + 2 < UNITS:
                        unit_x(f, s + 2)
                    if s >= 1:
                        unit_g(f, s - 1)
                    if f == 0 and 4 <= s < 4 + 2 * KD:
                        k, part = divmod(s - 4, 2)
                        at = slice(part * NPROJ // 2, (part + 1) * NPROJ // 2)
                        high_part(winh[:, k, at], wins[:, k, at], ld_win)
                    if f == 0 and 10 <= s < 10 + KI:
                        high_part(wouth[:, s - 10, :], wouts[:, s - 10, :], wout_scaled, s - 9)

            act.wait_ge(consts, N_CONST)
            early = [(w1h[:, i * SEG1:(i + 1) * SEG1], w1s[:, i * SEG1:(i + 1) * SEG1], ld_w1[i], 16 * EG)
                     for i in range(NWG)]
            early += [(w2h[:, i * SEG2:(i + 1) * SEG2], w2s[:, i * SEG2:(i + 1) * SEG2], ld_w2[i],
                       16 * (E // NW2)) for i in range(NW2)]
            turned(0, 0)
            high_part(*early[0])
            turned(0, 1)
            high_part(*early[1])
            turned(0, 2)
            gate(0, 0)
            turned(0, 3)
            high_part(*early[2])
            gate(0, 1)
            for e in early[3:]:
                high_part(*e)
            moe(0)

            def tap(n):
                h, c = divmod(n, NC)
                act.wait_ge(proj_psum, n + 1)
                act.activation(conv[:, ORDER[c], 512 * h:512 * (h + 1)], ps_proj[n % 2][:, :], ACT.Copy,
                               scale=cwt[:, ORDER[c], TAPS - 1:TAPS]).then_inc(tap_ready, 1)

            def conv_silu(n):
                h, c = divmod(n, NC)
                act.wait_ge(conv_sum, n + 1)
                part = conv[:, ORDER[c], 512 * h:512 * (h + 1)]
                act.activation(part, part, ACT.Silu, bias=cbt[:, ORDER[c]:ORDER[c] + 1]).then_inc(conv_ready, 1)

            def z_silu(t):
                act.wait_ge(z_psum, t + 1)
                act.activation(sz[:, t, :], ps_z[t % 2][:, :], ACT.Silu).then_inc(z_ready, 1)

            turned(1, 0)
            turned(1, 1)
            for n in range(NC * NH + 1):
                if n < NC * NH:
                    tap(n)
                if n == 0:
                    turned(1, 2)
                if n == 1:
                    turned(1, 3)
                if n >= 1:
                    conv_silu(n - 1)
                if 2 <= n < 2 + NT:
                    z_silu(n - 2)
                if n == DT_AT:
                    act.wait_ge(dt_in, 1)
                    act.activation(dtu[:, :, :], dta[:, :, :], ACT.Exp).then_inc(dt_exp, 1)
                    act.activation(aexp[:, :], alog[:, :], ACT.Exp).then_inc(a_exp, 1)
            act.wait_ge(cum_psum, 2)
            act.activation(ecum[:, :, :].rearrange("p t h -> p (t h)"), ps_cum, ACT.Exp).then_inc(cum_exp, 1)
            act.activation(eend[:, :, :].rearrange("p t h -> p (t h)"), ps_end, ACT.Exp).then_inc(cum_exp, 1)

            def copy_tokens(t):
                act.wait_ge(xtok_psum, t + 1)
                if t >= 1:
                    act.wait_ge(xd_ready, t)
                act.activation(xs[:, :], ps_xtok[:, :], ACT.Copy).then_inc(xs_ready, 1)
                if t % 2 == 0:
                    act.wait_ge(cb_psum, t + 1)
                    if t >= 2:
                        act.wait_ge(state_psum, t // 2)
                    act.activation(btok[:, :], ps_btok, ACT.Copy).then_inc(btok_ready, 1)

            def decays(t):
                hh = NHEADS // 2
                for i in range(2):
                    act.wait_ge(seg_psum, 2 * t + i + 1)
                    if t >= 1:
                        act.wait_ge(mm_ready, t)
                    act.activation(dec[:, i * hh:(i + 1) * hh, :].rearrange("p h l -> p (h l)"),
                                   ps_seg[i][:, :], ACT.Exp).then_inc(dec_ready, 1)

            def copy_state(t):
                act.wait_ge(state_psum, t // 2 + 1)
                if t >= 2:
                    act.wait_ge(yoff_psum, t // 2)
                act.activation(state[:, :], ps_state[:, :], ACT.Copy).then_inc(state_ready, 1)

            def squares(t):
                act.wait_ge(yg_ready, t + 1)
                if t >= 1:
                    act.wait_ge(ssq_ready, t)
                act.activation(ysq[:, :], yg[:, t % 2, :], ACT.Square, accum_out=ssq[:, t:t + 1])\
                    .then_inc(ssq_ready, 1)

            def y_high(t):
                act.wait_ge(yt_psum, t + 1)
                if t >= 1:
                    act.wait_ge(o_psum, t)
                act.activation(yth[:, :, :].rearrange("p k n -> p (k n)"), ps_yt[:, :], ACT.Copy)\
                    .then_inc(yth_ready, 1)

            for i in range(NT + 3):
                if i < NT:
                    copy_tokens(i)
                    decays(i)
                if 2 <= i < NT + 2:
                    y_high(i - 2)
                if 1 <= i < NT + 1:
                    if (i - 1) % 2 == 0:
                        copy_state(i - 1)
                    squares(i - 1)
                if i == NT:
                    turned(2, 0)
                if i == NT + 1:
                    turned(2, 1)
                    gate(1, 0)
                    turned(2, 2)

            turned(2, 3)
            gate(1, 1)
            moe(1)

        @block.tensor
        def _(pe):
            def turn(q, i):
                n = NT // 2 * q
                src = xn_late if q == 2 else xn
                pe.wait_ge(xn_ready, NT * q + 2 * i + 2)
                if i >= 3:
                    pe.wait_ge(xt_ready, n + i - 2)
                    if q == 1:
                        pe.wait_ge(xtl_ready, i - 2)
                for j in range(2):
                    for k in range(KD):
                        last = pe.transpose(ps_turn[i % 3][:, (j * KD + k) * P:(j * KD + k + 1) * P],
                                            src[:, 2 * i + j, k * P:(k + 1) * P], ident[:, :])
                last.then_inc(xt_psum, 1)

            def split3(out_ap, pairs):
                n = len(pairs)
                for a in range(3):
                    for i, (lh, ll, rh, rl) in enumerate(pairs):
                        l, r = ((lh, rh), (lh, rl), (ll, rh))[a]
                        last = pe.matmul(out_ap, l, r, start=(a == 0 and i == 0), stop=(a == 2 and i == n - 1))
                return last

            def logits(f, i):
                q = 2 * f
                for t in range(GT):
                    pe.wait_ge(xt_ready, NT // 2 * q + (GT * i + t) // 2 + 1)
                    for k in range(KD):
                        last = pe.matmul(ps_log[i][:, t, :], xT[:, GT * i + t, k, :], wgt[:, k, :],
                                         start=(k == 0), stop=(k == KD - 1))
                last.then_inc(logits_ready, 1)

            def route(f):
                pe.wait_ge(mask_ready, 2 * f + 2)
                pe.matmul(ps_rank, before16[:, :], m16[:, NT - 1:2 * NT - 1, :], start=True, stop=False)
                for d in range(1, NT):
                    last = pe.matmul(ps_rank, ones16[:, :], m16[:, NT - 1 - d:2 * NT - 1 - d, :],
                                     start=False, stop=(d == NT - 1))
                for t in range(NT):
                    last = pe.matmul(ps_cnt, ones16[:, :], m16[:, NT - 1 + t, :], start=(t == 0),
                                     stop=(t == NT - 1))
                last.then_inc(rank_ready, 1)
                for i in range(TK):
                    pe.wait_ge(tab_in, TK * f + i + 1)
                    last = pe.matmul(ps_tab.rearrange("p (a u) -> p a u", a=2), lane_oh[:, i, :], tab[:, :, i, :],
                                     start=(i == 0), stop=(i == TK - 1))
                last.then_inc(tab_ready, 1)

            def unit_turn_x(f, s):
                u = f * UNITS + s
                pe.wait_ge(xg_landed[u % XG], 16 * (u // XG + 1))
                if u >= 2:
                    pe.wait_ge(uxl_ready, u - 1)
                for k in range(KD):
                    last = pe.transpose(ps_xt[u % 2][:, k * P:(k + 1) * P], xg[:, u % XG, k * P:(k + 1) * P],
                                        ident[:, :])
                last.then_inc(uxt_psum, 1)

            def unit_up(f, s, e):
                u = f * UNITS + s
                pe.wait_ge(uxl_ready, u + 1)
                if u >= 2:
                    pe.wait_ge(g_ready, u - 1)
                b = u % 2
                pairs = []
                for k in range(KD):
                    at = e * (KD * FF) + k * FF
                    pairs.append((uxh[:, b, k, :], uxl[:, b, k, :],
                                  w1h[:, bass.ds(at, FF)], w1l[:, bass.ds(at, FF)]))
                split3(ps_h[b], pairs).then_inc(h_ready, 1)

            def unit_turn_g(f, s):
                u = f * UNITS + s
                pe.wait_ge(g_ready, u + 1)
                if u >= 2:
                    pe.wait_ge(gtl_ready, u - 1)
                for j in range(2):
                    last = pe.transpose(ps_gt[u % 2][:, j * P:(j + 1) * P], g[:, u % 2, j * FH:(j + 1) * FH],
                                        ident[:, :])
                last.then_inc(gt_psum, 1)

            def unit_down(f, s, e):
                u = f * UNITS + s
                pe.wait_ge(gtl_ready, u + 1)
                if u >= 2:
                    pe.wait_ge(y_ready, u - 1)
                b = u % 2
                pairs = []
                for j in range(2):
                    at = e * (2 * D) + j * D
                    pairs.append((gth[:, b, j, :], gtl[:, b, j, :],
                                  w2h[:, bass.ds(at, D)], w2l[:, bass.ds(at, D)]))
                split3(ps_y[b], pairs).then_inc(y_psum, 1)

            def moe(f):
                pe.wait_ge(expert_ready, f + 1)
                expert = {0: pe.value_load(ue[0:1, 0:1], min_val=0, max_val=E - 1)}
                unit_turn_x(f, 0)
                unit_turn_x(f, 1)
                if f == 0:
                    pe.wait_ge(w_hi, NWG + NW2)
                    pe.wait_ge(w_lo, NWG - NWP)
                    pe.wait_ge(w_lo_pool, NWP + NW2)
                for s in range(UNITS + 2):
                    if s < UNITS:
                        unit_up(f, s, expert[s])
                    if s + 1 < UNITS:
                        expert[s + 1] = pe.value_load(ue[0:1, s + 1:s + 2], min_val=0, max_val=E - 1)
                    if s + 2 < UNITS:
                        unit_turn_x(f, s + 2)
                    if 1 <= s <= UNITS:
                        unit_turn_g(f, s - 1)
                    if s >= 2:
                        unit_down(f, s - 2, expert.pop(s - 2))

            pe.wait_ge(consts, N_CONST)
            pe.wait_ge(ld_wg, 16)
            turn(0, 0)
            turn(0, 1)
            logits(0, 0)
            turn(0, 2)
            turn(0, 3)
            logits(0, 1)
            route(0)
            moe(0)

            def project(n):
                h, c = divmod(n, NC)
                pe.wait_ge(xtl_ready, 2 * h + 2)
                if n >= 2:
                    pe.wait_ge(conv_sum, n - 1)
                col = DI + ORDER[c] * P
                pairs = [(winh[:, k, col:col + P], winl[:, k, col:col + P],
                          xTh[:, 4 * h:4 * h + 4, k, :], xTl[:, 4 * h:4 * h + 4, k, :]) for k in range(KD)]
                split3(ps_proj[n % 2][:, :].rearrange("p (t n) -> p t n", t=4), pairs).then_inc(proj_psum, 1)

            def project_z(t):
                if t >= 2:
                    pe.wait_ge(z_ready, t - 1)
                pairs = [(xTh[:, t, k, :], xTl[:, t, k, :], winh[:, k, 0:DI], winl[:, k, 0:DI])
                         for k in range(KD)]
                split3(ps_z[t % 2][:, :], pairs).then_inc(z_psum, 1)

            pe.wait_ge(w_hi, NWG + NW2 + 2 * KD + KI)
            pe.wait_ge(w_lo, NWG - NWP + 2 * KD + KI)
            turn(1, 0)
            turn(1, 1)
            for n in range(NC * NH):
                project(n)
                if n == 0:
                    turn(1, 2)
                if n == 1:
                    turn(1, 3)
                if n == 2:
                    pe.wait_ge(xtl_ready, 4)
                    for t in range(NT):
                        pairs = [(xTh[:, t, k, :], xTl[:, t, k, :], winh[:, k, DI + CONVD:NPROJ],
                                  winl[:, k, DI + CONVD:NPROJ]) for k in range(KD)]
                        last = split3(ps_dt[:, t * NHEADS:(t + 1) * NHEADS], pairs)
                    last.then_inc(dt_psum, 1)
                if 1 <= n <= NT:
                    project_z(n - 1)
            pe.wait_ge(da_ready, 1)
            daf = da[:, :, :].rearrange("p t h -> p (t h)")
            pe.matmul(ps_cum, tri[:, :], daf, start=True, stop=True).then_inc(cum_psum, 1)
            pe.matmul(ps_end, after[:, :], daf, start=True, stop=True).then_inc(cum_psum, 1)

            def by_token(t):
                tok = slice(t * P, (t + 1) * P)
                pe.wait_ge(conv_ready, NC * (t // 4 + 1))
                if t == 0:
                    pe.wait_ge(conv_sum, NC * NH)
                else:
                    pe.wait_ge(xdt_ready, t)
                for c in range(KI):
                    last = pe.transpose(ps_xtok[:, c * P:(c + 1) * P], conv[:, c, tok], ident[:, :])
                last.then_inc(xtok_psum, 1)
                if t >= 1:
                    pe.wait_ge(cbm_ready, t)
                if t % 2 == 0:
                    pe.transpose(ps_btok, conv[:, KI, tok], ident[:, :])
                pe.matmul(ps_cb, conv[:, KI, tok], conv[:, KI + 1, tok], start=True, stop=True)\
                    .then_inc(cb_psum, 1)
                pe.wait_ge(seg_in, t + 1)
                hh = NHEADS // 2
                for i in range(2):
                    if t >= 1:
                        pe.wait_ge(dec_ready, 2 * t - 1 + i)
                    pe.matmul(ps_seg[i][:, :], after[:, :],
                              segm[:, t % 2, i * hh:(i + 1) * hh, :].rearrange("p h l -> p (h l)"),
                              start=True, stop=True).then_inc(seg_psum, 1)

            def carry(t):
                tok = slice(t * P, (t + 1) * P)
                if t % 2 == 0:
                    pe.wait_ge(xde_ready, t // 2 + 1)
                    pe.wait_ge(btok_ready, t // 2 + 1)
                    if t == 0:
                        pe.wait_ge(z_ready, NT)
                    else:
                        pe.wait_ge(yf_ready, t // 2)
                    pe.matmul(ps_state[:, :], btok[:, :], xde[:, :], start=True, stop=True)\
                        .then_inc(state_psum, 1)
                else:
                    pe.wait_ge(state_ready, t // 2 + 1)
                    pe.matmul(ps_yoff[:, :], conv[:, KI + 1, tok], state[:, :], start=True, stop=True)\
                        .then_inc(yoff_psum, 1)

            def within(t):
                pe.wait_ge(mm_ready, t + 1)
                pe.wait_ge(xdt_ready, t + 1)
                if t >= 1:
                    pe.wait_ge(yd_used, t)
                for h in range(NHEADS):
                    last = pe.matmul(ps_ydiag[:, h * HD:(h + 1) * HD], mm[:, t % 2, h, :],
                                     xdt[:, t % 2, h * HD:(h + 1) * HD], start=True, stop=True)
                last.then_inc(ydiag_psum, 1)

            def turn_y(t):
                pe.wait_ge(yg_ready, t + 1)
                if t >= 1:
                    pe.wait_ge(ytl_ready, t)
                else:
                    pe.wait_ge(z_ready, NT)
                for k in range(KI):
                    last = pe.transpose(ps_yt[:, k * P:(k + 1) * P], yg[:, t % 2, k * P:(k + 1) * P],
                                        ident[:, :])
                last.then_inc(yt_psum, 1)

            def project_out(t):
                pe.wait_ge(ytl_ready, t + 1)
                if t >= 1:
                    pe.wait_ge(o_used, t)
                else:
                    pe.wait_ge(cum_exp, 2)
                pairs = [(yth[:, k, :], ytl[:, k, :], wouth[:, k, :], woutl[:, k, :]) for k in range(KI)]
                split3(ps_o, pairs).then_inc(o_psum, 1)

            for i in range(NT + 3):
                if i < NT:
                    by_token(i)
                if i >= 3:
                    project_out(i - 3)
                if 2 <= i < NT + 2:
                    turn_y(i - 2)
                if 1 <= i < NT + 1:
                    carry(i - 1)
                    within(i - 1)
                if i == NT:
                    turn(2, 0)
                if i == NT + 1:
                    turn(2, 1)
                    logits(1, 0)
                    turn(2, 2)

            turn(2, 3)
            logits(1, 1)
            route(1)
            moe(1)

        @block.vector
        def _(dve):
            own = Chain(dve_own)

            def settle():
                dve.wait_ge(dve_own, own.n)

            def statistics(q, i):
                for t in (2 * i, 2 * i + 1):
                    own.add(dve.bn_stats(st[:, t, :], x_sb[:, t, :]))
                settle()
                for t in (2 * i, 2 * i + 1):
                    own.add(dve.bn_aggr(mv[:, t, :], st[:, t, :]))
                settle()
                dve.tensor_scalar(vare[:, 2 * i:2 * i + 2], mv[:, 2 * i:2 * i + 2, 1], EPS, None, ALU.add)\
                   .then_inc(var_ready, 1)

            def normalise(q, i):
                dst = xn_late if q == 2 else xn
                dve.wait_ge(rstd_ready, NT // 2 * q + i + 1)
                for t in (2 * i, 2 * i + 1):
                    dve.tensor_scalar(dst[:, t, :], x_sb[:, t, :], mv[:, t, 0:1], rstd[:, t:t + 1],
                                      ALU.subtract, ALU.mult).then_inc(xn_ready, 1)

            def gate(f, i):
                def over_e(a):
                    return a.unsqueeze(2).broadcast_to([P, GT, E])

                at = slice(i * GT, (i + 1) * GT)
                dve.wait_ge(logits_ready, 2 * f + i + 1)
                own.add(dve.tensor_reduce(lmax[:, at], ps_log[i], AX.X, ALU.max))
                settle()
                dve.tensor_tensor(gl[:, at, :], ps_log[i], over_e(lmax[:, at]), ALU.subtract).then_inc(gate_in, 1)
                dve.wait_ge(gate_exp, 2 * f + i + 1)
                own.add(dve.tensor_reduce(gsum[:, at], ge[:, at, :], AX.X, ALU.add))
                settle()
                own.add(dve.reciprocal(grec[:, at], gsum[:, at]))
                settle()
                own.add(dve.tensor_tensor(sc[:, at, :], ge[:, at, :], over_e(grec[:, at]), ALU.mult))
                settle()
                for t in range(i * GT, (i + 1) * GT):
                    own.add(dve.max(top[:, t, :], sc[:, t, :]))
                settle()
                for t in range(i * GT, (i + 1) * GT):
                    own.add(dve.max_index(topi[:, t, :], top[:, t, :], sc[:, t, :]))
                settle()
                for c in range(2):
                    own.add(dve.tensor_copy(idxf[:, c, at], topi[:, at, c]))
                settle()
                ohv = oh[:, :, :].rearrange("p (c t) e -> p c t e", c=2)
                for c in range(2):
                    own.add(dve.tensor_tensor(ohv[:, c, at, :], over_e(idxf[:, c, at]),
                                              lanes[:, 0:E].unsqueeze(1).broadcast_to([P, GT, E]), ALU.is_equal))
                if i == 0:
                    own.add(dve.memset(m16[:, 0:NT - 1, :], 0.0))
                settle()
                dve.tensor_tensor(m16[:, NT - 1 + i * GT:NT - 1 + (i + 1) * GT, :], ohv[:, 0, at, :],
                                  ohv[:, 1, at, :], ALU.add).then_inc(mask_ready, 1)

            def route(f):
                own.add(dve.tensor_tensor(wsum[:, :], top[:, :, 0], top[:, :, 1], ALU.add))
                settle()
                own.add(dve.tensor_scalar(wsum[:, :], wsum[:, :], TOPK_EPS, None, ALU.add))
                settle()
                own.add(dve.reciprocal(wrec[:, :], wsum[:, :]))
                settle()
                for c in range(2):
                    own.add(dve.scalar_tensor_tensor(out=cw[:, c, :], in0=top[:, :, c], scalar=0.5, in1=wrec[:, :],
                                                     op0=ALU.mult, op1=ALU.mult))
                dve.wait_ge(rank_ready, f + 1)
                own.add(dve.tensor_scalar(tr[:, :], ps_cnt, (P - 1) / 2.0, 1.0 / P, ALU.add, ALU.mult))
                settle()
                own.add(dve.tensor_scalar(tl[:, :], tr[:, :], ROUND, -ROUND, ALU.add, ALU.add))
                settle()
                own.add(dve.tensor_tensor_scan(incl[:, :], tl[:, :], zer[:, :], 0.0, ALU.add, ALU.add))
                settle()
                own.add(dve.tensor_tensor(base[:, :], incl[:, :], tl[:, :], ALU.subtract))
                settle()
                own.add(dve.scalar_tensor_tensor(out=slot[:, :, :],
                                                 in0=base[:, :].unsqueeze(1).broadcast_to([P, NT, E]),
                                                 scalar=float(P), in1=ps_rank, op0=ALU.mult, op1=ALU.add))
                settle()
                own.add(dve.tensor_tensor(osl[:, :, :].rearrange("p (c t) e -> p c (t e)", c=2),
                                          oh[:, :, :].rearrange("p (c t) e -> p c (t e)", c=2),
                                          slot[:, :, :].rearrange("p t e -> p (t e)").unsqueeze(1)
                                          .broadcast_to([P, 2, NT * E]), ALU.mult))
                settle()
                own.add(dve.tensor_reduce(slk[:, :], osl[:, :, :], AX.X, ALU.add))
                settle()
                own.add(dve.tensor_scalar(hif[:, :], slk[:, :], -(P - 1) / 2.0, 1.0 / P, ALU.add, ALU.mult))
                settle()
                own.add(dve.tensor_scalar(hi[:, :], hif[:, :], ROUND, -ROUND, ALU.add, ALU.add))
                settle()
                own.add(dve.scalar_tensor_tensor(out=lo[:, :], in0=hi[:, :], scalar=-float(P), in1=slk[:, :],
                                                 op0=ALU.mult, op1=ALU.add))
                own.add(dve.tensor_tensor(unit_oh[:, :, :], hi[:, :].unsqueeze(2).broadcast_to([P, TK, UNITS]),
                                          lanes[:, :].unsqueeze(1).broadcast_to([P, TK, UNITS]), ALU.is_equal))
                settle()
                own.add(dve.tensor_scalar(tab[:, 0, :, :], unit_oh[:, :, :], prow[:, 0:1], None, ALU.mult))
                own.add(dve.tensor_tensor(tab[:, 1, :, :], unit_oh[:, :, :],
                                          blk_id[:, :].unsqueeze(2).broadcast_to([P, TK, UNITS]), ALU.mult))
                settle()
                for i in range(TK):
                    dve.tensor_scalar(lane_oh[:, i, :], lanes16[:, :], lo[:, i:i + 1], None, ALU.is_equal)\
                       .then_inc(tab_in, 1)
                own.add(dve.tensor_tensor(ule[:, :, :], incl[:, :].unsqueeze(1).broadcast_to([P, UNITS, E]),
                                          lanes[:, :].unsqueeze(2).broadcast_to([P, UNITS, E]), ALU.is_le))
                settle()
                own.add(dve.tensor_reduce(uef[:, :], ule[:, :, :], AX.X, ALU.add))
                settle()
                dve.tensor_scalar(ue[:, :], uef[:, :], float(E - 1), None, ALU.min).then_inc(expert_ready, 1)
                dve.wait_ge(tab_ready, f + 1)
                own.add(dve.tensor_scalar(urow[:, :], ps_tab[:, UNITS:2 * UNITS], float(P), BIG, ALU.mult, ALU.add))
                settle()
                own.add(dve.tensor_tensor(srow[:, :], urow[:, :], ps_tab[:, 0:UNITS], ALU.add))
                settle()
                own.add(dve.tensor_scalar(cofs[:, :], srow[:, :], float(T), -float(T), ALU.is_ge, ALU.mult))
                own.add(dve.tensor_copy(sidx[:, :], srow[:, :]))
                settle()
                own.add(dve.tensor_tensor(urow[:, :], srow[:, :], cofs[:, :], ALU.add))
                settle()
                dve.tensor_scalar(gidx[:, :], urow[:, :], float(T - 1), None, ALU.min).then_inc(idx_ready, 1)

            def unit_x(f, s):
                u = f * UNITS + s
                dve.wait_ge(uxh_ready, u + 1)
                if u >= 2:
                    dve.wait_ge(h_ready, u - 1)
                dve.tensor_tensor(uxl[:, u % 2, :, :].rearrange("p k n -> p (k n)"), ps_xt[u % 2],
                                  uxh[:, u % 2, :, :].rearrange("p k n -> p (k n)").bitcast(F32),
                                  ALU.subtract).then_inc(uxl_ready, 1)

            def unit_gate(f, s):
                u = f * UNITS + s
                dve.wait_ge(sl_ready, u + 1)
                if u >= 2:
                    dve.wait_ge(gt_psum, u - 1)
                dve.tensor_tensor(g[:, u % 2, :], ps_h[u % 2][:, F:FF], sl[:, u % 2, :], ALU.mult)\
                   .then_inc(g_ready, 1)

            def unit_g(f, s):
                u = f * UNITS + s
                dve.wait_ge(gth_ready, u + 1)
                if u >= 2:
                    dve.wait_ge(y_psum, u - 1)
                dve.tensor_tensor(gtl[:, u % 2, :, :].rearrange("p k n -> p (k n)"), ps_gt[u % 2],
                                  gth[:, u % 2, :, :].rearrange("p k n -> p (k n)").bitcast(F32),
                                  ALU.subtract).then_inc(gtl_ready, 1)

            def unit_y(f, s):
                u = f * UNITS + s
                dve.wait_ge(y_psum, u + 1)
                if u >= YB:
                    dve.wait_ge(y_stored[u % YB], 16 * (u // YB))
                dve.tensor_copy(yo[:, u % YB, :], ps_y[u % 2]).then_inc(y_ready, 1)

            def moe(f):
                unit_x(f, 0)
                unit_x(f, 1)
                for s in range(UNITS + 2):
                    if s < UNITS:
                        unit_gate(f, s)
                    if s + 2 < UNITS:
                        unit_x(f, s + 2)
                    if 1 <= s <= UNITS:
                        unit_g(f, s - 1)
                    if s >= 2:
                        unit_y(f, s - 2)
                    if f == 0 and 5 <= s < 5 + 2 * KD:
                        k, part = divmod(s - 5, 2)
                        at = slice(part * NPROJ // 2, (part + 1) * NPROJ // 2)
                        dve.wait_ge(w_hi, NWG + NW2 + s - 4)
                        dve.tensor_tensor(winl[:, k, at], wins[:, k, at], winh[:, k, at].bitcast(F32),
                                          ALU.subtract).then_inc(w_lo, 1)
                    if f == 0 and s == 9:
                        dve.wait_ge(ld_wout, 16)
                        dve.wait_ge(ld_small, 16 * N_SMALL)
                        for k in range(KI):
                            dve.tensor_scalar(wouts[:, k, :], wouts[:, k, :], nsc[:, k:k + 1], None, ALU.mult)\
                               .then_inc(wout_scaled, 1)
                    if f == 0 and 11 <= s < 11 + KI:
                        k = s - 11
                        dve.wait_ge(w_hi, NWG + NW2 + 2 * KD + k + 1)
                        dve.tensor_tensor(woutl[:, k, :], wouts[:, k, :], wouth[:, k, :].bitcast(F32),
                                          ALU.subtract).then_inc(w_lo, 1)

            def combine(f, i):
                dve.wait_ge(y_back[i], 32 * (f + 1))
                for c in range(2):
                    for t in (2 * i, 2 * i + 1):
                        ins = dve.scalar_tensor_tensor(out=x_sb[:, t, :], in0=yin[:, c, t, :],
                                                       scalar=cw[:, c, t:t + 1], in1=x_sb[:, t, :],
                                                       op0=ALU.mult, op1=ALU.add)
                        if c == 0:
                            own.add(ins)
                        else:
                            ins.then_inc(x_done, 1)
                    if c == 0:
                        settle()

            def low_part(i):
                dve.wait_ge(w_hi, i + 1)
                at = slice(i * SEG1, (i + 1) * SEG1)
                dve.tensor_tensor(w1l[:, at], w1s[:, at], w1h[:, at].bitcast(F32), ALU.subtract).then_inc(w_lo, 1)

            dve.wait_ge(consts, N_CONST)
            for i in range(NT // 2 + 1):
                if i < NT // 2:
                    if i % (NT // 4) == 0:
                        dve.wait_ge(ld_x[i // (NT // 4)], 16)
                    statistics(0, i)
                if i >= 1:
                    normalise(0, i - 1)
            gate(0, 0)
            low_part(0)
            gate(0, 1)
            for i in range(1, NWG - NWP):
                low_part(i)
            route(0)
            moe(0)
            for i in range(NT // 2 + 1):
                if i < NT // 2:
                    combine(0, i)
                    dve.wait_ge(x_done, 2 * i + 2)
                    statistics(1, i)
                if i >= 1:
                    normalise(1, i - 1)

            def turned_low(i):
                dve.wait_ge(xt_ready, NT // 2 + i + 1)
                dve.tensor_tensor(xTl[:, 2 * i:2 * i + 2, :, :].rearrange("p t k n -> p (t k n)"),
                                  ps_turn[i % 3][:, :],
                                  xTh[:, 2 * i:2 * i + 2, :, :].rearrange("p t k n -> p (t k n)").bitcast(F32),
                                  ALU.subtract).then_inc(xtl_ready, 1)

            v = [P, NT, NHEADS]

            def flat(a):
                return a[:, :, :].rearrange("p t h -> p (t h)")

            def dt_steps():
                made = 0

                def chained(ins):
                    nonlocal made
                    own.add(ins)
                    made = own.n

                def previous():
                    dve.wait_ge(dve_own, made)

                dve.wait_ge(dt_psum, 1)
                chained(dve.tensor_tensor(dtx[:, :, :], ps_dt.rearrange("p (t h) -> p t h", t=NT),
                                          dtb[:, :].unsqueeze(1).broadcast_to(v), ALU.add))
                yield
                previous()
                dve.scalar_tensor_tensor(out=dta[:, :, :], in0=dtx[:, :, :], scalar=-1.0, in1=dtx[:, :, :],
                                         op0=ALU.mult, op1=ALU.min).then_inc(dt_in, 1)
                yield
                yield
                yield
                yield
                yield
                yield
                dve.wait_ge(dt_exp, 1)
                chained(dve.tensor_scalar(dtr[:, :, :], dtu[:, :, :], 2.0, None, ALU.add))
                yield
                previous()
                chained(dve.reciprocal(dtp[:, :, :], dtr[:, :, :]))
                yield
                previous()
                chained(dve.tensor_tensor(dts[:, :, :], dtu[:, :, :], dtp[:, :, :], ALU.mult))
                yield
                previous()
                chained(dve.tensor_tensor(dtq[:, :, :], dts[:, :, :], dts[:, :, :], ALU.mult))
                yield
                previous()
                chained(dve.tensor_scalar(dtp[:, :, :], dtq[:, :, :], ATANH[-1], None, ALU.mult))
                yield
                for coef in ATANH[-2:0:-1]:
                    previous()
                    chained(dve.scalar_tensor_tensor(out=dtp[:, :, :], in0=dtp[:, :, :], scalar=coef,
                                                     in1=dtq[:, :, :], op0=ALU.add, op1=ALU.mult))
                    yield
                previous()
                chained(dve.scalar_tensor_tensor(out=dtr[:, :, :], in0=dtp[:, :, :], scalar=1.0, in1=dts[:, :, :],
                                                 op0=ALU.add, op1=ALU.mult))
                chained(dve.tensor_scalar(dta[:, :, :], dtx[:, :, :], 0.0, None, ALU.max))
                yield
                previous()
                chained(dve.scalar_tensor_tensor(out=dtv[:, :, :], in0=dtr[:, :, :], scalar=2.0,
                                                 in1=dta[:, :, :], op0=ALU.mult, op1=ALU.add))
                yield
                previous()
                dve.wait_ge(a_exp, 1)
                dve.scalar_tensor_tensor(out=da[:, :, :], in0=dtv[:, :, :], scalar=-1.0,
                                         in1=aexp[:, :].unsqueeze(1).broadcast_to(v), op0=ALU.mult,
                                         op1=ALU.mult).then_inc(da_ready, 1)

            spans = 512 // SEQ
            turned_low(0)
            turned_low(1)
            steps = dt_steps()
            for n in range(NC * NH):
                h, c = divmod(n, NC)
                c = ORDER[c]
                dve.wait_ge(tap_ready, n + 1)
                src = ps_proj[n % 2][:, :].rearrange("p (b s) -> p b s", b=spans)
                dst = conv[:, c, 512 * h:512 * (h + 1)].rearrange("p (b s) -> p b s", b=spans)
                for back in range(1, TAPS):
                    ins = dve.scalar_tensor_tensor(out=dst[:, :, back:SEQ], in0=src[:, :, 0:SEQ - back],
                                                   scalar=cwt[:, c, TAPS - 1 - back:TAPS - back],
                                                   in1=dst[:, :, back:SEQ], op0=ALU.mult, op1=ALU.add)
                    if back < TAPS - 1:
                        own.add(ins)
                    else:
                        ins.then_inc(conv_sum, 1)
                    if n >= 3:
                        next(steps, None)
                    if back < TAPS - 1:
                        settle()
                if n == 0:
                    turned_low(2)
                if n == 1:
                    turned_low(3)
            for _ in steps:
                pass

            def heads(a):
                return a.rearrange("p (h d) -> p h d", h=NHEADS)

            def scale_dt(t):
                dve.wait_ge(xs_ready, t + 1)
                if t >= 2:
                    dve.wait_ge(ydiag_psum, t - 1)
                    if t % 2 == 0:
                        dve.wait_ge(xde_ready, t // 2)
                dve.tensor_tensor(heads(xdt[:, t % 2, :]), heads(ps_xtok[:, :]),
                                  dtv[:, t, :].unsqueeze(2).broadcast_to([P, NHEADS, HD]), ALU.mult)\
                   .then_inc(xdt_ready, 1)

            def mix_matrix(t):
                dve.wait_ge(cb_psum, t + 1)
                dve.wait_ge(btok_ready, t // 2 + 1)
                if t >= 2:
                    dve.wait_ge(mm_ready, t - 1)
                dve.tensor_tensor(cbm[:, t % 2, :], ps_cb, tri[:, :], ALU.mult).then_inc(cbm_ready, 1)
                dve.wait_ge(cbm_ready, t + 1)
                dve.wait_ge(dec_ready, 2 * t + 2)
                dve.tensor_tensor(mm[:, t % 2, :, :], dec[:, :, :],
                                  cbm[:, t % 2, :].unsqueeze(1).broadcast_to([P, NHEADS, P]), ALU.mult)\
                   .then_inc(mm_ready, 1)

            def gated(t):
                if t % 2 == 1:
                    dve.wait_ge(yoff_psum, t // 2 + 1)
                    if t >= 3:
                        dve.wait_ge(yg_ready, t)
                    dve.tensor_tensor(heads(yf[:, :]), heads(ps_yoff[:, :]),
                                      ecum[:, t, :].unsqueeze(2).broadcast_to([P, NHEADS, HD]), ALU.mult)\
                       .then_inc(yf_ready, 1)
                dve.wait_ge(ydiag_psum, t + 1)
                dve.wait_ge(xd_ready, t + 1)
                if t >= 1:
                    dve.wait_ge(yg_ready, t)
                dve.tensor_tensor(y1[:, :], ps_ydiag[:, :], xd[:, :], ALU.add).then_inc(yd_used, 1)
                dve.wait_ge(yd_used, t + 1)
                if t % 2 == 1:
                    dve.wait_ge(yf_ready, t // 2 + 1)
                    own.add(dve.tensor_tensor(y1[:, :], y1[:, :], yf[:, :], ALU.add))
                    settle()
                if t >= 2:
                    dve.wait_ge(yt_psum, t - 1)
                    dve.wait_ge(ssq_ready, t - 1)
                dve.tensor_tensor(yg[:, t % 2, :], y1[:, :], sz[:, t, :], ALU.mult).then_inc(yg_ready, 1)

            def y_variance(t):
                dve.wait_ge(ssq_ready, t + 1)
                dve.tensor_scalar(vy[:, t:t + 1], ssq[:, t:t + 1], 1.0 / DI, EPS, ALU.mult, ALU.add)\
                   .then_inc(vy_ready, 1)

            def y_low(t):
                dve.wait_ge(yth_ready, t + 1)
                if t >= 1:
                    dve.wait_ge(o_psum, t)
                dve.tensor_tensor(ytl[:, :, :].rearrange("p k n -> p (k n)"), ps_yt[:, :],
                                  yth[:, :, :].rearrange("p k n -> p (k n)").bitcast(F32), ALU.subtract)\
                   .then_inc(ytl_ready, 1)

            def add_mixed(t):
                dve.wait_ge(o_psum, t + 1)
                dve.wait_ge(ry_ready, t + 1)
                dve.scalar_tensor_tensor(out=x_sb[:, t, :], in0=ps_o, scalar=ry[:, t:t + 1],
                                         in1=x_sb[:, t, :], op0=ALU.mult, op1=ALU.add).then_inc(o_used, 1)

            for i in range(NT + 3):
                if 2 <= i < NT + 2:
                    y_variance(i - 2)
                if i < NT:
                    scale_dt(i)
                    mix_matrix(i)
                if i >= 3:
                    add_mixed(i - 3)
                if 2 <= i < NT + 2:
                    y_low(i - 2)
                if 1 <= i < NT + 1:
                    gated(i - 1)
                if i >= 4 and i % 2 == 0:
                    dve.wait_ge(o_used, i - 2)
                    statistics(2, i // 2 - 2)
                if i >= 5 and i % 2 == 1:
                    normalise(2, (i - 5) // 2)
                if i == NT + 1:
                    gate(1, 0)
            normalise(2, NT // 2 - 1)

            gate(1, 1)
            route(1)
            moe(1)
            for i in range(NT // 2):
                combine(1, i)

def kernel(**inputs):
    import concourse.bacc as bacc
    from concourse.bass_utils import run_bass_kernel_spmd

    get = {k: np.asarray(v) for k, v in inputs.items()}
    u = get["L0_attn_u"]
    conv_w = get["L0_attn_conv_w"]
    row = lambda a: np.ascontiguousarray(a.reshape(1, -1))
    cols = lambda a: np.ascontiguousarray(a.reshape(-1, P).T)
    arrays = {
        "u": np.ascontiguousarray(u.reshape(-1, u.shape[-1])),
        "w_in": np.ascontiguousarray(get["L0_attn_W_in"]),
        "conv_w": np.ascontiguousarray(conv_w.T[None]),
        "conv_b": cols(get["L0_attn_conv_b"]),
        "dt_bias": row(get["L0_attn_dt_bias"]),
        "a_log": row(get["L0_attn_A_log"]),
        "d_skip": row(get["L0_attn_D"]),
        "norm_scale": cols(get["L0_attn_norm_scale"]),
        "w_out": np.ascontiguousarray(get["L0_attn_W_out"]),
        "wg_t": np.ascontiguousarray(get["L0_ffn_wg"].T),
        "w1": np.ascontiguousarray(get["L0_ffn_w1"]),
        "w2": np.ascontiguousarray(get["L0_ffn_w2"]),
    }
    nc = bacc.Bacc("TRN2", target_bir_lowering=False, num_devices=1)
    args = [nc.dram_tensor(n, a.shape, mybir.dt.from_np(a.dtype), kind="ExternalInput").ap()
            for n, a in arrays.items()]
    out = nc.dram_tensor("out", arrays["u"].shape, F32, kind="ExternalOutput").ap()
    build(nc, *args, out)
    r = run_bass_kernel_spmd(nc, [arrays], core_ids=[0])
    return r.results[0]["out"].reshape(u.shape)
```

```python
from contextlib import ExitStack

import numpy as np
import concourse.bass as bass
from concourse import mybir

F32 = mybir.dt.float32
F32R = mybir.dt.float32r
BF16 = mybir.dt.bfloat16
I32 = mybir.dt.int32
U32 = mybir.dt.uint32
ALU = mybir.AluOpType
ACT = mybir.ActivationFunctionType
AX = mybir.AxisListType

P = 128
XG = 6
LEAD = 3
LANE_DVE = 13
YB = 3
BIG = 4096.0
HALF = (P - 1) / (2.0 * P)
ROUND = 12582912.0
EPS = 1e-5
TOPK_EPS = 1e-20
ATANH = [1.0 / (2 * i + 1) for i in range(8)]


class Chain:

    def __init__(self, sem):
        self.sem, self.n = sem, 0

    def add(self, ins):
        ins.then_inc(self.sem, 1)
        self.n += 1


def build(nc, u_in, w_in, conv_w, conv_b, dt_bias, a_log, d_skip, norm_scale, w_out, wg_t, w1, w2, out):
    T, D = u_in.shape
    NT = T // P
    KD = D // P
    E, _, FF = w1.shape
    F = FF // 2
    FH = F // 2
    DI = w_out.shape[0]
    KI = DI // P
    NHEADS = a_log.shape[1]
    HD = DI // NHEADS
    CONVD = conv_w.shape[1]
    NC = CONVD // P
    TAPS = conv_w.shape[2]
    NPROJ = w_in.shape[1]
    SEQ = 2 * P
    NH = T // 512
    UNITS = 2 * NT + E - 1
    TK = 2 * NT
    EG = 2
    NWG = E // EG
    NW2 = 2
    NWP = NWG - 1
    SEG1, SEG2 = EG * KD * FF, E // NW2 * 2 * D
    ORDER = [KI, KI + 1] + list(range(KI))
    WARM = 6
    DVE_TAPS = (3, NC * NH - 1)
    DT_AT = 4
    Z_AT = [1, 2, 4, 5, 7, 9, 11, 11]

    def tiles_of(q, i):
        if q == 2 and i >= NT // 2 - 1:
            return (NT // 2 - 1 + i,)
        return (2 * i, 2 * i + 1)

    def split_taps(n):
        return len([m for m in range(n) if m not in DVE_TAPS])

    xn_dram = nc.dram_tensor("xn_rows", (T, D), F32, kind="Internal").ap()
    y_dram = nc.dram_tensor("y_rows", (2 * T, D), F32, kind="Internal").ap()

    ctx = ExitStack()
    with ctx:
        def sb(name, shape, dt=F32):
            return ctx.enter_context(nc.sbuf_tensor(name, shape, dt))

        def sem(name):
            return ctx.enter_context(nc.semaphore(name))

        W1F, W2F = E * KD * FF, E * 2 * D
        x_sb = sb("x_sb", [P, NT, D])
        w1h = sb("w1h", [P, W1F], F32R)
        w2h = sb("w2h", [FH, W2F], F32R)
        with nc.sbuf_tensor("segl", [P, 2, NHEADS, P], F32R) as segl:
            pass
        winh = sb("winh", [P, KD, NPROJ], F32R)
        wouth = sb("wouth", [P, KI, D], F32R)

        def landing(name, shape):
            with nc.sbuf_tensor(name + "s", shape, F32) as raw:
                pass
            return raw, sb(name + "l", shape, F32R)

        w1s, w1l = landing("w1", [P, W1F])
        w2s, w2l = landing("w2", [FH, W2F])
        with nc.sbuf_tensor("xn_late", [P, NT, D], F32) as xn_late:
            pass
        wins, winl = landing("win", [P, KD, NPROJ])
        wouts, woutl = landing("wout", [P, KI, D])

        ident = sb("ident", [P, P])
        tri = sb("tri", [P, P])
        after = sb("after", [P, P], F32R)
        before16 = sb("before16", [P, P], BF16)
        ones16 = sb("ones16", [P, P], BF16)
        inv16 = sb("inv16", [P, P], BF16)
        half16 = sb("half16", [P, E], BF16)
        lanes = sb("lanes", [P, UNITS])
        lanes16 = sb("lanes16", [P, P], BF16)
        prow = sb("prow", [P, 1])
        tile_id = sb("tile_id", [P, TK])
        mhalf = sb("mhalf", [P, NT])
        table_call = sb("table_call", [P, 1])

        st = sb("st", [P, NT, 6])
        mv = sb("mv", [P, NT, 2])
        vare = sb("vare", [P, NT])
        rstd = sb("rstd", [P, NT])
        shift = sb("shift", [P, NT])
        wgt = sb("wgt", [P, KD, E])
        wsum = sb("wsum", [P, NT])
        wrec = sb("wrec", [P, NT])
        cw = sb("cw", [P, 2, NT])
        tl = sb("tl", [P, E])
        incl = sb("incl", [P, E])
        base = sb("base", [P, E])
        zer = sb("zer", [P, E])
        slk = sb("slk", [P, TK])
        hi = sb("hi", [P, TK])
        lo = sb("lo", [P, TK])
        srow = sb("srow", [P, UNITS])
        gidx = sb("gidx", [P, UNITS], I32)
        sidx = sb("sidx", [P, UNITS], I32)
        uef = sb("uef", [P, UNITS])
        ue = sb("ue", [P, UNITS], I32)
        cwt = sb("cwt", [P, NC, TAPS])
        cbt = sb("cbt", [P, NC])
        dtb = sb("dtb", [P, NHEADS])
        alog = sb("alog", [P, NHEADS])
        dsk = sb("dsk", [P, NHEADS])
        nsc = sb("nsc", [P, KI])
        ssq = sb("ssq", [P, NT])
        vy = sb("vy", [P, NT])
        ry = sb("ry", [P, NT])

        with nc.sbuf_tensor("xn", [P, NT, D], F32) as xn:
            pass
        segh = sb("segh", [P, 2, NHEADS, P], F32R)

        with ExitStack() as ffn:
            def fb(name, shape, dt=F32):
                return ffn.enter_context(nc.sbuf_tensor(name, shape, dt))

            xT = fb("xT", [P, NT, KD, P])
            lane_oh = fb("lane_oh", [P, TK, P], BF16)
            yin = fb("yin", [P, 2, NT, D])
            unit_oh = fb("unit_oh", [P, TK, UNITS])
            tab = fb("tab", [P, 3, TK, UNITS], BF16)
            lmax = fb("lmax", [P, NT])
            gl = fb("gl", [P, NT, E])
            ge = fb("ge", [P, NT, E])
            gsum = fb("gsum", [P, NT])
            grec = fb("grec", [P, NT])
            sc = fb("sc", [P, 2, NT])
            top = fb("top", [P, NT, 8])
            topi = fb("topi", [P, NT, 8], U32)
            oh = fb("oh", [P, TK, E])
            m16 = fb("m16", [P, 2 * NT - 1, E], BF16)
            slot = fb("slot", [P, NT, E])
            osl = fb("osl", [P, TK, E])
            ule = fb("ule", [P, UNITS, E])
            xg = fb("xg", [P, XG, D])
            uxh = fb("uxh", [P, 2, KD, P], F32R)
            uxl = fb("uxl", [P, 2, KD, P], F32R)
            sl = fb("sl", [P, 2, F])
            g = fb("g", [P, 2, F])
            gth = fb("gth", [FH, 2, 2, P], F32R)
            gtl = fb("gtl", [FH, 2, 2, P], F32R)
            yo = fb("yo", [P, YB, D])

        conv = sb("conv", [P, NC, T])
        sz = sb("sz", [P, NT, DI])
        with nc.sbuf_tensor("xTh", [P, NT, KD, P], F32R) as xTh, nc.sbuf_tensor("xTl", [P, NT, KD, P], F32R) as xTl:
            pass
        xdt = sb("xdt", [P, 2, DI])
        yg = sb("yg", [P, 2, DI])
        mm = sb("mm", [P, 2, NHEADS, P])
        aexp = sb("aexp", [P, NHEADS])
        dtx = sb("dtx", [P, NT, NHEADS])
        dta = sb("dta", [P, NT, NHEADS])
        dtu = sb("dtu", [P, NT, NHEADS])
        dtr = sb("dtr", [P, NT, NHEADS])
        dts = sb("dts", [P, NT, NHEADS])
        dtq = sb("dtq", [P, NT, NHEADS])
        dtp = sb("dtp", [P, NT, NHEADS])
        dtv = sb("dtv", [P, NT, NHEADS])
        da = sb("da", [P, NT, NHEADS])
        dah = sb("dah", [P, NT, NHEADS], F32R)
        dal = sb("dal", [P, NT, NHEADS])
        ecum = sb("ecum", [P, NT, NHEADS])
        eend = sb("eend", [P, NT, NHEADS])
        dec = sb("dec", [P, NHEADS, P])
        cbm = sb("cbm", [P, 2, P])
        with nc.sbuf_tensor("dt_rows", [NHEADS, T], F32) as dt_rows:
            pass
        xs = sb("xs", [P, DI])
        xd = sb("xd", [P, DI])
        xde = sb("xde", [P, DI])
        btok = sb("btok", [P, P])
        state = sb("state", [P, DI])
        with nc.sbuf_tensor("tap2", [P, 2, 512], F32) as tap2:
            pass
        y1 = sb("y1", [P, DI])
        yf = sb("yf", [P, DI])
        ysq = sb("ysq", [P, DI])
        yth = sb("yth", [P, KI, P], F32R)
        ytl = sb("ytl", [P, KI, P], F32R)

        bank = [ctx.enter_context(nc.psum_tensor(f"bank{i}", [P, 512], F32)) for i in range(8)]
        ps_turn = [bank[0], bank[1], bank[2]]
        GT = NT // 2
        ps_log = [bank[3 + i][:, 0:GT * E].rearrange("p (t e) -> p t e", t=GT) for i in range(2)]
        ps_rank = bank[6][:, 0:NT * E].rearrange("p (t e) -> p t e", t=NT)
        ps_cnt = bank[7][:, 0:E]
        ps_tab = bank[5][:, 0:3 * UNITS]
        ps_xt = [bank[0][:, 0:D], bank[1][:, 0:D]]
        ps_h = [bank[2][:, 0:FF], bank[3][:, 0:FF]]
        ps_y = [bank[4][:, 0:D], bank[5][:, 0:D]]
        ps_gt = [bank[6][0:FH, 0:2 * P], bank[7][0:FH, 0:2 * P]]
        ps_proj = [bank[1], bank[3], bank[4]]
        ps_z = [bank[5], bank[6]]
        TH = NT * NHEADS
        ps_dtrow = [bank[7][0:NHEADS, :], bank[2][0:NHEADS, :]]
        ps_dt, ps_cum, ps_end = (bank[7][:, i * TH:(i + 1) * TH] for i in range(3))
        ps_xtok = bank[0]
        ps_btok, ps_cb = bank[1][:, 0:P], bank[1][:, P:2 * P]
        ps_seg = [bank[2], bank[3]]
        ps_ydiag = bank[4]
        ps_yt = bank[5]
        ps_state = ps_yoff = bank[6]
        ps_o = bank[7][:, 0:D]

        ld_x = [sem(f"ld_x{i}") for i in range(2)]
        ld_wg = sem("ld_wg")
        ld_small = sem("ld_small")
        ld_w1 = [sem(f"ld_w1_{i}") for i in range(NWG)]
        ld_w2 = [sem(f"ld_w2_{i}") for i in range(NW2)]
        ld_win = sem("ld_win")
        ld_wout = sem("ld_wout")
        consts = sem("consts")
        w_hi = sem("w_hi")
        w_lo = sem("w_lo")
        w_lo_pool = sem("w_lo_pool")
        wout_scaled = sem("wout_scaled")
        dve_own = sem("dve_own")
        act_own = sem("act_own")
        pool_own = sem("pool_own")
        var_ready = sem("var_ready")
        rstd_ready = sem("rstd_ready")
        xn_ready = sem("xn_ready")
        xn_stored = sem("xn_stored")
        xt_psum = sem("xt_psum")
        xt_ready = sem("xt_ready")
        xtl_ready = sem("xtl_ready")
        logits_ready = sem("logits_ready")
        gate_in = sem("gate_in")
        gate_exp = sem("gate_exp")
        mask_ready = sem("mask_ready")
        rank_ready = sem("rank_ready")
        units_ready = sem("units_ready")
        lo_ready = sem("lo_ready")
        tab_rows = sem("tab_rows")
        tab_tiles = sem("tab_tiles")
        lane_in = sem("lane_in")
        lane_in_pool = sem("lane_in_pool")
        tab_ready = sem("tab_ready")
        idx_ready = sem("idx_ready")
        rows_ready = sem("rows_ready")
        expert_ready = sem("expert_ready")
        xg_landed = [sem(f"xg_landed{i}") for i in range(XG)]
        uxt_psum = sem("uxt_psum")
        uxh_ready = sem("uxh_ready")
        uxl_ready = sem("uxl_ready")
        h_ready = sem("h_ready")
        sl_ready = sem("sl_ready")
        g_ready = sem("g_ready")
        gt_psum = sem("gt_psum")
        gth_ready = sem("gth_ready")
        gtl_ready = sem("gtl_ready")
        y_psum = sem("y_psum")
        y_ready = sem("y_ready")
        y_stored = [sem(f"y_stored{i}") for i in range(YB)]
        y_back = [sem(f"y_back{i}") for i in range(4)]
        cw_ready = sem("cw_ready")
        y_scaled = sem("y_scaled")
        x_part = sem("x_part")
        x_done = sem("x_done")
        shift_ready = sem("shift_ready")
        out_stored = sem("out_stored")
        proj_psum = sem("proj_psum")
        tap_ready = sem("tap_ready")
        conv_sum = sem("conv_sum")
        conv_full = sem("conv_full")
        conv_ready = sem("conv_ready")
        z_psum = sem("z_psum")
        z_ready = sem("z_ready")
        dtrow_psum = sem("dtrow_psum")
        dtrow_ready = sem("dtrow_ready")
        dt_psum = sem("dt_psum")
        dt_in = sem("dt_in")
        dt_exp = sem("dt_exp")
        a_exp = sem("a_exp")
        da_ready = sem("da_ready")
        cum_psum = sem("cum_psum")
        cum_exp = sem("cum_exp")
        xtok_psum = sem("xtok_psum")
        cb_psum = sem("cb_psum")
        da_split = sem("da_split")
        seg_in = sem("seg_in")
        seg_low_first = sem("seg_low_first")
        seg_low_in = sem("seg_low_in")
        seg_psum = sem("seg_psum")
        xs_ready = sem("xs_ready")
        btok_ready = sem("btok_ready")
        dec_ready = sem("dec_ready")
        cbm_ready = sem("cbm_ready")
        mm_ready = sem("mm_ready")
        xdt_ready = sem("xdt_ready")
        xd_ready = sem("xd_ready")
        xde_ready = sem("xde_ready")
        ydiag_psum = sem("ydiag_psum")
        state_psum = sem("state_psum")
        state_ready = sem("state_ready")
        yoff_psum = sem("yoff_psum")
        yd_used = sem("yd_used")
        yf_ready = sem("yf_ready")
        yg_ready = sem("yg_ready")
        ssq_ready = sem("ssq_ready")
        vy_ready = sem("vy_ready")
        ry_ready = sem("ry_ready")
        yt_psum = sem("yt_psum")
        yth_ready = sem("yth_ready")
        ytl_ready = sem("ytl_ready")
        o_psum = sem("o_psum")
        o_used = sem("o_used")

        N_CONST = 13
        N_SMALL = 6

        block = ctx.enter_context(nc.Block())

        @block.sync
        def _(sp):
            xv = u_in.rearrange("(t p) d -> p t d", p=P)
            half = NT // 2
            for i in range(2):
                sp.dma_start(x_sb[:, i * half:(i + 1) * half, :], xv[:, i * half:(i + 1) * half, :])\
                  .then_inc(ld_x[i], 16)
            sp.dma_start(wgt[:, :, :], wg_t.rearrange("(k p) e -> p k e", p=P)).then_inc(ld_wg, 16)
            w1v = w1.rearrange("e (k p) f -> p e k f", p=P)
            w1sv = w1s[:, :].rearrange("p (e k f) -> p e k f", e=E, k=KD)
            for e in range(E):
                sp.dma_start(w1sv[:, e, :, :], w1v[:, e, :, :]).then_inc(ld_w1[e // EG], 16)
            w2v = w2.rearrange("e (j p) d -> p e j d", p=FH)
            w2sv = w2s[:, :].rearrange("p (e j d) -> p e j d", e=E, j=2)
            for e in range(E):
                sp.dma_start(w2sv[:, e, :, :], w2v[:, e, :, :]).then_inc(ld_w2[e // (E // NW2)], 16)

            def store_rows(q, src):
                for i in range(NT // 2):
                    sp.wait_ge(xn_ready, NT * q + 2 * i + 2)
                    dst = xn_dram[2 * i * P:2 * (i + 1) * P, :].rearrange("(t p) d -> p t d", p=P)
                    sp.dma_start(dst, src[:, 2 * i:2 * i + 2, :]).then_inc(xn_stored, 16)

            def fetch_rows(f):
                for i in range(YB):
                    uses = len([u for u in range(UNITS * (f + 1)) if u % YB == i])
                    sp.wait_ge(y_stored[i], 16 * uses)
                yv = y_dram.rearrange("(c t p) d -> p c t d", c=2, p=P)
                for i in range(NT // 2):
                    for c in range(2):
                        sp.dma_start(yin[:, c, 2 * i:2 * i + 2, :], yv[:, c, 2 * i:2 * i + 2, :])\
                          .then_inc(y_back[i], 16)

            store_rows(0, xn)
            sp.dma_start(cwt[:, :, :], conv_w.rearrange("a n k -> (a n) k").rearrange("(c p) k -> p c k", p=P))\
              .then_inc(ld_small, 16)
            sp.dma_start(cbt[:, :], conv_b).then_inc(ld_small, 16)
            sp.dma_start(nsc[:, :], norm_scale).then_inc(ld_small, 16)
            for dst, src in ((dtb, dt_bias), (alog, a_log), (dsk, d_skip)):
                sp.dma_start(dst[:, :], src.broadcast_to([P, NHEADS])).then_inc(ld_small, 16)
            sp.dma_start(wins[:, :, :], w_in.rearrange("(k p) n -> p k n", p=P)).then_inc(ld_win, 16)
            sp.dma_start(wouts[:, :, :], w_out.rearrange("(k p) n -> p k n", p=P)).then_inc(ld_wout, 16)
            fetch_rows(0)
            store_rows(2, xn_late)
            fetch_rows(1)
            for t in range(NT):
                sp.wait_ge(x_done, NT + t + 1)
                sp.dma_start(out[t * P:(t + 1) * P, :], x_sb[:, t, :]).then_inc(out_stored, 16)
            sp.wait_ge(out_stored, 16 * NT)

        @block.gpsimd
        def _(pool):
            own = Chain(pool_own)

            def select(dst, fill, compare, pattern, base, mult):
                pool.affine_select(out=dst, in_=dst, compare_op=compare, fill=fill, base=base,
                                   pattern=pattern, channel_multiplier=mult).then_inc(consts, 1)

            pool.memset(mhalf[:, :], -0.5).then_inc(consts, 1)
            own.add(pool.memset(ident[:, :], 0.0))
            own.add(pool.memset(tri[:, :], 1.0))
            after_raw = yin[:, 0, 0, 0:P]
            own.add(pool.memset(after_raw, 1.0))
            lane_raw = yin[:, 0, 0, P:2 * P]
            own.add(pool.memset(before16[:, :], 1.0))
            pool.memset(ones16[:, :], 1.0).then_inc(consts, 1)
            pool.memset(inv16[:, :], 1.0 / P).then_inc(consts, 1)
            pool.memset(half16[:, :], HALF / P).then_inc(consts, 1)
            pool.memset(zer[:, :], 0.0).then_inc(consts, 1)
            pool.wait_ge(pool_own, own.n)
            select(ident[:, :], 1.0, ALU.not_equal, [[-1, P]], 0, 1)
            select(tri[:, :], 0.0, ALU.is_ge, [[1, P]], 0, -1)
            own.add(pool.affine_select(out=after_raw, in_=after_raw, compare_op=ALU.is_gt, fill=0.0, base=0,
                                       pattern=[[-1, P]], channel_multiplier=1))
            pool.wait_ge(pool_own, own.n)
            pool.tensor_copy(after[:, :], after_raw).then_inc(consts, 1)
            select(before16[:, :], 0.0, ALU.is_gt, [[1, P]], 0, -1)
            iota = dict(allow_small_or_imprecise_dtypes=True)
            pool.iota(lanes[:, :], pattern=[[1, UNITS]], base=0, channel_multiplier=0, **iota).then_inc(consts, 1)
            own.add(pool.iota(lane_raw, pattern=[[1, P]], base=0, channel_multiplier=0, **iota))
            pool.wait_ge(pool_own, own.n)
            pool.tensor_scalar(lanes16[:, :], lane_raw, 1.0 / P, -HALF, ALU.mult, ALU.add).then_inc(consts, 1)
            pool.iota(prow[:, :], pattern=[[0, 1]], base=0, channel_multiplier=1, **iota).then_inc(consts, 1)
            pool.iota(tile_id[:, :], pattern=[[0, 2], [1, NT]], base=0, channel_multiplier=0, **iota)\
                .then_inc(consts, 1)

            def deviation(q, i):
                n = NT // 2 * q + i
                pool.wait_ge(var_ready, n + 1)
                ts = tiles_of(q, i)
                at = slice(ts[0], ts[-1] + 1)
                pool.tensor_tensor(rstd[:, at], vare[:, at], mhalf[:, 0:len(ts)], ALU.pow)\
                    .then_inc(rstd_ready, 1)

            def gather(f, s):
                u = f * UNITS + s
                if s == 0:
                    pool.wait_ge(idx_ready, f + 1)
                    pool.wait_ge(xn_stored, 16 * (NT // 2) * (f + 1))
                if u >= XG:
                    pool.wait_ge(uxt_psum, u - XG + 1)
                pool.indirect_dma_start(xg[:, u % XG, :], None, xn_dram,
                                        bass.IndirectOffsetOnAxis(ap=gidx[:, s:s + 1], axis=0))\
                    .then_inc(xg_landed[u % XG], 16)

            def scatter(f, s):
                u = f * UNITS + s
                if s == 0:
                    pool.wait_ge(rows_ready, f + 1)
                pool.wait_ge(y_ready, u + 1)
                pool.indirect_dma_start(y_dram, bass.IndirectOffsetOnAxis(ap=sidx[:, s:s + 1], axis=0),
                                        yo[:, u % YB, :], None, bounds_check=2 * T - 1, oob_is_err=False)\
                    .then_inc(y_stored[u % YB], 16)

            def lanes_of_slots(f):
                pool.wait_ge(lo_ready, f + 1)
                for i in range(LANE_DVE, TK):
                    pool.tensor_scalar(lane_oh[:, i, :], lanes16[:, :], lo[:, i:i + 1], None, ALU.is_equal)\
                        .then_inc(lane_in_pool, 1)

            def moe(f):
                for s in range(XG + LEAD):
                    gather(f, s)
                for s in range(UNITS):
                    scatter(f, s)
                    if s + XG + LEAD < UNITS:
                        gather(f, s + XG + LEAD)

            def low_part(l, s_, h, at, n):
                pool.wait_ge(w_hi, n)
                pool.tensor_tensor(l[:, at], s_[:, at], h[:, at].bitcast(F32), ALU.subtract)\
                    .then_inc(w_lo_pool, 1)

            def seg_input(t):
                if t == 0:
                    pool.wait_ge(da_split, 1)
                    pool.wait_ge(xt_psum, NT)
                if t >= 2:
                    pool.wait_ge(seg_psum, 2 * (t - 1))
                pool.tensor_tensor(segh[:, t % 2, :, :], tri[:, :].unsqueeze(1).broadcast_to([P, NHEADS, P]),
                                   dah[:, t, :].bitcast(F32).unsqueeze(2).broadcast_to([P, NHEADS, P]), ALU.mult)\
                    .then_inc(seg_in, 1)

            def skip_input(t):
                pool.wait_ge(xs_ready, t + 1)
                if t >= 1:
                    pool.wait_ge(yd_used, t)
                pool.tensor_tensor(xd[:, :].rearrange("p (h d) -> p h d", h=NHEADS),
                                   xs[:, :].rearrange("p (h d) -> p h d", h=NHEADS),
                                   dsk[:, :].unsqueeze(2).broadcast_to([P, NHEADS, HD]), ALU.mult)\
                    .then_inc(xd_ready, 1)

            def state_input(t):
                pool.wait_ge(xdt_ready, t + 1)
                if t == 0:
                    pool.wait_ge(cum_exp, 2)
                if t >= 2:
                    pool.wait_ge(state_psum, t // 2)
                pool.tensor_tensor(xde[:, :].rearrange("p (h d) -> p h d", h=NHEADS),
                                   xdt[:, t % 2, :].rearrange("p (h d) -> p h d", h=NHEADS),
                                   eend[:, t, :].unsqueeze(2).broadcast_to([P, NHEADS, HD]), ALU.mult)\
                    .then_inc(xde_ready, 1)

            def add_tap(n):
                h, c = divmod(n, NC)
                pool.wait_ge(conv_sum, n + 1)
                dst = conv[:, ORDER[c], 512 * h:512 * (h + 1)].rearrange("p (b s) -> p b s", s=SEQ)[:, :, 1:SEQ]
                src = tap2[:, split_taps(n) % 2, :].rearrange("p (b s) -> p b s", s=SEQ)[:, :, 0:SEQ - 1]
                pool.tensor_tensor(dst, dst, src, ALU.add).then_inc(conv_full, 1)

            def add_first(f, t):
                pool.wait_ge(y_scaled, (NT - 2) * f + t - 1)
                pool.tensor_tensor(x_sb[:, t, :], x_sb[:, t, :], yin[:, 0, t, :], ALU.add).then_inc(x_part, 1)

            def y_deviation(t):
                pool.wait_ge(vy_ready, t + 1)
                pool.tensor_tensor(ry[:, t:t + 1], vy[:, t:t + 1], mhalf[:, 0:1], ALU.pow)\
                    .then_inc(ry_ready, 1)

            pool.wait_ge(consts, N_CONST)
            for i in range(NT // 2):
                deviation(0, i)
            for i in range(NWP):
                low_part(w1l, w1s, w1h, slice(i * SEG1, (i + 1) * SEG1), i + 1)
            lanes_of_slots(0)
            moe(0)
            for i in range(NT // 2 + 1):
                if 1 <= i < NT // 2:
                    add_first(0, 2 * i)
                    add_first(0, 2 * i + 1)
                if i >= 1:
                    deviation(1, i - 1)
            for n in range(NC * NH):
                if n not in DVE_TAPS:
                    add_tap(n)
                if n in (NC * NH - 4, NC * NH - 1):
                    seg_input(0 if n < NC * NH - 1 else 1)
            for i in range(NT + 3):
                if i < NT:
                    if i % 2 == 0:
                        state_input(i)
                    if i == 0:
                        skip_input(i)
                    if i + 2 < NT:
                        seg_input(i + 2)
                if 1 <= i < NT:
                    skip_input(i)
                if 2 <= i < NT + 2:
                    y_deviation(i - 2)
                if i >= 4 and i % 2 == 0 and i < NT + 1:
                    deviation(2, i // 2 - 2)
                if i >= NT + 1:
                    deviation(2, i - NT // 2 - 2)
            lanes_of_slots(1)
            moe(1)
            for t in range(2, NT - 2):
                add_first(1, t)

        @block.scalar
        def _(act):
            def turned(q, i):
                act.wait_ge(xt_psum, NT // 2 * q + i + 1)
                ts = tiles_of(q, i)
                dst = (xTh if q == 1 else xT)[:, ts[0]:ts[-1] + 1, :, :].rearrange("p t k n -> p (t k n)")
                act.activation(dst, ps_turn[i % 3][:, 0:len(ts) * KD * P], ACT.Copy).then_inc(xt_ready, 1)

            def gate(f, i):
                act.wait_ge(gate_in, 2 * f + i + 1)
                at = slice(i * GT, (i + 1) * GT)
                act.activation(ge[:, at, :], gl[:, at, :], ACT.Exp).then_inc(gate_exp, 1)

            def slot_values(f):
                act.wait_ge(units_ready, f + 1)
                act.activation(tab[:, 0, :, :], unit_oh[:, :, :], ACT.Copy, scale=prow[:, 0:1])\
                   .then_inc(tab_rows, 1)
                for c in range(2):
                    at = slice(c * NT, (c + 1) * NT)
                    act.activation(tab[:, 2, at, :], unit_oh[:, at, :], ACT.Copy, scale=float(c * T) - BIG)\
                       .then_inc(tab_rows, 1)

            def high_part(dst, src, ready=None, count=16):
                if ready is not None:
                    act.wait_ge(ready, count)
                act.activation(dst, src, ACT.Copy).then_inc(w_hi, 1)

            def unit_x(f, s):
                u = f * UNITS + s
                act.wait_ge(uxt_psum, u + 1)
                if u >= 2:
                    act.wait_ge(h_ready, u - 1)
                act.activation(uxh[:, u % 2, :, :].rearrange("p k n -> p (k n)"), ps_xt[u % 2], ACT.Copy)\
                    .then_inc(uxh_ready, 1)

            def unit_silu(f, s):
                u = f * UNITS + s
                act.wait_ge(h_ready, u + 1)
                if u >= 2:
                    act.wait_ge(g_ready, u - 1)
                act.activation(sl[:, u % 2, :], ps_h[u % 2][:, 0:F], ACT.Silu).then_inc(sl_ready, 1)

            def unit_g(f, s):
                u = f * UNITS + s
                act.wait_ge(gt_psum, u + 1)
                if u >= 2:
                    act.wait_ge(y_psum, u - 1)
                act.activation(gth[:, u % 2, :, :].rearrange("p k n -> p (k n)"), ps_gt[u % 2], ACT.Copy)\
                    .then_inc(gth_ready, 1)

            def moe(f):
                act.wait_ge(act_own, f + 1)
                act.activation(table_call[:, :], mhalf[:, 0:1], ACT.Silu).then_inc(act_own, 1)
                unit_x(f, 0)
                unit_x(f, 1)
                for s in range(UNITS + 1):
                    if s < UNITS:
                        unit_silu(f, s)
                    if s + 2 < UNITS:
                        unit_x(f, s + 2)
                    if s >= 1:
                        unit_g(f, s - 1)
                    if f == 0 and 4 <= s < 4 + 2 * KD:
                        k, part = divmod(s - 4, 2)
                        at = slice(part * NPROJ // 2, (part + 1) * NPROJ // 2)
                        high_part(winh[:, k, at], wins[:, k, at], ld_win)
                    if f == 0 and 10 <= s < 10 + KI:
                        high_part(wouth[:, s - 10, :], wouts[:, s - 10, :], wout_scaled, s - 9)

            act.wait_ge(consts, N_CONST)
            early = [(w1h[:, i * SEG1:(i + 1) * SEG1], w1s[:, i * SEG1:(i + 1) * SEG1], ld_w1[i], 16 * EG)
                     for i in range(NWG)]
            early += [(w2h[:, i * SEG2:(i + 1) * SEG2], w2s[:, i * SEG2:(i + 1) * SEG2], ld_w2[i],
                       16 * (E // NW2)) for i in range(NW2)]
            act.activation(table_call[:, :], mhalf[:, 0:1], ACT.Exp).then_inc(act_own, 1)
            turned(0, 0)
            turned(0, 1)
            high_part(*early[0])
            turned(0, 2)
            turned(0, 3)
            gate(0, 0)
            high_part(*early[1])
            gate(0, 1)
            for e in early[2:5]:
                high_part(*e)
            slot_values(0)
            for e in early[5:]:
                high_part(*e)
            moe(0)

            def scale_first(f, t):
                if t == 2:
                    act.wait_ge(cw_ready, 2 * (f + 1))
                act.wait_ge(y_back[t // 2], 32 * (f + 1))
                act.activation(yin[:, 0, t, :], yin[:, 0, t, :], ACT.Copy, scale=cw[:, 0, t:t + 1])\
                   .then_inc(y_scaled, 1)

            def normalise(i):
                act.wait_ge(shift_ready, i + 1)
                for t in (2 * i, 2 * i + 1):
                    act.activation(xn[:, t, :], x_sb[:, t, :], ACT.Identity, bias=shift[:, t:t + 1],
                                   scale=rstd[:, t:t + 1]).then_inc(xn_ready, 1)

            for t in range(2, NT):
                scale_first(0, t)
            normalise(0)
            normalise(1)
            turned(1, 0)
            turned(1, 1)
            normalise(2)
            normalise(3)
            turned(1, 2)

            def tap(n):
                h, c = divmod(n, NC)
                act.wait_ge(proj_psum, n + 1)
                ins = act.activation(conv[:, ORDER[c], 512 * h:512 * (h + 1)], ps_proj[n % 3][:, :], ACT.Copy,
                                     scale=cwt[:, ORDER[c], TAPS - 1:TAPS])
                if n not in DVE_TAPS:
                    k = split_taps(n)
                    if k >= 2:
                        act.wait_ge(conv_full, k - 1)
                    ins = act.activation(tap2[:, k % 2, :], ps_proj[n % 3][:, :], ACT.Copy,
                                         scale=cwt[:, ORDER[c], TAPS - 2:TAPS - 1])
                ins.then_inc(tap_ready, 1)

            def conv_silu(n):
                h, c = divmod(n, NC)
                if n in DVE_TAPS:
                    act.wait_ge(conv_sum, n + 1)
                else:
                    act.wait_ge(conv_full, split_taps(n) + 1)
                part = conv[:, ORDER[c], 512 * h:512 * (h + 1)]
                act.activation(part, part, ACT.Silu, bias=cbt[:, ORDER[c]:ORDER[c] + 1]).then_inc(conv_ready, 1)

            def z_silu(t):
                act.wait_ge(z_psum, t + 1)
                act.activation(sz[:, t, :], ps_z[t % 2][:, :], ACT.Silu).then_inc(z_ready, 1)

            def copy_tokens(t):
                act.wait_ge(xtok_psum, t + 1)
                if t >= 1:
                    act.wait_ge(xd_ready, t)
                act.activation(xs[:, :], ps_xtok[:, :], ACT.Copy).then_inc(xs_ready, 1)
                if t % 2 == 0:
                    act.wait_ge(cb_psum, t + 1)
                    if t >= 2:
                        act.wait_ge(state_psum, t // 2)
                    act.activation(btok[:, :], ps_btok, ACT.Copy).then_inc(btok_ready, 1)

            def decays(t):
                hh = NHEADS // 2
                for i in range(2):
                    act.wait_ge(seg_psum, 2 * t + i + 1)
                    if t >= 1:
                        act.wait_ge(mm_ready, t)
                    act.activation(dec[:, i * hh:(i + 1) * hh, :].rearrange("p h l -> p (h l)"),
                                   ps_seg[i][:, :], ACT.Exp).then_inc(dec_ready, 1)

            def copy_state(t):
                act.wait_ge(state_psum, t // 2 + 1)
                if t >= 2:
                    act.wait_ge(yoff_psum, t // 2)
                act.activation(state[:, :], ps_state[:, :], ACT.Copy).then_inc(state_ready, 1)

            def squares(t):
                act.wait_ge(yg_ready, t + 1)
                if t >= 1:
                    act.wait_ge(ssq_ready, t)
                act.activation(ysq[:, :], yg[:, t % 2, :], ACT.Square, accum_out=ssq[:, t:t + 1])\
                    .then_inc(ssq_ready, 1)

            def seg_low(t):
                act.wait_ge(seg_psum, 2 * (t - 1))
                for h in range(NHEADS):
                    last = act.activation(segl[:, t % 2, h, :], tri[:, :], ACT.Copy, scale=dal[:, t, h:h + 1])
                last.then_inc(seg_low_in, 1)

            def y_high(t):
                act.wait_ge(yt_psum, t + 1)
                if t >= 1:
                    act.wait_ge(o_psum, t)
                act.activation(yth[:, :, :].rearrange("p k n -> p (k n)"), ps_yt[:, :], ACT.Copy)\
                    .then_inc(yth_ready, 1)

            for n in range(NC * NH + 2):
                if n < NC * NH:
                    tap(n)
                for t in range(NT):
                    if Z_AT[t] == n - 1:
                        z_silu(t)
                if n == NC * NH + 1:
                    copy_tokens(0)
                if n == 0:
                    turned(1, NT // 2 - 1)
                if n >= 2:
                    conv_silu(n - 2)
                if n == DT_AT:
                    act.wait_ge(dt_in, 1)
                    act.activation(dtu[:, :, :], dta[:, :, :], ACT.Exp).then_inc(dt_exp, 1)
                    act.activation(aexp[:, :], alog[:, :], ACT.Exp).then_inc(a_exp, 1)
            for i in range(NT + 3):
                if i < NT:
                    if i >= 1:
                        copy_tokens(i)
                    decays(i)
                if i == 0:
                    act.wait_ge(cum_psum, 2)
                    act.activation(ecum[:, :, :].rearrange("p t h -> p (t h)"), ps_cum, ACT.Exp).then_inc(cum_exp, 1)
                    act.activation(eend[:, :, :].rearrange("p t h -> p (t h)"), ps_end, ACT.Exp).then_inc(cum_exp, 1)
                if 2 <= i < NT + 2:
                    squares(i - 2)
                if 1 <= i < NT + 1:
                    if (i - 1) % 2 == 0:
                        copy_state(i - 1)
                if i + 2 < NT:
                    seg_low(i + 2)
                if 2 <= i < NT + 2:
                    y_high(i - 2)
                if i == NT:
                    turned(2, 0)
                    turned(2, 1)

            turned(2, 2)
            turned(2, 3)
            gate(1, 0)
            turned(2, 4)
            gate(1, 1)
            slot_values(1)
            moe(1)
            for t in range(2, NT - 2):
                scale_first(1, t)

        @block.tensor
        def _(pe):
            def turn(q, i):
                n = NT // 2 * q
                src = xn_late if q == 2 else xn
                ts = tiles_of(q, i)
                pe.wait_ge(xn_ready, NT * q + ts[-1] + 1)
                if i >= 3:
                    pe.wait_ge(xt_ready, n + i - 2)
                    if q == 1:
                        pe.wait_ge(xtl_ready, i - 2)
                for j, t in enumerate(ts):
                    for k in range(KD):
                        last = pe.transpose(ps_turn[i % 3][:, (j * KD + k) * P:(j * KD + k + 1) * P],
                                            src[:, t, k * P:(k + 1) * P], ident[:, :])
                last.then_inc(xt_psum, 1)

            def split3(out_ap, pairs):
                n = len(pairs)
                for a in range(3):
                    for i, (lh, ll, rh, rl) in enumerate(pairs):
                        l, r = ((lh, rh), (lh, rl), (ll, rh))[a]
                        last = pe.matmul(out_ap, l, r, start=(a == 0 and i == 0), stop=(a == 2 and i == n - 1))
                return last

            def logits(f, i):
                pe.wait_ge(xt_ready, NT // 2 * 2 * f + i + 1)
                for t in tiles_of(2 * f, i):
                    for k in range(KD):
                        last = pe.matmul(ps_log[t // GT][:, t % GT, :], xT[:, t, k, :], wgt[:, k, :],
                                         start=(k == 0), stop=(k == KD - 1))
                last.then_inc(logits_ready, 1)

            def keep_warm(count, free):
                for _ in range(count):
                    pe.matmul(free[:, :], ones16[:, :], ones16[:, 0:1].broadcast_to([P, 512]), start=True, stop=True)

            def route(f):
                pe.wait_ge(mask_ready, 2 * f + 2)
                pe.matmul(ps_rank, before16[:, :], m16[:, NT - 1:2 * NT - 1, :], start=True, stop=False)
                for d in range(1, NT):
                    last = pe.matmul(ps_rank, ones16[:, :], m16[:, NT - 1 - d:2 * NT - 1 - d, :],
                                     start=False, stop=(d == NT - 1))
                pe.matmul(ps_cnt, ones16[:, :], half16[:, :], start=True, stop=False)
                for t in range(NT):
                    last = pe.matmul(ps_cnt, inv16[:, :], m16[:, NT - 1 + t, :], start=False,
                                     stop=(t == NT - 1))
                last.then_inc(rank_ready, 1)
                keep_warm(WARM + 2, bank[4])
                pe.wait_ge(tab_tiles, f + 1)
                pe.wait_ge(tab_rows, 3 * (f + 1))
                for i in range(TK):
                    if i < LANE_DVE:
                        pe.wait_ge(lane_in, LANE_DVE * f + i + 1)
                    else:
                        pe.wait_ge(lane_in_pool, (TK - LANE_DVE) * f + i - LANE_DVE + 1)
                    last = pe.matmul(ps_tab.rearrange("p (a u) -> p a u", a=3), lane_oh[:, i, :], tab[:, :, i, :],
                                     start=(i == 0), stop=(i == TK - 1))
                last.then_inc(tab_ready, 1)

            def unit_turn_x(f, s):
                u = f * UNITS + s
                pe.wait_ge(xg_landed[u % XG], 16 * (u // XG + 1))
                if u >= 2:
                    pe.wait_ge(uxl_ready, u - 1)
                for k in range(KD):
                    last = pe.transpose(ps_xt[u % 2][:, k * P:(k + 1) * P], xg[:, u % XG, k * P:(k + 1) * P],
                                        ident[:, :])
                last.then_inc(uxt_psum, 1)

            def unit_up(f, s, e):
                u = f * UNITS + s
                pe.wait_ge(uxl_ready, u + 1)
                if u >= 2:
                    pe.wait_ge(g_ready, u - 1)
                b = u % 2
                pairs = []
                for k in range(KD):
                    at = e * (KD * FF) + k * FF
                    pairs.append((uxh[:, b, k, :], uxl[:, b, k, :],
                                  w1h[:, bass.ds(at, FF)], w1l[:, bass.ds(at, FF)]))
                split3(ps_h[b], pairs).then_inc(h_ready, 1)

            def unit_turn_g(f, s):
                u = f * UNITS + s
                pe.wait_ge(g_ready, u + 1)
                if u >= 2:
                    pe.wait_ge(gtl_ready, u - 1)
                for j in range(2):
                    last = pe.transpose(ps_gt[u % 2][:, j * P:(j + 1) * P], g[:, u % 2, j * FH:(j + 1) * FH],
                                        ident[:, :])
                last.then_inc(gt_psum, 1)

            def unit_down(f, s, e):
                u = f * UNITS + s
                pe.wait_ge(gtl_ready, u + 1)
                if u >= 2:
                    pe.wait_ge(y_ready, u - 1)
                b = u % 2
                pairs = []
                for j in range(2):
                    at = e * (2 * D) + j * D
                    pairs.append((gth[:, b, j, :], gtl[:, b, j, :],
                                  w2h[:, bass.ds(at, D)], w2l[:, bass.ds(at, D)]))
                split3(ps_y[b], pairs).then_inc(y_psum, 1)

            def moe(f):
                keep_warm(2 * WARM - 1, bank[4])
                pe.wait_ge(expert_ready, f + 1)
                expert = {0: pe.value_load(ue[0:1, 0:1], min_val=0, max_val=E - 1)}
                unit_turn_x(f, 0)
                unit_turn_x(f, 1)
                if f == 0:
                    pe.wait_ge(w_hi, NWG)
                    pe.wait_ge(w_lo, NWG - NWP)
                    pe.wait_ge(w_lo_pool, NWP)
                for s in range(UNITS + 2):
                    if s < UNITS:
                        unit_up(f, s, expert[s])
                    if s + 1 < UNITS:
                        expert[s + 1] = pe.value_load(ue[0:1, s + 1:s + 2], min_val=0, max_val=E - 1)
                    if s + 2 < UNITS:
                        unit_turn_x(f, s + 2)
                    if 1 <= s <= UNITS:
                        unit_turn_g(f, s - 1)
                    if f == 0 and s == 2:
                        pe.wait_ge(w_hi, NWG + NW2)
                        pe.wait_ge(w_lo, NWG - NWP + NW2)
                    if s >= 2:
                        unit_down(f, s - 2, expert.pop(s - 2))

            pe.wait_ge(consts, N_CONST)
            keep_warm(WARM + 1, bank[4])
            pe.wait_ge(ld_wg, 16)
            turn(0, 0)
            keep_warm(WARM // 2, bank[4])
            turn(0, 1)
            logits(0, 0)
            logits(0, 1)
            turn(0, 2)
            turn(0, 3)
            keep_warm(WARM // 2 + 1, bank[5])
            logits(0, 2)
            logits(0, 3)
            route(0)
            moe(0)

            def project(n):
                h, c = divmod(n, NC)
                pe.wait_ge(xtl_ready, 2 * h + 2)
                if n >= 3:
                    pe.wait_ge(conv_sum, n - 2)
                col = DI + ORDER[c] * P
                pairs = [(winh[:, k, col:col + P], winl[:, k, col:col + P],
                          xTh[:, 4 * h:4 * h + 4, k, :], xTl[:, 4 * h:4 * h + 4, k, :]) for k in range(KD)]
                split3(ps_proj[n % 3][:, :].rearrange("p (t n) -> p t n", t=4), pairs).then_inc(proj_psum, 1)

            def project_dt(h):
                pe.wait_ge(xtl_ready, 2 * h + 2)
                pairs = [(winh[:, k, DI + CONVD:NPROJ], winl[:, k, DI + CONVD:NPROJ],
                          xTh[:, 4 * h:4 * h + 4, k, :], xTl[:, 4 * h:4 * h + 4, k, :]) for k in range(KD)]
                split3(ps_dtrow[h].rearrange("p (t n) -> p t n", t=4), pairs).then_inc(dtrow_psum, 1)

            def turn_dt():
                pe.wait_ge(dtrow_ready, 2)
                for t in range(NT):
                    last = pe.transpose(ps_dt[:, t * NHEADS:(t + 1) * NHEADS], dt_rows[:, t * P:(t + 1) * P],
                                        ident[0:NHEADS, 0:NHEADS])
                last.then_inc(dt_psum, 1)

            def project_z(t):
                if t >= 2:
                    pe.wait_ge(z_ready, t - 1)
                pairs = [(xTh[:, t, k, :], xTl[:, t, k, :], winh[:, k, 0:DI], winl[:, k, 0:DI])
                         for k in range(KD)]
                split3(ps_z[t % 2][:, :], pairs).then_inc(z_psum, 1)

            pe.wait_ge(w_hi, NWG + NW2 + 2 * KD + KI)
            pe.wait_ge(w_lo, NWG - NWP + NW2 + 2 * KD + KI)
            pe.wait_ge(shift_ready, 1)
            keep_warm(WARM, bank[5])
            turn(1, 0)
            turn(1, 1)
            keep_warm(WARM // 2, bank[5])
            project_dt(0)
            project(0)
            turn(1, 2)
            for n in range(1, NC * NH):
                project(n)
                if n == 2:
                    project_dt(1)
                if n == 3:
                    turn_dt()
                for t in range(NT):
                    if Z_AT[t] == n:
                        project_z(t)
                if n == 1:
                    turn(1, 3)
            pe.wait_ge(da_ready, 1)
            daf = da[:, :, :].rearrange("p t h -> p (t h)")
            pe.matmul(ps_cum, tri[:, :], daf, start=True, stop=True).then_inc(cum_psum, 1)
            pe.matmul(ps_end, after[:, :].bitcast(F32), daf, start=True, stop=True).then_inc(cum_psum, 1)

            def by_token(t):
                tok = slice(t * P, (t + 1) * P)
                pe.wait_ge(conv_ready, NC * (t // 4 + 1))
                if t >= 1:
                    pe.wait_ge(xdt_ready, t)
                for c in range(KI):
                    last = pe.transpose(ps_xtok[:, c * P:(c + 1) * P], conv[:, c, tok], ident[:, :])
                last.then_inc(xtok_psum, 1)
                if t >= 1:
                    pe.wait_ge(cbm_ready, t)
                else:
                    pe.wait_ge(conv_sum, NC * NH - 2)
                if t % 2 == 0:
                    pe.transpose(ps_btok, conv[:, KI, tok], ident[:, :])
                pe.matmul(ps_cb, conv[:, KI, tok], conv[:, KI + 1, tok], start=True, stop=True)\
                    .then_inc(cb_psum, 1)
                pe.wait_ge(seg_in, t + 1)
                if t < 2:
                    pe.wait_ge(seg_low_first, t + 1)
                else:
                    pe.wait_ge(seg_low_in, t - 1)
                hh = NHEADS // 2
                for i in range(2):
                    if t >= 1:
                        pe.wait_ge(dec_ready, 2 * t - 1 + i)
                    elif i == 1:
                        pe.wait_ge(conv_sum, NC * NH)
                    for part, first in ((segh, True), (segl, False)):
                        last = pe.matmul(ps_seg[i][:, :], after[:, :],
                                         part[:, t % 2, i * hh:(i + 1) * hh, :].rearrange("p h l -> p (h l)"),
                                         start=first, stop=not first)
                    last.then_inc(seg_psum, 1)

            def carry(t):
                tok = slice(t * P, (t + 1) * P)
                if t % 2 == 0:
                    pe.wait_ge(xde_ready, t // 2 + 1)
                    pe.wait_ge(btok_ready, t // 2 + 1)
                    if t == 0:
                        pe.wait_ge(z_ready, NT)
                    else:
                        pe.wait_ge(yf_ready, t // 2)
                    pe.matmul(ps_state[:, :], btok[:, :], xde[:, :], start=True, stop=True)\
                        .then_inc(state_psum, 1)
                else:
                    pe.wait_ge(state_ready, t // 2 + 1)
                    pe.matmul(ps_yoff[:, :], conv[:, KI + 1, tok], state[:, :], start=True, stop=True)\
                        .then_inc(yoff_psum, 1)

            def within(t):
                pe.wait_ge(mm_ready, t + 1)
                pe.wait_ge(xdt_ready, t + 1)
                if t >= 1:
                    pe.wait_ge(yd_used, t)
                for h in range(NHEADS):
                    last = pe.matmul(ps_ydiag[:, h * HD:(h + 1) * HD], mm[:, t % 2, h, :],
                                     xdt[:, t % 2, h * HD:(h + 1) * HD], start=True, stop=True)
                last.then_inc(ydiag_psum, 1)

            def turn_y(t):
                pe.wait_ge(yg_ready, t + 1)
                if t >= 1:
                    pe.wait_ge(ytl_ready, t)
                else:
                    pe.wait_ge(z_ready, NT)
                for k in range(KI):
                    last = pe.transpose(ps_yt[:, k * P:(k + 1) * P], yg[:, t % 2, k * P:(k + 1) * P],
                                        ident[:, :])
                last.then_inc(yt_psum, 1)

            def project_out(t):
                pe.wait_ge(ytl_ready, t + 1)
                if t >= 1:
                    pe.wait_ge(o_used, t)
                else:
                    pe.wait_ge(cum_exp, 2)
                pairs = [(yth[:, k, :], ytl[:, k, :], wouth[:, k, :], woutl[:, k, :]) for k in range(KI)]
                split3(ps_o, pairs).then_inc(o_psum, 1)

            for i in range(NT + 3):
                if i < NT:
                    by_token(i)
                if 1 <= i < NT + 1:
                    carry(i - 1)
                    within(i - 1)
                if i == NT + 1:
                    turn_y(NT - 1)
                if i >= 3:
                    project_out(i - 3)
                if i == NT + 1:
                    logits(1, 0)
                    logits(1, 1)
                if 2 <= i < NT + 1:
                    turn_y(i - 2)
                if i == NT:
                    turn(2, 0)
                    turn(2, 1)
                    keep_warm(WARM - 1, bank[2])

            turn(2, 2)
            keep_warm(WARM // 2, bank[5])
            logits(1, 2)
            turn(2, 3)
            turn(2, 4)
            logits(1, 3)
            logits(1, 4)
            route(1)
            moe(1)

        @block.vector
        def _(dve):
            own = Chain(dve_own)

            def settle():
                dve.wait_ge(dve_own, own.n)

            def statistics(q, i):
                ts = tiles_of(q, i)
                at = slice(ts[0], ts[-1] + 1)
                for t in ts:
                    own.add(dve.bn_stats(st[:, t, :], x_sb[:, t, :]))
                settle()
                for t in ts:
                    own.add(dve.bn_aggr(mv[:, t, :], st[:, t, :]))
                settle()
                dve.tensor_scalar(vare[:, at], mv[:, at, 1], EPS, None, ALU.add).then_inc(var_ready, 1)

            def normalise(q, i):
                dst = xn_late if q == 2 else xn
                dve.wait_ge(rstd_ready, NT // 2 * q + i + 1)
                for t in tiles_of(q, i):
                    dve.tensor_scalar(dst[:, t, :], x_sb[:, t, :], mv[:, t, 0:1], rstd[:, t:t + 1],
                                      ALU.subtract, ALU.mult).then_inc(xn_ready, 1)

            def gate(f, i):
                def over_e(a):
                    return a.unsqueeze(2).broadcast_to([P, GT, E])

                at = slice(i * GT, (i + 1) * GT)
                dve.wait_ge(logits_ready, NT // 2 * f + GT // 2 * (i + 1) + f * i)
                own.add(dve.tensor_reduce(lmax[:, at], ps_log[i], AX.X, ALU.max))
                settle()
                dve.tensor_tensor(gl[:, at, :], ps_log[i], over_e(lmax[:, at]), ALU.subtract).then_inc(gate_in, 1)
                dve.wait_ge(gate_exp, 2 * f + i + 1)
                for t in range(i * GT, (i + 1) * GT):
                    own.add(dve.max(top[:, t, :], ge[:, t, :]))
                settle()
                for t in range(i * GT, (i + 1) * GT):
                    own.add(dve.max_index(topi[:, t, :], top[:, t, :], ge[:, t, :]))
                settle()
                ohv = oh[:, :, :].rearrange("p (c t) e -> p c t e", c=2)
                for c in range(2):
                    own.add(dve.tensor_tensor(ohv[:, c, at, :], over_e(topi[:, at, c]),
                                              lanes[:, 0:E].unsqueeze(1).broadcast_to([P, GT, E]), ALU.is_equal))
                if i == 0:
                    own.add(dve.memset(m16[:, 0:NT - 1, :], 0.0))
                settle()
                dve.tensor_tensor(m16[:, NT - 1 + i * GT:NT - 1 + (i + 1) * GT, :], ohv[:, 0, at, :],
                                  ohv[:, 1, at, :], ALU.add).then_inc(mask_ready, 1)

            def weights(f):
                own.add(dve.tensor_reduce(gsum[:, :], ge[:, :, :], AX.X, ALU.add))
                settle()
                own.add(dve.reciprocal(grec[:, :], gsum[:, :]))
                settle()
                for c in range(2):
                    own.add(dve.tensor_tensor(sc[:, c, :], top[:, :, c], grec[:, :], ALU.mult))
                settle()
                own.add(dve.tensor_tensor(wsum[:, :], sc[:, 0, :], sc[:, 1, :], ALU.add))
                settle()
                own.add(dve.tensor_scalar(wsum[:, :], wsum[:, :], TOPK_EPS, None, ALU.add))
                settle()
                own.add(dve.reciprocal(wrec[:, :], wsum[:, :]))
                settle()
                for c in range(2):
                    dve.scalar_tensor_tensor(out=cw[:, c, :], in0=sc[:, c, :], scalar=0.5, in1=wrec[:, :],
                                             op0=ALU.mult, op1=ALU.mult).then_inc(cw_ready, 1)

            def route(f):
                dve.wait_ge(rank_ready, f + 1)
                own.add(dve.tensor_scalar(tl[:, :], ps_cnt, ROUND, -ROUND, ALU.add, ALU.add))
                settle()
                own.add(dve.tensor_tensor_scan(incl[:, :], tl[:, :], zer[:, :], 0.0, ALU.add, ALU.add))
                settle()
                own.add(dve.scalar_tensor_tensor(out=base[:, :], in0=incl[:, :], scalar=-HALF, in1=tl[:, :],
                                                 op0=ALU.add, op1=ALU.subtract))
                settle()
                own.add(dve.scalar_tensor_tensor(out=slot[:, :, :], in0=ps_rank, scalar=1.0 / P,
                                                 in1=base[:, :].unsqueeze(1).broadcast_to([P, NT, E]),
                                                 op0=ALU.mult, op1=ALU.add))
                settle()
                own.add(dve.tensor_tensor(osl[:, :, :].rearrange("p (c t) e -> p c (t e)", c=2),
                                          oh[:, :, :].rearrange("p (c t) e -> p c (t e)", c=2),
                                          slot[:, :, :].rearrange("p t e -> p (t e)").unsqueeze(1)
                                          .broadcast_to([P, 2, NT * E]), ALU.mult))
                settle()
                own.add(dve.tensor_reduce(slk[:, :], osl[:, :, :], AX.X, ALU.add))
                settle()
                own.add(dve.tensor_scalar(hi[:, :], slk[:, :], ROUND, -ROUND, ALU.add, ALU.add))
                settle()
                dve.tensor_tensor(lo[:, :], slk[:, :], hi[:, :], ALU.subtract).then_inc(lo_ready, 1)
                dve.tensor_tensor(unit_oh[:, :, :], hi[:, :].unsqueeze(2).broadcast_to([P, TK, UNITS]),
                                  lanes[:, :].unsqueeze(1).broadcast_to([P, TK, UNITS]), ALU.is_equal)\
                   .then_inc(units_ready, 1)
                dve.wait_ge(units_ready, f + 1)
                dve.tensor_tensor(tab[:, 1, :, :], unit_oh[:, :, :],
                                  tile_id[:, :].unsqueeze(2).broadcast_to([P, TK, UNITS]), ALU.mult)\
                   .then_inc(tab_tiles, 1)
                dve.wait_ge(lo_ready, f + 1)
                for i in range(LANE_DVE):
                    dve.tensor_scalar(lane_oh[:, i, :], lanes16[:, :], lo[:, i:i + 1], None, ALU.is_equal)\
                       .then_inc(lane_in, 1)
                dve.wait_ge(tab_ready, f + 1)
                own.add(dve.tensor_copy(srow[:, :], ps_tab[:, 0:UNITS]))
                settle()
                dve.scalar_tensor_tensor(out=gidx[:, :], in0=ps_tab[:, UNITS:2 * UNITS], scalar=float(P),
                                         in1=srow[:, :], op0=ALU.mult, op1=ALU.add).then_inc(idx_ready, 1)
                dve.wait_ge(idx_ready, f + 1)
                own.add(dve.tensor_scalar(srow[:, :], gidx[:, :], BIG, None, ALU.add))
                settle()
                dve.tensor_tensor(sidx[:, :], srow[:, :], ps_tab[:, 2 * UNITS:3 * UNITS], ALU.add)\
                   .then_inc(rows_ready, 1)
                own.add(dve.tensor_tensor(ule[:, :, :], incl[:, :].unsqueeze(1).broadcast_to([P, UNITS, E]),
                                          lanes[:, :].unsqueeze(2).broadcast_to([P, UNITS, E]), ALU.is_le))
                settle()
                own.add(dve.tensor_reduce(uef[:, :], ule[:, :, :], AX.X, ALU.add))
                settle()
                dve.tensor_scalar(ue[:, :], uef[:, :], float(E - 1), None, ALU.min).then_inc(expert_ready, 1)

            def unit_x(f, s):
                u = f * UNITS + s
                dve.wait_ge(uxh_ready, u + 1)
                if u >= 2:
                    dve.wait_ge(h_ready, u - 1)
                dve.tensor_tensor(uxl[:, u % 2, :, :].rearrange("p k n -> p (k n)"), ps_xt[u % 2],
                                  uxh[:, u % 2, :, :].rearrange("p k n -> p (k n)").bitcast(F32),
                                  ALU.subtract).then_inc(uxl_ready, 1)

            def unit_gate(f, s):
                u = f * UNITS + s
                dve.wait_ge(sl_ready, u + 1)
                if u >= 2:
                    dve.wait_ge(gt_psum, u - 1)
                dve.tensor_tensor(g[:, u % 2, :], ps_h[u % 2][:, F:FF], sl[:, u % 2, :], ALU.mult)\
                   .then_inc(g_ready, 1)

            def unit_g(f, s):
                u = f * UNITS + s
                dve.wait_ge(gth_ready, u + 1)
                if u >= 2:
                    dve.wait_ge(y_psum, u - 1)
                dve.tensor_tensor(gtl[:, u % 2, :, :].rearrange("p k n -> p (k n)"), ps_gt[u % 2],
                                  gth[:, u % 2, :, :].rearrange("p k n -> p (k n)").bitcast(F32),
                                  ALU.subtract).then_inc(gtl_ready, 1)

            def unit_y(f, s):
                u = f * UNITS + s
                dve.wait_ge(y_psum, u + 1)
                if u >= YB:
                    dve.wait_ge(y_stored[u % YB], 16 * (u // YB))
                dve.tensor_copy(yo[:, u % YB, :], ps_y[u % 2]).then_inc(y_ready, 1)

            def moe(f):
                unit_x(f, 0)
                unit_x(f, 1)
                if f == 0:
                    low_part_2(1)
                for s in range(UNITS + 2):
                    if s < UNITS:
                        unit_gate(f, s)
                    if s + 2 < UNITS:
                        unit_x(f, s + 2)
                    if 1 <= s <= UNITS:
                        unit_g(f, s - 1)
                    if s >= 2:
                        unit_y(f, s - 2)
                    if f == 0 and 5 <= s < 5 + 2 * KD:
                        k, part = divmod(s - 5, 2)
                        at = slice(part * NPROJ // 2, (part + 1) * NPROJ // 2)
                        dve.wait_ge(w_hi, NWG + NW2 + s - 4)
                        dve.tensor_tensor(winl[:, k, at], wins[:, k, at], winh[:, k, at].bitcast(F32),
                                          ALU.subtract).then_inc(w_lo, 1)
                    if f == 0 and s == 9:
                        dve.wait_ge(ld_wout, 16)
                        dve.wait_ge(ld_small, 16 * N_SMALL)
                        for k in range(KI):
                            dve.tensor_scalar(wouts[:, k, :], wouts[:, k, :], nsc[:, k:k + 1], None, ALU.mult)\
                               .then_inc(wout_scaled, 1)
                    if f == 0 and 11 <= s < 11 + KI:
                        k = s - 11
                        dve.wait_ge(w_hi, NWG + NW2 + 2 * KD + k + 1)
                        dve.tensor_tensor(woutl[:, k, :], wouts[:, k, :], wouth[:, k, :].bitcast(F32),
                                          ALU.subtract).then_inc(w_lo, 1)

            def combine(f, i):
                if i == 0:
                    dve.wait_ge(cw_ready, 2 * (f + 1))
                dve.wait_ge(y_back[i], 32 * (f + 1))
                own_sum = i == 0 or (f == 1 and i == NT // 2 - 1)
                for t in (2 * i, 2 * i + 1):
                    if own_sum:
                        own.add(dve.scalar_tensor_tensor(out=x_sb[:, t, :], in0=yin[:, 0, t, :],
                                                         scalar=cw[:, 0, t:t + 1], in1=x_sb[:, t, :],
                                                         op0=ALU.mult, op1=ALU.add))
                if own_sum:
                    settle()
                for t in (2 * i, 2 * i + 1):
                    if not own_sum:
                        dve.wait_ge(x_part, (NT - 2) * f + t - 1)
                    dve.scalar_tensor_tensor(out=x_sb[:, t, :], in0=yin[:, 1, t, :], scalar=cw[:, 1, t:t + 1],
                                             in1=x_sb[:, t, :], op0=ALU.mult, op1=ALU.add).then_inc(x_done, 1)

            def mean_shift(i):
                dve.wait_ge(rstd_ready, NT // 2 + i + 1)
                at = slice(2 * i, 2 * i + 2)
                dve.scalar_tensor_tensor(out=shift[:, at], in0=mv[:, at, 0], scalar=-1.0, in1=rstd[:, at],
                                         op0=ALU.mult, op1=ALU.mult).then_inc(shift_ready, 1)

            def turned_low(i):
                dve.wait_ge(xt_ready, NT // 2 + i + 1)
                dve.tensor_tensor(xTl[:, 2 * i:2 * i + 2, :, :].rearrange("p t k n -> p (t k n)"),
                                  ps_turn[i % 3][:, :],
                                  xTh[:, 2 * i:2 * i + 2, :, :].rearrange("p t k n -> p (t k n)").bitcast(F32),
                                  ALU.subtract).then_inc(xtl_ready, 1)

            def low_part(i):
                dve.wait_ge(w_hi, i + 1)
                at = slice(i * SEG1, (i + 1) * SEG1)
                dve.tensor_tensor(w1l[:, at], w1s[:, at], w1h[:, at].bitcast(F32), ALU.subtract).then_inc(w_lo, 1)

            def low_part_2(i):
                dve.wait_ge(w_hi, NWG + i + 1)
                at = slice(i * SEG2, (i + 1) * SEG2)
                dve.tensor_tensor(w2l[:, at], w2s[:, at], w2h[:, at].bitcast(F32), ALU.subtract).then_inc(w_lo, 1)

            dve.wait_ge(consts, N_CONST)
            for i in range(NT // 2 + 1):
                if i < NT // 2:
                    if i % (NT // 4) == 0:
                        dve.wait_ge(ld_x[i // (NT // 4)], 16)
                    statistics(0, i)
                if i >= 1:
                    normalise(0, i - 1)
            gate(0, 0)
            gate(0, 1)
            route(0)
            low_part(NWG - 1)
            low_part_2(0)
            moe(0)
            weights(0)
            for i in range(NT // 2 + 1):
                if i < NT // 2:
                    combine(0, i)
                if i >= 1:
                    mean_shift(i - 1)
                if i < NT // 2:
                    dve.wait_ge(x_done, 2 * i + 2)
                    statistics(1, i)
                if i == 2:
                    turned_low(0)
                    turned_low(1)
            turned_low(2)

            v = [P, NT, NHEADS]

            def flat(a):
                return a[:, :, :].rearrange("p t h -> p (t h)")

            def dt_steps():
                made = 0

                def chained(ins):
                    nonlocal made
                    own.add(ins)
                    made = own.n

                def previous():
                    dve.wait_ge(dve_own, made)

                dve.wait_ge(dt_psum, 1)
                chained(dve.tensor_tensor(dtx[:, :, :], ps_dt.rearrange("p (t h) -> p t h", t=NT),
                                          dtb[:, :].unsqueeze(1).broadcast_to(v), ALU.add))
                yield
                previous()
                dve.scalar_tensor_tensor(out=dta[:, :, :], in0=dtx[:, :, :], scalar=-1.0, in1=dtx[:, :, :],
                                         op0=ALU.mult, op1=ALU.min).then_inc(dt_in, 1)
                yield
                yield
                yield
                yield
                dve.wait_ge(dt_exp, 1)
                chained(dve.tensor_scalar(dtr[:, :, :], dtu[:, :, :], 2.0, None, ALU.add))
                yield
                previous()
                chained(dve.reciprocal(dtp[:, :, :], dtr[:, :, :]))
                yield
                previous()
                chained(dve.tensor_tensor(dts[:, :, :], dtu[:, :, :], dtp[:, :, :], ALU.mult))
                yield
                previous()
                chained(dve.tensor_tensor(dtq[:, :, :], dts[:, :, :], dts[:, :, :], ALU.mult))
                yield
                previous()
                chained(dve.tensor_scalar(dtp[:, :, :], dtq[:, :, :], ATANH[-1], None, ALU.mult))
                yield
                for coef in ATANH[-2:0:-1]:
                    previous()
                    chained(dve.scalar_tensor_tensor(out=dtp[:, :, :], in0=dtp[:, :, :], scalar=coef,
                                                     in1=dtq[:, :, :], op0=ALU.add, op1=ALU.mult))
                    yield
                previous()
                chained(dve.scalar_tensor_tensor(out=dtr[:, :, :], in0=dtp[:, :, :], scalar=1.0, in1=dts[:, :, :],
                                                 op0=ALU.add, op1=ALU.mult))
                chained(dve.tensor_scalar(dta[:, :, :], dtx[:, :, :], 0.0, None, ALU.max))
                yield
                previous()
                chained(dve.scalar_tensor_tensor(out=dtv[:, :, :], in0=dtr[:, :, :], scalar=2.0,
                                                 in1=dta[:, :, :], op0=ALU.mult, op1=ALU.add))
                yield
                previous()
                dve.wait_ge(a_exp, 1)
                dve.scalar_tensor_tensor(out=da[:, :, :], in0=dtv[:, :, :], scalar=-1.0,
                                         in1=aexp[:, :].unsqueeze(1).broadcast_to(v), op0=ALU.mult,
                                         op1=ALU.mult).then_inc(da_ready, 1)
                yield
                dve.wait_ge(da_ready, 1)
                chained(dve.tensor_copy(dah[:, :, :], da[:, :, :]))
                yield
                previous()
                dve.tensor_tensor(dal[:, :, :], da[:, :, :], dah[:, :, :].bitcast(F32), ALU.subtract)\
                   .then_inc(da_split, 1)

            spans = 512 // SEQ
            steps = dt_steps()
            for n in range(NC * NH):
                h, c = divmod(n, NC)
                c = ORDER[c]
                dve.wait_ge(tap_ready, n + 1)
                src = ps_proj[n % 3][:, :].rearrange("p (b s) -> p b s", b=spans)
                dst = conv[:, c, 512 * h:512 * (h + 1)].rearrange("p (b s) -> p b s", b=spans)
                for back in range(1 if n in DVE_TAPS else 2, TAPS):
                    ins = dve.scalar_tensor_tensor(out=dst[:, :, back:SEQ], in0=src[:, :, 0:SEQ - back],
                                                   scalar=cwt[:, c, TAPS - 1 - back:TAPS - back],
                                                   in1=dst[:, :, back:SEQ], op0=ALU.mult, op1=ALU.add)
                    if back < TAPS - 1:
                        own.add(ins)
                    else:
                        ins.then_inc(conv_sum, 1)
                    if n >= 3:
                        next(steps, None)
                    if n >= 5:
                        next(steps, None)
                    if back < TAPS - 1:
                        settle()
                if n == 0:
                    turned_low(NT // 2 - 1)
                if n in (1, 2):
                    dve.wait_ge(dtrow_psum, n)
                    dve.tensor_copy(dt_rows[:, 512 * (n - 1):512 * n], ps_dtrow[n - 1]).then_inc(dtrow_ready, 1)
            for _ in steps:
                pass

            def first_seg_low(t):
                dve.tensor_tensor(segl[:, t, :, :], tri[:, :].unsqueeze(1).broadcast_to([P, NHEADS, P]),
                                  dal[:, t, :].unsqueeze(2).broadcast_to([P, NHEADS, P]), ALU.mult)\
                   .then_inc(seg_low_first, 1)

            dve.wait_ge(da_split, 1)
            dve.wait_ge(z_psum, NT)
            dve.wait_ge(proj_psum, NC * NH)
            first_seg_low(0)

            def heads(a):
                return a.rearrange("p (h d) -> p h d", h=NHEADS)

            def scale_dt(t):
                dve.wait_ge(xs_ready, t + 1)
                if t >= 2:
                    dve.wait_ge(ydiag_psum, t - 1)
                    if t % 2 == 0:
                        dve.wait_ge(xde_ready, t // 2)
                dve.tensor_tensor(heads(xdt[:, t % 2, :]), heads(ps_xtok[:, :]),
                                  dtv[:, t, :].unsqueeze(2).broadcast_to([P, NHEADS, HD]), ALU.mult)\
                   .then_inc(xdt_ready, 1)

            def mix_matrix(t):
                dve.wait_ge(cb_psum, t + 1)
                dve.wait_ge(btok_ready, t // 2 + 1)
                if t >= 2:
                    dve.wait_ge(mm_ready, t - 1)
                dve.tensor_tensor(cbm[:, t % 2, :], ps_cb, tri[:, :], ALU.mult).then_inc(cbm_ready, 1)
                if t == 0:
                    first_seg_low(1)
                dve.wait_ge(cbm_ready, t + 1)
                dve.wait_ge(dec_ready, 2 * t + 2)
                dve.tensor_tensor(mm[:, t % 2, :, :], dec[:, :, :],
                                  cbm[:, t % 2, :].unsqueeze(1).broadcast_to([P, NHEADS, P]), ALU.mult)\
                   .then_inc(mm_ready, 1)

            def gated(t):
                if t % 2 == 1:
                    dve.wait_ge(yoff_psum, t // 2 + 1)
                    if t >= 3:
                        dve.wait_ge(yg_ready, t)
                    dve.tensor_tensor(heads(yf[:, :]), heads(ps_yoff[:, :]),
                                      ecum[:, t, :].unsqueeze(2).broadcast_to([P, NHEADS, HD]), ALU.mult)\
                       .then_inc(yf_ready, 1)
                dve.wait_ge(ydiag_psum, t + 1)
                dve.wait_ge(xd_ready, t + 1)
                if t >= 1:
                    dve.wait_ge(yg_ready, t)
                dve.tensor_tensor(y1[:, :], ps_ydiag[:, :], xd[:, :], ALU.add).then_inc(yd_used, 1)
                dve.wait_ge(yd_used, t + 1)
                if t % 2 == 1:
                    dve.wait_ge(yf_ready, t // 2 + 1)
                    own.add(dve.tensor_tensor(y1[:, :], y1[:, :], yf[:, :], ALU.add))
                    settle()
                if t >= 2:
                    dve.wait_ge(yt_psum, t - 1)
                    dve.wait_ge(ssq_ready, t - 1)
                dve.tensor_tensor(yg[:, t % 2, :], y1[:, :], sz[:, t, :], ALU.mult).then_inc(yg_ready, 1)

            def y_variance(t):
                dve.wait_ge(ssq_ready, t + 1)
                dve.tensor_scalar(vy[:, t:t + 1], ssq[:, t:t + 1], 1.0 / DI, EPS, ALU.mult, ALU.add)\
                   .then_inc(vy_ready, 1)

            def y_low(t):
                dve.wait_ge(yth_ready, t + 1)
                if t >= 1:
                    dve.wait_ge(o_psum, t)
                dve.tensor_tensor(ytl[:, :, :].rearrange("p k n -> p (k n)"), ps_yt[:, :],
                                  yth[:, :, :].rearrange("p k n -> p (k n)").bitcast(F32), ALU.subtract)\
                   .then_inc(ytl_ready, 1)

            def add_mixed(t):
                dve.wait_ge(o_psum, t + 1)
                dve.wait_ge(ry_ready, t + 1)
                dve.scalar_tensor_tensor(out=x_sb[:, t, :], in0=ps_o, scalar=ry[:, t:t + 1],
                                         in1=x_sb[:, t, :], op0=ALU.mult, op1=ALU.add).then_inc(o_used, 1)

            for i in range(NT + 3):
                if i < NT:
                    scale_dt(i)
                    mix_matrix(i)
                if 1 <= i < NT + 1:
                    gated(i - 1)
                if 2 <= i < NT + 2:
                    y_variance(i - 2)
                if i >= 3:
                    add_mixed(i - 3)
                if 2 <= i < NT + 2:
                    y_low(i - 2)
                if i >= 4 and i % 2 == 0 and i < NT + 1:
                    dve.wait_ge(o_used, i - 2)
                    statistics(2, i // 2 - 2)
                if i >= NT + 1:
                    dve.wait_ge(o_used, i - 2)
                    statistics(2, i - NT // 2 - 2)
                if i >= 5 and i % 2 == 1:
                    normalise(2, (i - 5) // 2)
            normalise(2, 3)
            normalise(2, 4)
            gate(1, 0)

            gate(1, 1)
            route(1)
            moe(1)
            weights(1)
            for i in range(NT // 2):
                combine(1, i)

def kernel(**inputs):
    import concourse.bacc as bacc
    from concourse.bass_utils import run_bass_kernel_spmd

    get = {k: np.asarray(v) for k, v in inputs.items()}
    u = get["L0_attn_u"]
    conv_w = get["L0_attn_conv_w"]
    row = lambda a: np.ascontiguousarray(a.reshape(1, -1))
    cols = lambda a: np.ascontiguousarray(a.reshape(-1, P).T)
    arrays = {
        "u": np.ascontiguousarray(u.reshape(-1, u.shape[-1])),
        "w_in": np.ascontiguousarray(get["L0_attn_W_in"]),
        "conv_w": np.ascontiguousarray(conv_w.T[None]),
        "conv_b": cols(get["L0_attn_conv_b"]),
        "dt_bias": row(get["L0_attn_dt_bias"]),
        "a_log": row(get["L0_attn_A_log"]),
        "d_skip": row(get["L0_attn_D"]),
        "norm_scale": cols(get["L0_attn_norm_scale"]),
        "w_out": np.ascontiguousarray(get["L0_attn_W_out"]),
        "wg_t": np.ascontiguousarray(get["L0_ffn_wg"].T),
        "w1": np.ascontiguousarray(get["L0_ffn_w1"]),
        "w2": np.ascontiguousarray(get["L0_ffn_w2"]),
    }
    nc = bacc.Bacc("TRN2", target_bir_lowering=False, num_devices=1)
    args = [nc.dram_tensor(n, a.shape, mybir.dt.from_np(a.dtype), kind="ExternalInput").ap()
            for n, a in arrays.items()]
    out = nc.dram_tensor("out", arrays["u"].shape, F32, kind="ExternalOutput").ap()
    build(nc, *args, out)
    r = run_bass_kernel_spmd(nc, [arrays], core_ids=[0])
    return r.results[0]["out"].reshape(u.shape)
```
